# Optimizing a Trainium2 kernel written in Bass

```python
import numpy as np
import jax
import jax.numpy as jnp

def _softmax(x, axis=-1):
    return jax.nn.softmax(x, axis=axis)

def _gelu(x):
    return jax.nn.gelu(x, approximate=True)

def _silu(x):
    return jax.nn.silu(x)

def _sigmoid(x):
    return jax.nn.sigmoid(x)

def _layernorm(x, axis=-1, eps=1e-05):
    m = jnp.mean(x, axis=axis, keepdims=True)
    v = jnp.var(x, axis=axis, keepdims=True)
    return (x - m) / jnp.sqrt(v + eps)

def _scatter_add(tgt, idx, src, axis=0):
    return tgt.at[idx].add(src)

def _segment_sum(src, seg, n):
    return jax.ops.segment_sum(src, seg, n)
kernel_name = 'mk_seq_preln_d1_jaxref_r4_0e1c33'

def setup_inputs(seed: int=0):
    np.random.seed(seed)
    _w = jnp.asarray

    def _L0_attn_setup():
        import jax, jax.numpy as jnp
        import numpy as np
        NHEAD = 8
        ATTN_EPS = 1e-06
        LN_EPS = 1e-05

        def _layernorm(y, g, b):
            mu = jnp.mean(y, axis=-1, keepdims=True)
            var = jnp.var(y, axis=-1, keepdims=True)
            return (y - mu) * jax.lax.rsqrt(var + LN_EPS) * g + b
        key = jax.random.key(seed)
        ks = jax.random.split(key, 6)
        B, L, D = (2, 2048, 256)
        s = 1.0 / np.sqrt(D)
        return {'x': jax.random.normal(ks[0], (B, L, D), jnp.float32), 'Wq': jax.random.normal(ks[1], (D, D), jnp.float32) * s, 'Wm': jax.random.normal(ks[2], (D, D), jnp.float32) * s, 'W1': jax.random.normal(ks[3], (D, 2 * D), jnp.float32) * s, 'W2': jax.random.normal(ks[4], (2 * D, D), jnp.float32) * (1.0 / np.sqrt(2 * D)), 'g1': jnp.ones((D,), jnp.float32), 'b1': jnp.zeros((D,), jnp.float32), 'g2': jnp.ones((D,), jnp.float32), 'b2': jnp.zeros((D,), jnp.float32)}
    _L0_attn_in = _L0_attn_setup()

    def _L0_ffn_setup():
        import jax, jax.numpy as jnp
        import numpy as np
        B, T, C, D = (2, 1024, 256, 128)
        E = 8
        MIN_E = 2
        EPS = 1e-12
        NEG = -1000000000.0

        def _xavier(key, shape, fan_in, fan_out):
            bound = (6.0 / (fan_in + fan_out)) ** 0.5
            return jax.random.uniform(key, shape, jnp.float32, -bound, bound)

        def _forward(hidden_states, sim_matrix, gates, q_proj, k_proj, v_proj, o_proj):
            b, t, c = hidden_states.shape
            x = hidden_states.reshape(b * t, c)
            xn = x / jnp.maximum(jnp.linalg.norm(x, axis=-1, keepdims=True), EPS)
            sn = sim_matrix / jnp.maximum(jnp.linalg.norm(sim_matrix, axis=0, keepdims=True), EPS)
            logits = xn @ sn - jax.nn.sigmoid(gates)
            gated = jax.nn.relu(logits)
            mask = (gated > 0).astype(logits.dtype)
            inactive = jnp.sum(mask, axis=1) == 0
            top_idx = jax.lax.top_k(logits, MIN_E)[1]
            n = mask.shape[0]
            fb = jnp.zeros_like(mask).at[jnp.arange(n)[:, None], top_idx].set(1.0)
            mask = jnp.where(inactive[:, None] & (fb > 0), 1.0, mask)
            masked_logits = jnp.where(mask > 0, gated, NEG)
            routing_weights = jax.nn.softmax(masked_logits, axis=-1)
            m = jax.lax.stop_gradient(mask)
            q = jnp.einsum('tc,ecd,te->td', x, q_proj, m)
            k = jnp.einsum('tc,ecd,te->td', x, k_proj, m)
            v = jnp.einsum('tc,ecd,te->td', x, v_proj, m)
            qh = q.reshape(b, t, D)
            kh = k.reshape(b, t, D)
            vh = v.reshape(b, t, D)
            scores = jnp.einsum('bqd,bkd->bqk', qh, kh) / jnp.sqrt(jnp.asarray(D, qh.dtype))
            causal = jnp.tril(jnp.ones((t, t), bool))
            scores = jnp.where(causal, scores, jnp.finfo(scores.dtype).min)
            attn = jax.nn.softmax(scores, axis=-1)
            attn_out = jnp.einsum('bqk,bkd->bqd', attn, vh).reshape(b * t, D)
            final = jnp.einsum('td,edc,te->tc', attn_out, o_proj, m * routing_weights)
            return final.reshape(b, t, c)
        key = jax.random.key(seed)
        k = jax.random.split(key, 6)
        hidden_states = jax.random.normal(k[0], (B, T, C), jnp.float32)
        sim_matrix = jax.random.normal(k[1], (C, E), jnp.float32)
        gates = jnp.zeros((E,), jnp.float32)
        q_proj = _xavier(k[2], (E, C, D), C, D)
        k_proj = _xavier(k[3], (E, C, D), C, D)
        v_proj = _xavier(k[4], (E, C, D), C, D)
        o_proj = _xavier(k[5], (E, D, C), D, C)
        return dict(hidden_states=hidden_states, sim_matrix=sim_matrix, gates=gates, q_proj=q_proj, k_proj=k_proj, v_proj=v_proj, o_proj=o_proj)
    _L0_ffn_in = _L0_ffn_setup()
    _d = {'L0_attn_x': _L0_attn_in['x'], 'L0_attn_Wq': _L0_attn_in['Wq'], 'L0_attn_Wm': _L0_attn_in['Wm'], 'L0_attn_W1': _L0_attn_in['W1'], 'L0_attn_W2': _L0_attn_in['W2'], 'L0_attn_g1': _L0_attn_in['g1'], 'L0_attn_b1': _L0_attn_in['b1'], 'L0_attn_g2': _L0_attn_in['g2'], 'L0_attn_b2': _L0_attn_in['b2'], 'L0_ffn_sim_matrix': _L0_ffn_in['sim_matrix'], 'L0_ffn_gates': _L0_ffn_in['gates'], 'L0_ffn_q_proj': _L0_ffn_in['q_proj'], 'L0_ffn_k_proj': _L0_ffn_in['k_proj'], 'L0_ffn_v_proj': _L0_ffn_in['v_proj'], 'L0_ffn_o_proj': _L0_ffn_in['o_proj']}
    _x0 = _d['L0_attn_x']
    _d['L0_attn_x'] = jax.random.normal(jax.random.fold_in(jax.random.key(seed), 1), (4, 2048, 256), dtype=_x0.dtype)
    del _x0
    return _d

def reference(L0_attn_x, L0_attn_Wq, L0_attn_Wm, L0_attn_W1, L0_attn_W2, L0_attn_g1, L0_attn_b1, L0_attn_g2, L0_attn_b2, L0_ffn_sim_matrix, L0_ffn_gates, L0_ffn_q_proj, L0_ffn_k_proj, L0_ffn_v_proj, L0_ffn_o_proj):

    def _L0_attn_ref(x, Wq, Wm, W1, W2, g1, b1, g2, b2):
        import jax, jax.numpy as jnp
        import numpy as np
        NHEAD = 8
        ATTN_EPS = 1e-06
        LN_EPS = 1e-05

        def _layernorm(y, g, b):
            mu = jnp.mean(y, axis=-1, keepdims=True)
            var = jnp.var(y, axis=-1, keepdims=True)
            return (y - mu) * jax.lax.rsqrt(var + LN_EPS) * g + b
        B, L, D = x.shape
        H = NHEAD
        d = D // H
        q = (x @ Wq).reshape(B, L, H, d)
        feat = jax.nn.elu(q) + 1.0
        Q = feat
        K = feat
        V = q / L
        KV = jnp.einsum('nshd,nshv->nhdv', K, V)
        Ksum = K.sum(axis=1)
        Z = 1.0 / (jnp.einsum('nlhd,nhd->nlh', Q, Ksum) + ATTN_EPS)
        msg = jnp.einsum('nlhd,nhdv,nlh->nlhv', Q, KV, Z) * L
        msg = msg.reshape(B, L, D) @ Wm
        x = x + _layernorm(msg, g1, b1)
        mlp = jax.nn.relu(msg @ W1) @ W2
        x = x + _layernorm(mlp, g2, b2)
        return x

    def _L0_ffn_ref(hidden_states, sim_matrix, gates, q_proj, k_proj, v_proj, o_proj):
        import jax, jax.numpy as jnp
        import numpy as np
        B, T, C, D = (2, 1024, 256, 128)
        E = 8
        MIN_E = 2
        EPS = 1e-12
        NEG = -1000000000.0

        def _xavier(key, shape, fan_in, fan_out):
            bound = (6.0 / (fan_in + fan_out)) ** 0.5
            return jax.random.uniform(key, shape, jnp.float32, -bound, bound)

        def _forward(hidden_states, sim_matrix, gates, q_proj, k_proj, v_proj, o_proj):
            b, t, c = hidden_states.shape
            x = hidden_states.reshape(b * t, c)
            xn = x / jnp.maximum(jnp.linalg.norm(x, axis=-1, keepdims=True), EPS)
            sn = sim_matrix / jnp.maximum(jnp.linalg.norm(sim_matrix, axis=0, keepdims=True), EPS)
            logits = xn @ sn - jax.nn.sigmoid(gates)
            gated = jax.nn.relu(logits)
            mask = (gated > 0).astype(logits.dtype)
            inactive = jnp.sum(mask, axis=1) == 0
            top_idx = jax.lax.top_k(logits, MIN_E)[1]
            n = mask.shape[0]
            fb = jnp.zeros_like(mask).at[jnp.arange(n)[:, None], top_idx].set(1.0)
            mask = jnp.where(inactive[:, None] & (fb > 0), 1.0, mask)
            masked_logits = jnp.where(mask > 0, gated, NEG)
            routing_weights = jax.nn.softmax(masked_logits, axis=-1)
            m = jax.lax.stop_gradient(mask)
            q = jnp.einsum('tc,ecd,te->td', x, q_proj, m)
            k = jnp.einsum('tc,ecd,te->td', x, k_proj, m)
            v = jnp.einsum('tc,ecd,te->td', x, v_proj, m)
            qh = q.reshape(b, t, D)
            kh = k.reshape(b, t, D)
            vh = v.reshape(b, t, D)
            scores = jnp.einsum('bqd,bkd->bqk', qh, kh) / jnp.sqrt(jnp.asarray(D, qh.dtype))
            causal = jnp.tril(jnp.ones((t, t), bool))
            scores = jnp.where(causal, scores, jnp.finfo(scores.dtype).min)
            attn = jax.nn.softmax(scores, axis=-1)
            attn_out = jnp.einsum('bqk,bkd->bqd', attn, vh).reshape(b * t, D)
            final = jnp.einsum('td,edc,te->tc', attn_out, o_proj, m * routing_weights)
            return final.reshape(b, t, c)
        return _forward(hidden_states, sim_matrix, gates, q_proj, k_proj, v_proj, o_proj)
    x = L0_attn_x
    x = x + _L0_attn_ref(_layernorm(x, axis=-1), L0_attn_Wq, L0_attn_Wm, L0_attn_W1, L0_attn_W2, L0_attn_g1, L0_attn_b1, L0_attn_g2, L0_attn_b2)
    x = x + _L0_ffn_ref(_layernorm(x, axis=-1), L0_ffn_sim_matrix, L0_ffn_gates, L0_ffn_q_proj, L0_ffn_k_proj, L0_ffn_v_proj, L0_ffn_o_proj)
    return x

_drawn_inputs = setup_inputs


def setup_inputs(seed=0):
    import zlib

    import numpy as np

    out = dict(_drawn_inputs(seed))
    spreads = {'L0_attn_g1': (1.0, 0.2),
     'L0_attn_b1': (0.0, 0.1),
     'L0_attn_g2': (1.0, 0.2),
     'L0_attn_b2': (0.0, 0.1),
     'L0_ffn_gates': (0.0, 0.1)}
    factors = {}
    for name, (base, spread) in spreads.items():
        noise = np.random.default_rng([zlib.crc32(name.encode()), seed]).standard_normal(out[name].shape)
        drawn = base * np.exp(spread * noise) if base else spread * noise
        out[name] = jnp.asarray(drawn.astype(out[name].dtype))
    for name, factor in factors.items():
        out[name] = (out[name] * factor).astype(out[name].dtype)
    return out
```

```python
from contextlib import ExitStack

import concourse.bass as bass
from concourse import mybir

ALU = mybir.AluOpType
ACT = mybir.ActivationFunctionType
F32 = mybir.dt.float32
F32R = mybir.dt.float32r
AX_X = mybir.AxisListType.X

P = 128
TILES = 4
BLOCK = P * TILES
LN_EPS = 1e-5
ATTN_EPS = 1e-6
NORM_EPS = 1e-12
MASKED = -3.0e38


class Blk:

    def __init__(self, b, j, batches, per_batch):
        self.b, self.j, self.batches, self.per_batch = b, j, batches, per_batch

    @property
    def s(self):
        return self.b * self.per_batch + self.j

    @property
    def par(self):
        return self.j % 2

    @property
    def turn(self):
        return self.b * (self.per_batch // 2) + self.j // 2

    def plus(self, k):
        j = self.j + k
        b = self.b + j // self.per_batch if not 0 <= j < self.per_batch else self.b
        if isinstance(b, int) and b >= self.batches:
            return None
        return Blk(b, j % self.per_batch, self.batches, self.per_batch)


class Flag:

    def __init__(self, sem, per, ahead=0):
        self.sem, self.per, self.ahead = sem, per, ahead

    def at(self, n, k=None):
        return (n + self.ahead) * self.per + (self.per if k is None else k)

    def grant(self, eng):
        eng.sem_inc(self.sem, self.ahead * self.per)


def settle(eng, paces):
    eng.sem_inc(paces[eng.engine])


def loop_blocks(eng, batches, per_batch, body):
    with eng.Fori(0, batches - 1, 1) as b:
        for j in range(per_batch):
            body(Blk(b, j, batches, per_batch))
    for j in range(per_batch):
        body(Blk(batches - 1, j, batches, per_batch))


class Ctx:

    def __init__(self, nc, stack, prefix):
        self.nc, self.stack, self.prefix = nc, stack, prefix

    def sb(self, name, shape, dt=F32):
        return self.stack.enter_context(self.nc.sbuf_tensor(self.prefix + name, shape, dt))

    def ps(self, name, shape, dt=F32):
        return self.stack.enter_context(self.nc.psum_tensor(self.prefix + name, shape, dt))

    def sem(self, name):
        return self.stack.enter_context(self.nc.semaphore(self.prefix + name))

    def flag(self, name, per, ahead=0):
        return Flag(self.sem(name), per, ahead)


def rows(dram, blk, width):
    return dram[bass.ds(blk.s * BLOCK, BLOCK), :].rearrange("(t p) c -> p t c", p=P)


def product(eng, out, pairs, begin=True, end=True):
    n = 3 * len(pairs)
    i = 0
    for (ah, al), (bh, bl) in pairs:
        for a, b in ((ah, bl), (ah, bh), (al, bh)):
            last = eng.matmul(out, a, b, start=(begin and i == 0), stop=(end and i == n - 1))
            i += 1
    return last


def stage1(nc, t, d):
    B, NB, C = d["B"], d["NB"], d["C"]
    H = 8
    with ExitStack() as st:
        c = Ctx(nc, st, "a_")
        x = c.sb("x", [P, 2, TILES, C])
        h = c.sb("h", [P, 2, TILES, C])
        base = c.sb("base", [P, 2, TILES, C])
        stats = c.sb("stats", [P, 2, TILES, 6])
        mv = c.sb("mv", [P, 2, TILES, 2])
        ve = c.sb("ve", [P, 2, TILES])
        rstd = c.sb("rstd", [P, 2, TILES])
        rstd1 = c.sb("rstd1", [P, 2, TILES])
        negmu = c.sb("negmu", [P, 2, TILES])
        negmur = c.sb("negmur", [P, 2, TILES])
        hT_hi = c.sb("hT_hi", [P, 2, BLOCK], F32R)
        hT_lo = c.sb("hT_lo", [P, 2, BLOCK], F32R)
        negpart = c.sb("negpart", [P, 2, 2, C])
        expneg = c.sb("expneg", [P, 2, 2, C])
        q = c.sb("q", [P, TILES, C])
        feat = c.sb("feat", [P, 2, TILES, C])
        fsum = c.sb("fsum", [P, TILES, C])
        wq_raw = c.sb("wq_raw", [P, 2, C])
        wq_hi = c.sb("wq_hi", [P, 2, C], F32R)
        wq_lo = c.sb("wq_lo", [P, 2, C], F32R)
        wm = c.sb("wm", [P, 2, C])
        w1 = c.sb("w1", [P, 2, 2 * C])
        w2_raw = c.sb("w2_raw", [P, 4, C])
        w_raw = c.sb("w_raw", [P, d["WCOLS"]])
        ones = c.sb("ones", [P, P])
        headmask = c.sb("headmask", [P, P])
        kvT = c.sb("kvT", [P, 2, P])
        gT = c.sb("gT", [P, 2, C])
        ks_st = c.sb("ks_st", [P, C])
        g_st_hi = c.sb("g_st_hi", [P, 2 * C], F32R)
        g_st_lo = c.sb("g_st_lo", [P, 2 * C], F32R)
        gw_st_hi = c.sb("gw_st_hi", [P, 2, 2 * C], F32R)
        gw_st_lo = c.sb("gw_st_lo", [P, 2, 2 * C], F32R)
        sim = c.sb("sim", [P, 2, 8])
        simsq = c.sb("simsq", [P, 2, 8])
        simn = c.sb("simn", [P, 3, 8])
        sn = c.sb("sn", [P, 2, 8])
        gates = c.sb("gates", [P, 2, 8])

        trp = [c.ps(f"trp{i}", [P, BLOCK]) for i in range(2)]
        qp = [c.ps(f"qp{i}", [P, 2, C]) for i in range(2)]
        kvp = [c.ps(f"kvp{i}", [P, 2, C]) for i in range(2)]
        misc = [c.ps(f"misc{i}", [P, 2 * C]) for i in range(2)]

        w_in = c.sem("w_in")
        small_in = c.sem("small_in")
        raw_in = c.sem("raw_in")
        x_in = [c.flag(f"x_in{i}", 16) for i in range(2)]
        consts = c.sem("consts")
        wq_split = c.sem("wq_split")
        w2_split = c.sem("w2_split")
        w_split = c.flag("w_split", 4)
        gate_pool = c.sem("gate_pool")
        gate_act = c.sem("gate_act")
        gate_pe = c.sem("gate_pe")
        gate_dve = c.sem("gate_dve")
        st_ready = c.flag("st_ready", TILES)
        mv_ready = c.flag("mv_ready", TILES)
        pool_small = c.flag("pool_small", 5)
        h_ready = c.flag("h_ready", TILES)
        base_ready = c.flag("base_ready", TILES)
        base_out = [c.flag(f"base_out{i}", 16) for i in range(2)]
        transposed = c.flag("transposed", 2)
        hi_ready = c.flag("hi_ready", 2)
        lo_ready = c.flag("lo_ready", 2)
        q_done = c.flag("q_done", 2)
        neg_ready = c.flag("neg_ready", 2)
        q_copied = c.flag("q_copied", 2)
        exp_ready = c.flag("exp_ready", 2)
        feat_ready = c.flag("feat_ready", 2)
        feat_out = [c.flag(f"feat_out{i}", 16, ahead=1) for i in range(2)]
        summed = c.flag("summed", 1, ahead=1)
        kv_done = c.flag("kv_done", 1)
        kv_masked = c.flag("kv_masked", 2)
        ks_done = c.flag("ks_done", 1, ahead=1)
        ks_copied = c.flag("ks_copied", 1)
        g_done = c.flag("g_done", 1)
        gT_done = c.flag("gT_done", 1)
        gT_copied = c.flag("gT_copied", 1)
        gw_done = c.flag("gw_done", 2)
        fold_hi = c.flag("fold_hi", 3)
        fold_lo = c.flag("fold_lo", 3, ahead=1)
        fold_out = c.flag("fold_out", 16 * 5, ahead=1)

        x2d, feat2d, base2d = t["x2d"], t["feat"], t["base"]

        paces = {e.engine: c.sem(f"pace_{k}") for k, e in enumerate((nc.sync, nc.gpsimd, nc.vector))}

        with nc.Block() as block:

            @block.sync
            def _(sp):
                for g in feat_out:
                    g.grant(sp)
                fold_out.grant(sp)
                first = Blk(0, 0, B, NB)
                sp.dma_start(wq_raw[:, :, :], t["Wq"].rearrange("(h p) n -> p h n", p=P)).then_inc(w_in, 16)
                for k in (0, 1):
                    blk = first.plus(k)
                    sp.dma_start(x[:, blk.par, :, :], rows(x2d, blk, C)).then_inc(x_in[blk.par].sem, 16)
                sp.dma_start(sim[:, :, :], t["sim"].rearrange("(h p) n -> p h n", p=P)).then_inc(small_in, 16)
                sp.dma_start(gates[:, 0, :], t["gates"].partition_broadcast(P)).then_inc(small_in, 16)
                sp.dma_start(wm[:, :, :], t["Wm"].rearrange("(h p) n -> p h n", p=P)).then_inc(small_in, 16)
                sp.dma_start(w1[:, :, :], t["W1"].rearrange("(h p) n -> p h n", p=P)).then_inc(small_in, 16)
                sp.dma_start(w2_raw[:, :, :], t["W2"].rearrange("(h p) n -> p h n", p=P)).then_inc(small_in, 16)
                E, D = d["E"], d["D"]
                for k, name in enumerate(("Wqe", "Wke", "Wve")):
                    for half in range(2):
                        dst = w_raw[:, half * E * 3 * D:(half + 1) * E * 3 * D].rearrange("p (e n) -> p e n", e=E)
                        sp.dma_start(dst[:, :, k * D:(k + 1) * D],
                                     t[name][:, half * P:(half + 1) * P, :].rearrange("e p n -> p e n")).then_inc(raw_in, 16)
                sp.dma_start(w_raw[:, 6 * E * D:].rearrange("p (e n) -> p e n", e=E),
                             t["Woe"].rearrange("e p n -> p e n")).then_inc(raw_in, 16)

                def body(blk):
                    after = blk.plus(2)
                    if after is not None:
                        sp.wait_ge(h_ready.sem, h_ready.at(blk.s))
                        sp.wait_ge(base_ready.sem, base_ready.at(blk.s))
                        settle(sp, paces)
                        sp.dma_start(x[:, blk.par, :, :], rows(x2d, after, C)).then_inc(x_in[blk.par].sem, 16)
                    sp.wait_ge(base_ready.sem, base_ready.at(blk.s))
                    settle(sp, paces)
                    sp.dma_start(rows(base2d, blk, C), base[:, blk.par, :, :]).then_inc(base_out[blk.par].sem, 16)
                    sp.wait_ge(feat_ready.sem, feat_ready.at(blk.s))
                    settle(sp, paces)
                    sp.dma_start(rows(feat2d, blk, C), feat[:, blk.par, :, :]).then_inc(feat_out[blk.par].sem, 16)
                    if blk.j == NB - 1:
                        sp.wait_ge(ks_copied.sem, ks_copied.at(blk.b))
                        sp.wait_ge(fold_hi.sem, fold_hi.at(blk.b))
                        sp.wait_ge(fold_lo.sem, fold_lo.at(blk.b))
                        settle(sp, paces)
                        r = bass.ds(blk.b * P, P)
                        sp.dma_start(t["ks"][r, :], ks_st[:, :]).then_inc(fold_out.sem, 16)
                        sp.dma_start(t["g_hi"][r, :], g_st_hi[:, :].bitcast(F32)).then_inc(fold_out.sem, 16)
                        sp.dma_start(t["g_lo"][r, :], g_st_lo[:, :].bitcast(F32)).then_inc(fold_out.sem, 16)
                        sp.dma_start(t["gw_hi"][r, :], gw_st_hi[:, :, :].bitcast(F32).rearrange("p h n -> p (h n)")).then_inc(fold_out.sem, 16)
                        sp.dma_start(t["gw_lo"][r, :], gw_st_lo[:, :, :].bitcast(F32).rearrange("p h n -> p (h n)")).then_inc(fold_out.sem, 16)

                loop_blocks(sp, B, NB, body)
                turns = B * NB // 2
                for par in range(2):
                    sp.wait_ge(base_out[par].sem, base_out[par].at(turns - 1))
                    sp.wait_ge(feat_out[par].sem, feat_out[par].at(turns - 1))
                sp.wait_ge(fold_out.sem, fold_out.at(B - 1))
                settle(sp, paces)

            @block.gpsimd
            def _(pool):
                summed.grant(pool)
                pool.memset(t["ident"][:, :], 0.0).then_inc(consts, 1)
                pool.memset(ones[:, :], 1.0).then_inc(consts, 1)
                pool.memset(t["minus_half"][:, :], -0.5).then_inc(consts, 1)
                pool.memset(t["half"][:, :], 0.5).then_inc(consts, 1)
                pool.memset(t["minus_one"][:, :], -1.0).then_inc(consts, 1)
                pool.memset(headmask[:, :], 0.0).then_inc(consts, 1)
                pool.wait_ge(consts, 6)
                pool.affine_select(out=t["ident"][:, :], in_=t["ident"][:, :], compare_op=ALU.not_equal, fill=1.0,
                                   base=0, pattern=[[-1, P]], channel_multiplier=1).then_inc(consts, 1)
                for k in range(4):
                    pool.wait_ge(consts, 7 + k)
                    pool.memset(headmask[32 * k:32 * k + 32, 32 * k:32 * k + 32], 1.0).then_inc(consts, 1)

                def row_scales(blk):
                    p = blk.par
                    pool.wait_ge(mv_ready.sem, mv_ready.at(blk.s))
                    settle(pool, paces)
                    pool.tensor_scalar(ve[:, p, :], mv[:, p, :, 1], LN_EPS, None, ALU.add).then_inc(pool_small.sem, 1)
                    pool.tensor_scalar(negmu[:, p, :], mv[:, p, :, 0], -1.0, None, ALU.mult).then_inc(pool_small.sem, 1)
                    pool.wait_ge(pool_small.sem, pool_small.at(blk.s, 1))
                    pool.tensor_tensor(rstd[:, p, :], ve[:, p, :], t["minus_half"][:, 0:TILES], ALU.pow).then_inc(pool_small.sem, 1)
                    pool.wait_ge(pool_small.sem, pool_small.at(blk.s, 3))
                    settle(pool, paces)
                    pool.tensor_scalar(rstd1[:, p, :], rstd[:, p, :], 1.0, None, ALU.add).then_inc(pool_small.sem, 1)
                    pool.tensor_tensor(negmur[:, p, :], negmu[:, p, :], rstd[:, p, :], ALU.mult).then_inc(pool_small.sem, 1)

                first = Blk(0, 0, B, NB)
                pool.wait_ge(consts, 11)
                row_scales(first)
                row_scales(first.plus(1))

                pool.wait_ge(gate_dve, 2)
                pool.tensor_tensor(simn[:, 1, :], simn[:, 0, :], t["half"][:, 0:8], ALU.pow).then_inc(gate_pool, 1)
                pool.wait_ge(gate_pool, 1)
                pool.tensor_scalar(simn[:, 0, :], simn[:, 1, :], NORM_EPS, None, ALU.max).then_inc(gate_pool, 1)
                pool.wait_ge(gate_pool, 2)
                pool.tensor_tensor(simn[:, 2, :], simn[:, 0, :], t["minus_one"][:, 0:8], ALU.pow).then_inc(gate_pool, 1)
                pool.wait_ge(gate_act, 1)
                pool.tensor_scalar(gates[:, 0, :], gates[:, 1, :], 1.0, None, ALU.add).then_inc(gate_pool, 1)
                pool.wait_ge(gate_pool, 4)
                pool.tensor_tensor(t["sig"][:, :], gates[:, 0, :], t["minus_one"][:, 0:8], ALU.pow).then_inc(gate_pool, 1)
                pool.wait_ge(raw_in, 16 * 7)
                wqkv_raw, wo_raw = w_raw[:, 0:6 * d["E"] * d["D"]], w_raw[:, 6 * d["E"] * d["D"]:]

                def body(blk):
                    after = blk.plus(2)
                    if after is not None:
                        pool.wait_ge(h_ready.sem, h_ready.at(blk.s))
                        pool.wait_ge(base_ready.sem, base_ready.at(blk.s))
                        row_scales(after)
                    parts = []
                    for raw, hi, lo in ((wqkv_raw, t["wqkv_hi"], t["wqkv_lo"]), (wo_raw, t["wo_hi"], t["wo_lo"])):
                        n = raw.shape[1] // (B * NB)
                        cols = bass.ds(blk.s * n, n)
                        pool.tensor_copy(hi[:, cols], raw[:, cols]).then_inc(w_split.sem, 1)
                        parts.append((raw[:, cols], hi[:, cols], lo[:, cols]))
                    for k, (raw, hi, lo) in enumerate(parts):
                        pool.wait_ge(w_split.sem, w_split.at(blk.s, k + 1))
                        pool.tensor_tensor(lo, raw, hi.bitcast(F32), ALU.subtract).then_inc(w_split.sem, 1)
                    pool.wait_ge(feat_ready.sem, feat_ready.at(blk.s))
                    if blk.j == 0:
                        pool.wait_ge(ks_done.sem, ks_done.at(blk.b - 1))
                        settle(pool, paces)
                        pool.tensor_copy(fsum[:, :, :], feat[:, blk.par, :, :]).then_inc(summed.sem, 1)
                    else:
                        pool.wait_ge(summed.sem, summed.at(blk.s - 1))
                        pool.tensor_tensor(fsum[:, :, :], fsum[:, :, :], feat[:, blk.par, :, :], ALU.add).then_inc(summed.sem, 1)

                loop_blocks(pool, B, NB, body)

            @block.vector
            def _(dve):
                fold_lo.grant(dve)
                dve.wait_ge(w_in, 16)
                dve.tensor_copy(wq_hi[:, :, :], wq_raw[:, :, :]).then_inc(wq_split, 1)
                dve.wait_ge(wq_split, 1)
                dve.tensor_tensor(wq_lo[:, :, :], wq_raw[:, :, :], wq_hi[:, :, :].bitcast(F32), ALU.subtract).then_inc(wq_split, 1)

                def moments(blk):
                    p = blk.par
                    dve.wait_ge(x_in[p].sem, x_in[p].at(blk.turn))
                    for i in range(TILES):
                        dve.bn_stats(stats[:, p, i, :], x[:, p, i, :]).then_inc(st_ready.sem, 1)
                    dve.wait_ge(st_ready.sem, st_ready.at(blk.s))
                    settle(dve, paces)
                    for i in range(TILES):
                        dve.bn_aggr(mv[:, p, i, :], stats[:, p, i, :]).then_inc(mv_ready.sem, 1)

                def normalise(blk):
                    p = blk.par
                    dve.wait_ge(pool_small.sem, pool_small.at(blk.s))
                    for i in range(TILES):
                        dve.tensor_scalar(h[:, p, i, :], x[:, p, i, :], mv[:, p, i, 0:1], rstd[:, p, i:i + 1],
                                          ALU.subtract, ALU.mult).then_inc(h_ready.sem, 1)

                def split_low(blk):
                    for half in range(2):
                        dve.wait_ge(hi_ready.sem, hi_ready.at(blk.s, half + 1))
                        dve.tensor_tensor(hT_lo[:, half, :], trp[half][:, :], hT_hi[:, half, :].bitcast(F32),
                                          ALU.subtract).then_inc(lo_ready.sem, 1)

                def features(blk, slot_waits=True):
                    if slot_waits:
                        dve.wait_ge(feat_out[blk.par].sem, feat_out[blk.par].at(blk.turn - 1))
                        dve.wait_ge(summed.sem, summed.at(blk.s - 2))
                    for bank in range(2):
                        dve.wait_ge(exp_ready.sem, exp_ready.at(blk.s, bank + 1))
                        dve.scalar_tensor_tensor(out=feat[:, blk.par, 2 * bank:2 * bank + 2, :],
                                                 in0=q[:, 2 * bank:2 * bank + 2, :], scalar=0.0,
                                                 in1=expneg[:, bank, :, :], op0=ALU.max, op1=ALU.add).then_inc(feat_ready.sem, 1)

                first = Blk(0, 0, B, NB)
                moments(first)
                moments(first.plus(1))
                normalise(first)
                normalise(first.plus(1))
                dve.memset(t["sn_hi"][:, :, :].bitcast(F32), 0.0).then_inc(gate_dve, 0 + 1)
                dve.memset(t["sn_lo"][:, :, :].bitcast(F32), 0.0).then_inc(w2_split, 1)
                dve.wait_ge(small_in, 16 * 5)
                dve.tensor_tensor(simsq[:, :, :], sim[:, :, :], sim[:, :, :], ALU.mult).then_inc(wq_split, 1)
                dve.wait_ge(gate_pe, 1)
                dve.tensor_copy(simn[:, 0, :], misc[0][:, 0:8]).then_inc(gate_dve, 1)
                dve.wait_ge(gate_pool, 3)
                for half in range(2):
                    dve.tensor_tensor(sn[:, half, :], sim[:, half, :], simn[:, 2, :], ALU.mult).then_inc(gate_dve, 1)
                dve.wait_ge(gate_dve, 4)
                dve.tensor_copy(t["sn_hi"][:, :, 0:8], sn[:, :, :]).then_inc(gate_dve, 1)
                dve.wait_ge(gate_dve, 5)
                dve.wait_ge(w2_split, 1)
                dve.tensor_tensor(t["sn_lo"][:, :, 0:8], sn[:, :, :], t["sn_hi"][:, :, 0:8].bitcast(F32), ALU.subtract).then_inc(gate_dve, 1)
                split_low(first)
                dve.tensor_copy(t["w2_hi"][:, :, :], w2_raw[:, :, :]).then_inc(w2_split, 1)
                dve.wait_ge(w2_split, 2)
                dve.tensor_tensor(t["w2_lo"][:, :, :], w2_raw[:, :, :], t["w2_hi"][:, :, :].bitcast(F32), ALU.subtract).then_inc(w2_split, 1)
                features(first, slot_waits=False)
                def body(blk):
                    nxt, after = blk.plus(1), blk.plus(2)
                    if nxt is not None:
                        split_low(nxt)
                    if after is not None:
                        moments(after)
                    if nxt is not None:
                        features(nxt)
                    if after is not None:
                        dve.wait_ge(transposed.sem, transposed.at(blk.s))
                        normalise(after)
                    if blk.j == NB - 1:
                        dve.wait_ge(kv_done.sem, kv_done.at(blk.b))
                        for half in range(2):
                            dve.tensor_tensor(kvT[:, half, :], kvp[half][:, 0, half * P:(half + 1) * P], headmask[:, :],
                                              ALU.mult).then_inc(kv_masked.sem, 1)
                        dve.wait_ge(fold_out.sem, fold_out.at(blk.b - 1))
                        dve.wait_ge(fold_hi.sem, fold_hi.at(blk.b, 1))
                        dve.tensor_tensor(g_st_lo[:, :], misc[1][:, :], g_st_hi[:, :].bitcast(F32), ALU.subtract).then_inc(fold_lo.sem, 1)
                        for half, bank in enumerate((misc[0][:, :], kvp[1][:, :, :].rearrange("p a n -> p (a n)"))):
                            dve.wait_ge(fold_hi.sem, fold_hi.at(blk.b, 2 + half))
                            dve.tensor_tensor(gw_st_lo[:, half, :], bank, gw_st_hi[:, half, :].bitcast(F32),
                                              ALU.subtract).then_inc(fold_lo.sem, 1)

                loop_blocks(dve, B, NB, body)

            @block.scalar
            def _(act):
                def split_high(blk):
                    for half in range(2):
                        act.wait_ge(transposed.sem, transposed.at(blk.s, half + 1))
                        act.activation(hT_hi[:, half, :], trp[half][:, :], ACT.Copy).then_inc(hi_ready.sem, 1)

                def exps(blk, slot_waits=True):
                    for bank in range(2):
                        act.wait_ge(q_done.sem, q_done.at(blk.s, bank + 1))
                        if slot_waits:
                            act.wait_ge(feat_ready.sem, feat_ready.at(blk.s - 1, bank + 1))
                        act.activation(negpart[:, bank, :, :], qp[bank][:, :, :], ACT.Relu, scale=-1.0).then_inc(neg_ready.sem, 1)
                        act.activation(q[:, 2 * bank:2 * bank + 2, :], qp[bank][:, :, :], ACT.Copy).then_inc(q_copied.sem, 1)
                        act.wait_ge(neg_ready.sem, neg_ready.at(blk.s, bank + 1))
                        act.wait_ge(q_copied.sem, q_copied.at(blk.s, bank + 1))
                        act.activation(expneg[:, bank, :, :], negpart[:, bank, :, :], ACT.Exp, scale=-1.0).then_inc(exp_ready.sem, 1)

                def residual(blk):
                    p = blk.par
                    act.wait_ge(pool_small.sem, pool_small.at(blk.s))
                    act.wait_ge(x_in[p].sem, x_in[p].at(blk.turn))
                    for i in range(TILES):
                        act.activation(base[:, p, i, :], x[:, p, i, :], ACT.Identity, scale=rstd1[:, p, i:i + 1],
                                       bias=negmur[:, p, i:i + 1]).then_inc(base_ready.sem, 1)

                act.wait_ge(small_in, 16 * 5)
                act.activation(gates[:, 1, :], gates[:, 0, :], ACT.Exp, scale=-1.0).then_inc(gate_act, 1)
                first = Blk(0, 0, B, NB)
                split_high(first)
                exps(first, slot_waits=False)
                residual(first)
                residual(first.plus(1))

                def body(blk):
                    nxt, after = blk.plus(1), blk.plus(2)
                    if nxt is not None:
                        split_high(nxt)
                        exps(nxt)
                    if after is not None:
                        act.wait_ge(base_out[blk.par].sem, base_out[blk.par].at(blk.turn))
                        residual(after)
                    if blk.j == NB - 1:
                        act.wait_ge(fold_out.sem, fold_out.at(blk.b - 1))
                        act.wait_ge(ks_done.sem, ks_done.at(blk.b))
                        act.activation(ks_st[:, :], misc[0][:, 0:C], ACT.Copy).then_inc(ks_copied.sem, 1)
                        act.wait_ge(g_done.sem, g_done.at(blk.b))
                        act.activation(g_st_hi[:, :], misc[1][:, :], ACT.Copy).then_inc(fold_hi.sem, 1)
                        act.wait_ge(gT_done.sem, gT_done.at(blk.b))
                        act.activation(gT[:, :, :], kvp[0][:, :, :], ACT.Copy).then_inc(gT_copied.sem, 1)
                        for half, bank in enumerate((misc[0][:, :], kvp[1][:, :, :].rearrange("p a n -> p (a n)"))):
                            act.wait_ge(gw_done.sem, gw_done.at(blk.b, half + 1))
                            act.activation(gw_st_hi[:, half, :], bank, ACT.Copy).then_inc(fold_hi.sem, 1)

                loop_blocks(act, B, NB, body)

            @block.tensor
            def _(pe):
                ks_done.grant(pe)
                ident = t["ident"]

                def transposes(blk):
                    for half in range(2):
                        for i in range(TILES):
                            pe.wait_ge(h_ready.sem, h_ready.at(blk.s, i + 1))
                            last = pe.transpose(trp[half][:, i * P:(i + 1) * P], h[:, blk.par, i, half * P:(half + 1) * P], ident[:, :])
                        last.then_inc(transposed.sem, 1)

                def project_q(blk):
                    for half in range(2):
                        pe.wait_ge(lo_ready.sem, lo_ready.at(blk.s, half + 1))
                    for i in range(TILES):
                        cols = slice(i * P, (i + 1) * P)
                        last = product(pe, qp[i // 2][:, i % 2, :],
                                       [((hT_hi[:, hf, cols], hT_lo[:, hf, cols]), (wq_hi[:, hf, :], wq_lo[:, hf, :]))
                                        for hf in range(2)])
                        if i % 2:
                            last.then_inc(q_done.sem, 1)

                first = Blk(0, 0, B, NB)
                pe.wait_ge(consts, 11)
                pe.wait_ge(wq_split, 3)
                for half in range(2):
                    last = pe.matmul(misc[0][:, 0:8], ones[:, :], simsq[:, half, :], start=(half == 0), stop=(half == 1))
                last.then_inc(gate_pe, 1)
                transposes(first)
                project_q(first)

                def body(blk):
                    nxt = blk.plus(1)
                    if nxt is not None:
                        pe.wait_ge(lo_ready.sem, lo_ready.at(blk.s))
                        transposes(nxt)
                    if blk.j == 0:
                        pe.wait_ge(fold_lo.sem, fold_lo.at(blk.b - 1))
                    for i in range(TILES):
                        pe.wait_ge(feat_ready.sem, feat_ready.at(blk.s, i // 2 + 1))
                        for half in range(2):
                            last = pe.matmul(kvp[half][:, 0, :], q[:, i, half * P:(half + 1) * P], feat[:, blk.par, i, :],
                                             start=(blk.j == 0 and i == 0), stop=(blk.j == NB - 1 and i == TILES - 1))
                    if blk.j == NB - 1:
                        last.then_inc(kv_done.sem, 1)
                    if nxt is not None:
                        pe.wait_ge(exp_ready.sem, exp_ready.at(blk.s))
                        project_q(nxt)
                    if blk.j == NB - 1:
                        fold(blk)

                def fold(blk):
                    pe.wait_ge(summed.sem, summed.at(blk.s))
                    for i in range(TILES):
                        last = pe.matmul(misc[0][:, 0:C], ones[:, :], fsum[:, i, :], start=(i == 0), stop=(i == TILES - 1))
                    last.then_inc(ks_done.sem, 1)
                    pe.wait_ge(kv_masked.sem, kv_masked.at(blk.b))
                    for half in range(2):
                        last = pe.matmul(misc[1][:, half * C:(half + 1) * C], kvT[:, half, :], wm[:, half, :], start=True, stop=True)
                    last.then_inc(g_done.sem, 1)
                    for nh in range(2):
                        for half in range(2):
                            last = pe.matmul(kvp[0][:, nh, half * P:(half + 1) * P], wm[:, half, nh * P:(nh + 1) * P],
                                             kvT[:, half, :], start=True, stop=True)
                    last.then_inc(gT_done.sem, 1)
                    pe.wait_ge(gT_copied.sem, gT_copied.at(blk.b))
                    pe.wait_ge(ks_copied.sem, ks_copied.at(blk.b))
                    for half, bank in enumerate((misc[0][:, :], kvp[1][:, :, :].rearrange("p a n -> p (a n)"))):
                        for nh in range(2):
                            last = pe.matmul(bank, gT[:, nh, half * P:(half + 1) * P], w1[:, nh, :], start=(nh == 0), stop=(nh == 1))
                        last.then_inc(gw_done.sem, 1)

                loop_blocks(pe, B, NB, body)


def stage2(nc, t, d):
    B, NB, C, E, D = d["B"], d["NB"], d["C"], d["E"], d["D"]
    W3 = 3 * D
    CH = TILES * E
    with ExitStack() as st:
        c = Ctx(nc, st, "b_")
        feat = c.sb("feat", [P, 2, TILES, C])
        base = c.sb("base", [P, 2, TILES, C])
        ksum = c.sb("ksum", [P, C])
        g_hi = c.sb("g_hi", [P, 2, C], F32R)
        g_lo = c.sb("g_lo", [P, 2, C], F32R)
        gw_hi = c.sb("gw_hi", [P, 2, 2 * C], F32R)
        gw_lo = c.sb("gw_lo", [P, 2, 2 * C], F32R)
        den = c.sb("den", [P, 2, TILES * 8])
        z = c.sb("z", [P, TILES * 8])
        fz = c.sb("fz", [P, TILES, C])
        fT_hi = c.sb("fT_hi", [P, 2, BLOCK], F32R)
        fT_lo = c.sb("fT_lo", [P, 2, BLOCK], F32R)
        hid_hi = c.sb("hid_hi", [P, 4, BLOCK], F32R)
        hid_lo = c.sb("hid_lo", [P, 4, BLOCK], F32R)
        g1b = c.sb("g1b", [P, C])
        g2b = c.sb("g2b", [P, C])
        b1b = c.sb("b1b", [P, C])
        b2b = c.sb("b2b", [P, C])
        b12 = c.sb("b12", [P, C])
        stats = c.sb("stats", [P, 3, TILES, 6])
        mv = c.sb("mv", [P, 3, TILES, 2])
        ve = c.sb("ve", [P, 3, TILES])
        rstd = c.sb("rstd", [P, 3, TILES])
        negmu = c.sb("negmu", [P, TILES])
        negmur = c.sb("negmur", [P, TILES])
        nrm = c.sb("nrm", [P, 4, TILES])
        rnorm = c.sb("rnorm", [P, TILES])
        u = c.sb("u", [P, 2, TILES, C])
        x1 = c.sb("x1", [P, 2, TILES, C])
        h2 = c.sb("h2", [P, TILES, C])
        h2T_hi = c.sb("h2T_hi", [P, 2, 2, BLOCK], F32R)
        h2T_lo = c.sb("h2T_lo", [P, 2, 2, BLOCK], F32R)
        lg = c.sb("lg", [P, TILES, E])
        logit = c.sb("logit", [P, TILES, E])
        above = c.sb("above", [P, TILES, E, E])
        atleast = c.sb("atleast", [P, TILES, E, E])
        before = c.sb("before", [P, E, E])
        notbefore = c.sb("notbefore", [P, E, E])
        rank = c.sb("rank", [P, TILES, E])
        top = c.sb("top", [P, 3, TILES])
        fallback = c.sb("fallback", [P, TILES, E])
        positive = c.sb("positive", [P, TILES, E])
        mask = c.sb("mask", [P, 2, TILES, E])
        gated = c.sb("gated", [P, TILES, E])
        expo = c.sb("expo", [P, 2, TILES, E])
        halves = c.sb("halves", [P, TILES, 6])
        total = c.sb("total", [P, 2, TILES])
        route = c.sb("route", [P, 2, TILES, E])
        acc = c.sb("acc", [P, 2, W3])
        v_hi = c.sb("v_hi", [P, 2, TILES, D], F32R)
        v_lo = c.sb("v_lo", [P, 2, TILES, D], F32R)
        qk_hi = c.sb("qk_hi", [P, 2, 2, BLOCK], F32R)
        qk_lo = c.sb("qk_lo", [P, 2, 2, BLOCK], F32R)

        F = [c.ps(f"F{i}", [P, BLOCK]) for i in range(4)]
        X = [c.ps(f"X{i}", [P, W3]) for i in range(2)]
        QK = [c.ps(f"QK{i}", [P, BLOCK]) for i in range(2)]

        setup_in = c.sem("setup_in")
        setup = c.sem("setup")
        feat_in = [c.flag(f"feat_in{i}", 16) for i in range(2)]
        base_in = [c.flag(f"base_in{i}", 16) for i in range(2)]
        ks_in = c.flag("ks_in", 16)
        fold_in = c.flag("fold_in", 16 * 4)
        prod_ready = c.flag("prod_ready", 1)
        den_ready = c.flag("den_ready", 1)
        z_steps = c.flag("z_steps", 2)
        fz_ready = c.flag("fz_ready", 1)
        res_ready = c.flag("res_ready", 1)
        f_transposed = c.flag("f_transposed", 2)
        f_hi = c.flag("f_hi", 2)
        f_lo = c.flag("f_lo", 2)
        msg_done = c.flag("msg_done", 2)
        hid_done = c.flag("hid_done", 4)
        h_hi = c.flag("h_hi", 4)
        h_lo = c.flag("h_lo", 4)
        mlp_done = c.flag("mlp_done", 2)
        st_ready = c.flag("st_ready", 3 * TILES)
        mv_ready = c.flag("mv_ready", 3 * TILES)
        rstd_steps = c.flag("rstd_steps", 6)
        h2_steps = c.flag("h2_steps", 2)
        rn_steps = c.flag("rn_steps", 5)
        u_ready = c.flag("u_ready", 2 * TILES)
        x1_steps = c.flag("x1_steps", 2 * TILES)
        x1_out = [c.flag(f"x1_out{i}", 16, ahead=1) for i in range(2)]
        h2_ready = c.flag("h2_ready", TILES)
        h2_transposed = c.flag("h2_transposed", 2)
        h2_hi = c.flag("h2_hi", 2)
        h2_lo = c.flag("h2_lo", 2)
        lg_done = c.flag("lg_done", 2)
        lg_ready = c.flag("lg_ready", 2)
        gate_steps = c.flag("gate_steps", 8)
        top_steps = c.flag("top_steps", 3)
        route_steps = c.flag("route_steps", 5)
        mask_ready = c.flag("mask_ready", 1)
        expo_in = c.flag("expo_in", 1)
        expo_ready = c.flag("expo_ready", 1)
        route_ready = c.flag("route_ready", 1, ahead=1)
        route_out = [c.flag(f"route_out{i}", 16, ahead=1) for i in range(2)]
        expert_done = c.flag("expert_done", CH)
        combined = c.flag("combined", CH, ahead=1)
        qk_transposed = c.flag("qk_transposed", TILES, ahead=1)
        v_hi_ready = c.flag("v_hi_ready", TILES)
        v_lo_ready = c.flag("v_lo_ready", TILES, ahead=1)
        v_out = [c.flag(f"v_out{i}", 32, ahead=1) for i in range(2)]
        qk_hi_ready = c.flag("qk_hi_ready", 2)
        qk_lo_ready = c.flag("qk_lo_ready", 2, ahead=1)
        qk_out = [c.flag(f"qk_out{i}", 64, ahead=1) for i in range(2)]

        first = Blk(0, 0, B, NB)
        turns = B * NB // 2

        paces = {e.engine: c.sem(f"pace_{k}") for k, e in enumerate((nc.sync, nc.gpsimd, nc.vector))}

        with nc.Block() as block:

            @block.sync
            def _(sp):
                for g in (*x1_out, *route_out, *v_out, *qk_out):
                    g.grant(sp)

                def load_feat(blk):
                    sp.dma_start(feat[:, blk.par, :, :], rows(t["feat"], blk, C)).then_inc(feat_in[blk.par].sem, 16)

                def load_base(blk):
                    sp.dma_start(base[:, blk.par, :, :], rows(t["base"], blk, C)).then_inc(base_in[blk.par].sem, 16)

                def load_ksum(b):
                    sp.dma_start(ksum[:, :], t["ks"][bass.ds(b * P, P), :]).then_inc(ks_in.sem, 16)

                def load_fold(b):
                    r = bass.ds(b * P, P)
                    sp.dma_start(g_hi[:, :, :].bitcast(F32).rearrange("p h n -> p (h n)"), t["g_hi"][r, :]).then_inc(fold_in.sem, 16)
                    sp.dma_start(g_lo[:, :, :].bitcast(F32).rearrange("p h n -> p (h n)"), t["g_lo"][r, :]).then_inc(fold_in.sem, 16)
                    sp.dma_start(gw_hi[:, :, :].bitcast(F32).rearrange("p h n -> p (h n)"), t["gw_hi"][r, :]).then_inc(fold_in.sem, 16)
                    sp.dma_start(gw_lo[:, :, :].bitcast(F32).rearrange("p h n -> p (h n)"), t["gw_lo"][r, :]).then_inc(fold_in.sem, 16)

                load_ksum(0)
                load_feat(first)
                load_fold(0)
                load_base(first)
                load_feat(first.plus(1))
                load_base(first.plus(1))
                for dst, name in ((g1b, "g1"), (g2b, "g2"), (b1b, "b1"), (b2b, "b2")):
                    sp.dma_start(dst[:, :], t[name].partition_broadcast(P)).then_inc(setup_in, 16)

                def body(blk):
                    nxt, after = blk.plus(1), blk.plus(2)
                    if after is not None:
                        sp.wait_ge(fz_ready.sem, fz_ready.at(blk.s))
                        settle(sp, paces)
                        load_feat(after)
                        sp.wait_ge(res_ready.sem, res_ready.at(blk.s))
                        settle(sp, paces)
                        load_base(after)
                    if blk.j == NB - 2 and after is not None:
                        sp.wait_ge(prod_ready.sem, prod_ready.at(nxt.s))
                        settle(sp, paces)
                        load_ksum(after.b)
                        sp.wait_ge(hid_done.sem, hid_done.at(nxt.s))
                        settle(sp, paces)
                        load_fold(after.b)
                    sp.wait_ge(v_lo_ready.sem, v_lo_ready.at(blk.s))
                    settle(sp, paces)
                    sp.dma_start(rows(t["v_hi"], blk, D), v_hi[:, blk.par, :, :].bitcast(F32)).then_inc(v_out[blk.par].sem, 16)
                    sp.dma_start(rows(t["v_lo"], blk, D), v_lo[:, blk.par, :, :].bitcast(F32)).then_inc(v_out[blk.par].sem, 16)
                    cols = bass.ds(blk.s * BLOCK, BLOCK)
                    for name, src, ready in (("T_hi", qk_hi, qk_hi_ready), ("T_lo", qk_lo, qk_lo_ready)):
                        sp.wait_ge(ready.sem, ready.at(blk.s))
                        settle(sp, paces)
                        for i, w in enumerate("qk"):
                            sp.dma_start(t[w + name][:, cols], src[:, blk.par, i, :].bitcast(F32)).then_inc(qk_out[blk.par].sem, 16)
                    if nxt is not None:
                        store_front(nxt)

                def store_front(blk):
                    sp.wait_ge(x1_steps.sem, x1_steps.at(blk.s))
                    settle(sp, paces)
                    sp.dma_start(rows(t["x1"], blk, C), x1[:, blk.par, :, :]).then_inc(x1_out[blk.par].sem, 16)
                    sp.wait_ge(route_ready.sem, route_ready.at(blk.s))
                    settle(sp, paces)
                    sp.dma_start(rows(t["route"], blk, E), route[:, blk.par, :, :]).then_inc(route_out[blk.par].sem, 16)

                store_front(first)
                loop_blocks(sp, B, NB, body)
                for par in range(2):
                    for g in (x1_out, route_out, v_out, qk_out):
                        sp.wait_ge(g[par].sem, g[par].at(turns - 1))
                        settle(sp, paces)

            @block.gpsimd
            def _(pool):
                v_lo_ready.grant(pool)
                route_ready.grant(pool)
                pool.memset(before[:, :, :], 1.0).then_inc(setup, 1)
                pool.wait_ge(setup, 1)
                pool.affine_select(out=before[:, :, :], in_=before[:, :, :], compare_op=ALU.is_gt, fill=0.0, base=0,
                                   pattern=[[1, E], [-1, E]], channel_multiplier=0).then_inc(setup, 1)
                pool.wait_ge(setup, 2)
                pool.tensor_scalar(notbefore[:, :, :], before[:, :, :], -1.0, 1.0, ALU.mult, ALU.add).then_inc(setup, 1)
                pool.wait_ge(setup_in, 64)
                pool.tensor_tensor(b12[:, :], b1b[:, :], b2b[:, :], ALU.add).then_inc(setup, 1)
                pool.wait_ge(setup, 4)

                def ksum_product(blk):
                    pool.wait_ge(feat_in[blk.par].sem, feat_in[blk.par].at(blk.turn))
                    pool.wait_ge(ks_in.sem, ks_in.at(blk.b))
                    if not (isinstance(blk.s, int) and blk.s == 0):
                        pool.wait_ge(f_transposed.sem, f_transposed.at(blk.s - 1))
                    pool.tensor_tensor(fz[:, :, :], feat[:, blk.par, :, :],
                                       ksum[:, :].unsqueeze(1).to_broadcast([P, TILES, C]), ALU.mult).then_inc(prod_ready.sem, 1)

                def normalise_feat(blk):
                    pool.wait_ge(den_ready.sem, den_ready.at(blk.s))
                    settle(pool, paces)
                    pool.tensor_scalar(den[:, 1, :], den[:, 0, :], ATTN_EPS, None, ALU.add).then_inc(z_steps.sem, 1)
                    pool.wait_ge(z_steps.sem, z_steps.at(blk.s, 1))
                    pool.tensor_tensor(z[:, :], den[:, 1, :], t["minus_one"][:, :], ALU.pow).then_inc(z_steps.sem, 1)
                    pool.wait_ge(z_steps.sem, z_steps.at(blk.s, 2))
                    pool.tensor_tensor(fz[:, :, :].rearrange("p t (h k) -> p (t h) k", h=8),
                                       feat[:, blk.par, :, :].rearrange("p t (h k) -> p (t h) k", h=8),
                                       z[:, :].unsqueeze(2).to_broadcast([P, TILES * 8, C // 8]), ALU.mult).then_inc(fz_ready.sem, 1)

                def residual(blk):
                    pool.wait_ge(base_in[blk.par].sem, base_in[blk.par].at(blk.turn))
                    pool.wait_ge(x1_out[blk.par].sem, x1_out[blk.par].at(blk.turn - 1))
                    pool.tensor_tensor(x1[:, blk.par, :, :], base[:, blk.par, :, :],
                                       b12[:, :].unsqueeze(1).to_broadcast([P, TILES, C]), ALU.add).then_inc(res_ready.sem, 1)

                def rstds(blk, n):
                    pool.wait_ge(mv_ready.sem, mv_ready.at(blk.s, (n + 1) * TILES))
                    settle(pool, paces)
                    pool.tensor_scalar(ve[:, n, :], mv[:, n, :, 1], LN_EPS, None, ALU.add).then_inc(rstd_steps.sem, 1)
                    pool.wait_ge(rstd_steps.sem, rstd_steps.at(blk.s, 2 * n + 1))
                    pool.tensor_tensor(rstd[:, n, :], ve[:, n, :], t["minus_half"][:, 0:TILES], ALU.pow).then_inc(rstd_steps.sem, 1)

                def x1_scales(blk):
                    pool.wait_ge(rstd_steps.sem, rstd_steps.at(blk.s))
                    settle(pool, paces)
                    pool.tensor_scalar(negmu[:, :], mv[:, 2, :, 0], -1.0, None, ALU.mult).then_inc(h2_steps.sem, 1)
                    pool.wait_ge(h2_steps.sem, h2_steps.at(blk.s, 1))
                    pool.tensor_tensor(negmur[:, :], negmu[:, :], rstd[:, 2, :], ALU.mult).then_inc(h2_steps.sem, 1)
                    pool.tensor_scalar(nrm[:, 0, :], mv[:, 2, :, 1], float(C), None, ALU.mult).then_inc(rn_steps.sem, 1)
                    pool.wait_ge(rn_steps.sem, rn_steps.at(blk.s, 1))
                    pool.tensor_tensor(nrm[:, 1, :], nrm[:, 0, :], t["half"][:, 0:TILES], ALU.pow).then_inc(rn_steps.sem, 1)
                    pool.wait_ge(rn_steps.sem, rn_steps.at(blk.s, 2))
                    pool.tensor_tensor(nrm[:, 2, :], nrm[:, 1, :], rstd[:, 2, :], ALU.mult).then_inc(rn_steps.sem, 1)
                    pool.wait_ge(rn_steps.sem, rn_steps.at(blk.s, 3))
                    settle(pool, paces)
                    pool.tensor_scalar(nrm[:, 3, :], nrm[:, 2, :], NORM_EPS, None, ALU.max).then_inc(rn_steps.sem, 1)
                    pool.wait_ge(rn_steps.sem, rn_steps.at(blk.s, 4))
                    pool.tensor_tensor(rnorm[:, :], nrm[:, 3, :], t["minus_one"][:, 0:TILES], ALU.pow).then_inc(rn_steps.sem, 1)

                def routing(blk):
                    p = blk.par
                    pool.wait_ge(expo_ready.sem, expo_ready.at(blk.s))
                    pool.wait_ge(mask_ready.sem, mask_ready.at(blk.s))
                    pool.tensor_tensor(expo[:, 1, :, :], expo[:, 0, :, :], mask[:, p, :, :], ALU.mult).then_inc(route_steps.sem, 1)
                    pool.wait_ge(route_steps.sem, route_steps.at(blk.s, 1))
                    pool.tensor_tensor(halves[:, :, 0:4], expo[:, 1, :, 0:4], expo[:, 1, :, 4:8], ALU.add).then_inc(route_steps.sem, 1)
                    pool.wait_ge(route_steps.sem, route_steps.at(blk.s, 2))
                    pool.tensor_tensor(halves[:, :, 4:6], halves[:, :, 0:2], halves[:, :, 2:4], ALU.add).then_inc(route_steps.sem, 1)
                    pool.wait_ge(route_steps.sem, route_steps.at(blk.s, 3))
                    pool.tensor_tensor(total[:, 0, :], halves[:, :, 4], halves[:, :, 5], ALU.add).then_inc(route_steps.sem, 1)
                    pool.wait_ge(route_steps.sem, route_steps.at(blk.s, 4))
                    pool.tensor_tensor(total[:, 1, :], total[:, 0, :], t["minus_one"][:, 0:TILES], ALU.pow).then_inc(route_steps.sem, 1)
                    pool.wait_ge(route_steps.sem, route_steps.at(blk.s, 5))
                    pool.wait_ge(route_out[p].sem, route_out[p].at(blk.turn - 1))
                    pool.tensor_tensor(route[:, p, :, :], expo[:, 1, :, :],
                                       total[:, 1, :].unsqueeze(2).to_broadcast([P, TILES, E]), ALU.mult).then_inc(route_ready.sem, 1)

                def v_low(blk, i):
                    p = blk.par
                    if i == 0:
                        pool.wait_ge(v_out[p].sem, v_out[p].at(blk.turn - 1))
                    pool.wait_ge(v_hi_ready.sem, v_hi_ready.at(blk.s, i + 1))
                    pool.tensor_tensor(v_lo[:, p, i, :], acc[:, i % 2, 2 * D:], v_hi[:, p, i, :].bitcast(F32),
                                       ALU.subtract).then_inc(v_lo_ready.sem, 1)

                ksum_product(first)
                normalise_feat(first)
                residual(first)
                rstds(first, 0)
                rstds(first, 1)
                rstds(first, 2)
                x1_scales(first)
                ksum_product(first.plus(1))
                routing(first)

                def body(blk):
                    nxt, after = blk.plus(1), blk.plus(2)
                    if nxt is not None:
                        normalise_feat(nxt)
                        residual(nxt)
                    v_low(blk, 0)
                    if nxt is not None:
                        rstds(nxt, 0)
                    v_low(blk, 1)
                    if nxt is not None:
                        rstds(nxt, 1)
                    if nxt is not None:
                        rstds(nxt, 2)
                        x1_scales(nxt)
                    v_low(blk, 2)
                    if after is not None:
                        ksum_product(after)
                    v_low(blk, 3)
                    if nxt is not None:
                        routing(nxt)

                loop_blocks(pool, B, NB, body)

            @block.scalar
            def _(act):
                def f_high(blk):
                    for half in range(2):
                        act.wait_ge(f_transposed.sem, f_transposed.at(blk.s, half + 1))
                        act.activation(fT_hi[:, half, :], F[half][:, :], ACT.Copy).then_inc(f_hi.sem, 1)

                def hidden_high(blk, k):
                    act.wait_ge(hid_done.sem, hid_done.at(blk.s, k + 1))
                    act.activation(hid_hi[:, k, :], F[k % 2][:, :], ACT.Relu).then_inc(h_hi.sem, 1)

                def normalise_x1(blk):
                    act.wait_ge(h2_steps.sem, h2_steps.at(blk.s))
                    act.wait_ge(x1_steps.sem, x1_steps.at(blk.s))
                    for i in range(TILES):
                        act.activation(h2[:, i, :], x1[:, blk.par, i, :], ACT.Identity, scale=rstd[:, 2, i:i + 1],
                                       bias=negmur[:, i:i + 1]).then_inc(h2_ready.sem, 1)

                def h2_high(blk):
                    for half in range(2):
                        act.wait_ge(h2_transposed.sem, h2_transposed.at(blk.s, half + 1))
                        act.activation(h2T_hi[:, blk.par, half, :], F[2 + half][:, :], ACT.Copy).then_inc(h2_hi.sem, 1)

                def gate_exp(blk):
                    act.wait_ge(expo_in.sem, expo_in.at(blk.s))
                    act.activation(expo[:, 0, :, :], gated[:, :, :], ACT.Exp).then_inc(expo_ready.sem, 1)

                def v_high(blk, i):
                    act.wait_ge(combined.sem, combined.at(blk.s, (i + 1) * E))
                    if i == 0:
                        act.wait_ge(v_out[blk.par].sem, v_out[blk.par].at(blk.turn - 1))
                    act.activation(v_hi[:, blk.par, i, :], acc[:, i % 2, 2 * D:], ACT.Copy).then_inc(v_hi_ready.sem, 1)

                def qk_high(blk):
                    act.wait_ge(qk_out[blk.par].sem, qk_out[blk.par].at(blk.turn - 1))
                    act.wait_ge(qk_transposed.sem, qk_transposed.at(blk.s))
                    for k in range(2):
                        act.activation(qk_hi[:, blk.par, k, :], QK[k][:, :], ACT.Copy).then_inc(qk_hi_ready.sem, 1)

                f_high(first)
                for k in range(4):
                    hidden_high(first, k)
                normalise_x1(first)
                h2_high(first)
                gate_exp(first)

                def body(blk):
                    nxt = blk.plus(1)
                    if nxt is not None:
                        f_high(nxt)
                    v_high(blk, 0)
                    if nxt is not None:
                        for k in range(4):
                            hidden_high(nxt, k)
                    v_high(blk, 1)
                    if nxt is not None:
                        normalise_x1(nxt)
                    v_high(blk, 2)
                    if nxt is not None:
                        h2_high(nxt)
                    v_high(blk, 3)
                    qk_high(blk)
                    if nxt is not None:
                        gate_exp(nxt)

                loop_blocks(act, B, NB, body)

            @block.vector
            def _(dve):
                combined.grant(dve)
                qk_lo_ready.grant(dve)
                msg = [F[2 + i // 2][:, (i % 2) * C:(i % 2 + 1) * C] for i in range(TILES)]
                mlp = [F[i // 2][:, (i % 2) * C:(i % 2 + 1) * C] for i in range(TILES)]

                def denominators(blk):
                    dve.wait_ge(prod_ready.sem, prod_ready.at(blk.s))
                    dve.tensor_reduce(den[:, 0, :], fz[:, :, :].rearrange("p t (h k) -> p (t h) k", h=8),
                                      AX_X, ALU.add).then_inc(den_ready.sem, 1)

                def f_low(blk, half):
                    dve.wait_ge(f_hi.sem, f_hi.at(blk.s, half + 1))
                    dve.tensor_tensor(fT_lo[:, half, :], F[half][:, :], fT_hi[:, half, :].bitcast(F32),
                                      ALU.subtract).then_inc(f_lo.sem, 1)

                def moments(blk, n, i):
                    if n == 0:
                        dve.wait_ge(msg_done.sem, msg_done.at(blk.s, i // 2 + 1))
                    elif n == 1:
                        dve.wait_ge(mlp_done.sem, mlp_done.at(blk.s, i // 2 + 1))
                    else:
                        dve.wait_ge(x1_steps.sem, x1_steps.at(blk.s, TILES + i + 1))
                    src = (msg[i], mlp[i], x1[:, blk.par, i, :])[n]
                    dve.bn_stats(stats[:, n, i, :], src).then_inc(st_ready.sem, 1)

                def gather(blk, n):
                    dve.wait_ge(st_ready.sem, st_ready.at(blk.s, (n + 1) * TILES))
                    settle(dve, paces)
                    for i in range(TILES):
                        dve.bn_aggr(mv[:, n, i, :], stats[:, n, i, :]).then_inc(mv_ready.sem, 1)

                def centre(blk, n, i):
                    dve.wait_ge(mv_ready.sem, mv_ready.at(blk.s, n * TILES + i + 1))
                    dve.scalar_tensor_tensor(out=u[:, n, i, :], in0=(msg, mlp)[n][i], scalar=mv[:, n, i, 0:1],
                                             in1=(g1b, g2b)[n][:, :], op0=ALU.subtract, op1=ALU.mult).then_inc(u_ready.sem, 1)

                def add_norm(blk, n, i):
                    dve.wait_ge(u_ready.sem, u_ready.at(blk.s, n * TILES + i + 1))
                    dve.wait_ge(rstd_steps.sem, rstd_steps.at(blk.s, 2 * n + 2))
                    if n == 0:
                        dve.wait_ge(res_ready.sem, res_ready.at(blk.s))
                    else:
                        dve.wait_ge(x1_steps.sem, x1_steps.at(blk.s, i + 1))
                    dve.scalar_tensor_tensor(out=x1[:, blk.par, i, :], in0=u[:, n, i, :], scalar=rstd[:, n, i:i + 1],
                                             in1=x1[:, blk.par, i, :], op0=ALU.mult, op1=ALU.add).then_inc(x1_steps.sem, 1)

                def hidden_low(blk, k):
                    dve.wait_ge(h_hi.sem, h_hi.at(blk.s, k + 1))
                    dve.scalar_tensor_tensor(out=hid_lo[:, k, :], in0=F[k % 2][:, :], scalar=0.0,
                                             in1=hid_hi[:, k, :].bitcast(F32), op0=ALU.max, op1=ALU.subtract).then_inc(h_lo.sem, 1)

                def h2_low(blk, half):
                    dve.wait_ge(h2_hi.sem, h2_hi.at(blk.s, half + 1))
                    dve.tensor_tensor(h2T_lo[:, blk.par, half, :], F[2 + half][:, :], h2T_hi[:, blk.par, half, :].bitcast(F32),
                                      ALU.subtract).then_inc(h2_lo.sem, 1)

                def logits(blk):
                    dve.wait_ge(rn_steps.sem, rn_steps.at(blk.s))
                    for bank in range(2):
                        dve.wait_ge(lg_done.sem, lg_done.at(blk.s, bank + 1))
                        dve.tensor_tensor(lg[:, 2 * bank:2 * bank + 2, :],
                                          F[bank][:, :].rearrange("p (t n) -> p t n", t=2)[:, :, 0:E],
                                          rnorm[:, 2 * bank:2 * bank + 2].unsqueeze(2).to_broadcast([P, 2, E]),
                                          ALU.mult).then_inc(lg_ready.sem, 1)

                def router(blk):
                    p = blk.par
                    n = [0]

                    def step(ins):
                        n[0] += 1
                        ins.then_inc(gate_steps.sem, 1)
                        dve.wait_ge(gate_steps.sem, gate_steps.at(blk.s, n[0]))

                    def per_tile(a):
                        return a.unsqueeze(2).to_broadcast([P, TILES, E])

                    def pairs(a):
                        return a.rearrange("p t e j -> p t (e j)")

                    def order(a):
                        return a[:, :, :].rearrange("p e j -> p (e j)").unsqueeze(1).to_broadcast([P, TILES, E * E])

                    dve.wait_ge(lg_ready.sem, lg_ready.at(blk.s))
                    step(dve.tensor_tensor(logit[:, :, :], lg[:, :, :],
                                           t["sig"][:, :].unsqueeze(1).to_broadcast([P, TILES, E]), ALU.subtract))
                    dve.tensor_reduce(top[:, 0, :], logit[:, :, :], AX_X, ALU.max).then_inc(top_steps.sem, 1)
                    lj = logit[:, :, :].unsqueeze(2).to_broadcast([P, TILES, E, E])
                    le = logit[:, :, :].unsqueeze(3).to_broadcast([P, TILES, E, E])
                    step(dve.tensor_tensor(above[:, :, :, :], lj, le, ALU.is_gt))
                    step(dve.tensor_tensor(atleast[:, :, :, :], lj, le, ALU.is_ge))
                    step(dve.tensor_tensor(pairs(atleast), pairs(atleast), order(before), ALU.mult))
                    step(dve.tensor_tensor(pairs(above), pairs(above), order(notbefore), ALU.mult))
                    step(dve.tensor_tensor(pairs(above), pairs(above), pairs(atleast), ALU.add))
                    step(dve.tensor_reduce(rank[:, :, :], above[:, :, :, :], AX_X, ALU.add))
                    dve.wait_ge(top_steps.sem, top_steps.at(blk.s, 1))
                    dve.tensor_scalar(top[:, 1, :], top[:, 0, :], 0.0, None, ALU.is_le).then_inc(top_steps.sem, 1)
                    dve.tensor_scalar(top[:, 2, :], top[:, 0, :], 0.0, None, ALU.max).then_inc(top_steps.sem, 1)
                    dve.wait_ge(top_steps.sem, top_steps.at(blk.s, 2))
                    step(dve.scalar_tensor_tensor(out=fallback[:, :, :], in0=rank[:, :, :], scalar=2.0,
                                                  in1=per_tile(top[:, 1, :]), op0=ALU.is_lt, op1=ALU.mult))
                    dve.wait_ge(route_ready.sem, route_ready.at(blk.s - 1))
                    dve.scalar_tensor_tensor(out=mask[:, p, :, :], in0=logit[:, :, :], scalar=0.0, in1=fallback[:, :, :],
                                             op0=ALU.is_gt, op1=ALU.max).then_inc(mask_ready.sem, 1)
                    dve.wait_ge(top_steps.sem, top_steps.at(blk.s, 3))
                    dve.scalar_tensor_tensor(out=gated[:, :, :], in0=logit[:, :, :], scalar=0.0, in1=per_tile(top[:, 2, :]),
                                             op0=ALU.max, op1=ALU.subtract).then_inc(expo_in.sem, 1)
                    assert n[0] == gate_steps.per

                def combine(blk, k):
                    i, e = k // E, k % E
                    m = mask[:, blk.par, i, e:e + 1]
                    dve.wait_ge(expert_done.sem, expert_done.at(blk.s, k + 1))
                    if k == 0:
                        dve.wait_ge(mask_ready.sem, mask_ready.at(blk.s))
                    if e == 0:
                        dve.wait_ge(qk_transposed.sem, qk_transposed.at(blk.s, i - 1))
                        dve.wait_ge(v_lo_ready.sem, v_lo_ready.at(blk.s, i - 1))
                        dve.tensor_scalar(acc[:, i % 2, :], X[k % 2][:, :], m, None, ALU.mult).then_inc(combined.sem, 1)
                    else:
                        dve.wait_ge(combined.sem, combined.at(blk.s, k))
                        dve.scalar_tensor_tensor(out=acc[:, i % 2, :], in0=X[k % 2][:, :], scalar=m, in1=acc[:, i % 2, :],
                                                 op0=ALU.mult, op1=ALU.add).then_inc(combined.sem, 1)

                def qk_low(blk):
                    for k in range(2):
                        dve.wait_ge(qk_hi_ready.sem, qk_hi_ready.at(blk.s, k + 1))
                        dve.tensor_tensor(qk_lo[:, blk.par, k, :], QK[k][:, :], qk_hi[:, blk.par, k, :].bitcast(F32),
                                          ALU.subtract).then_inc(qk_lo_ready.sem, 1)

                def front(blk, k):
                    if k == 0:
                        denominators(blk)
                    if k in (4, 5):
                        f_low(blk, k - 4)
                    if k in (8, 9):
                        moments(blk, 0, 2 * (k - 8))
                        moments(blk, 0, 2 * (k - 8) + 1)
                    if k == 9:
                        gather(blk, 0)
                    if k in (9, 10):
                        hidden_low(blk, k - 9)
                    if k in (11, 12):
                        centre(blk, 0, 2 * (k - 11))
                        centre(blk, 0, 2 * (k - 11) + 1)
                    if k in (12, 13):
                        hidden_low(blk, k - 10)
                    if k in (14, 15):
                        add_norm(blk, 0, 2 * (k - 14))
                        add_norm(blk, 0, 2 * (k - 14) + 1)
                    if k in (16, 17):
                        moments(blk, 1, 2 * (k - 16))
                        moments(blk, 1, 2 * (k - 16) + 1)
                    if k == 17:
                        gather(blk, 1)
                    if k in (18, 19):
                        centre(blk, 1, 2 * (k - 18))
                        centre(blk, 1, 2 * (k - 18) + 1)
                    if k in (20, 21):
                        add_norm(blk, 1, 2 * (k - 20))
                        add_norm(blk, 1, 2 * (k - 20) + 1)
                    if k in (21, 22):
                        moments(blk, 2, 2 * (k - 21))
                        moments(blk, 2, 2 * (k - 21) + 1)
                    if k == 22:
                        gather(blk, 2)
                    if k in (26, 27):
                        h2_low(blk, k - 26)
                    if k == 30:
                        logits(blk)

                dve.wait_ge(setup, 4)
                for k in range(CH):
                    front(first, k)
                router(first)

                def body(blk):
                    nxt = blk.plus(1)
                    for k in range(CH):
                        if nxt is not None:
                            front(nxt, k)
                        combine(blk, k)
                    if nxt is not None:
                        router(nxt)
                    dve.wait_ge(qk_out[blk.par].sem, qk_out[blk.par].at(blk.turn - 1))
                    qk_low(blk)

                loop_blocks(dve, B, NB, body)

            @block.tensor
            def _(pe):
                qk_transposed.grant(pe)
                ident = t["ident"]

                def split(hi, lo, *at):
                    return hi[(slice(None), *at)], lo[(slice(None), *at)]

                def f_transpose(blk):
                    if not (isinstance(blk.s, int) and blk.s == 0):
                        pe.wait_ge(lg_ready.sem, lg_ready.at(blk.s - 1))
                    pe.wait_ge(fz_ready.sem, fz_ready.at(blk.s))
                    for half in range(2):
                        for i in range(TILES):
                            last = pe.transpose(F[half][:, i * P:(i + 1) * P], fz[:, i, half * P:(half + 1) * P], ident[:, :])
                        last.then_inc(f_transposed.sem, 1)

                def message(blk):
                    pe.wait_ge(f_lo.sem, f_lo.at(blk.s))
                    pe.wait_ge(fold_in.sem, fold_in.at(blk.b))
                    for i in range(TILES):
                        cols = slice(i * P, (i + 1) * P)
                        last = product(pe, F[2 + i // 2][:, (i % 2) * C:(i % 2 + 1) * C],
                                       [(split(fT_hi, fT_lo, hf, cols), split(g_hi, g_lo, hf)) for hf in range(2)])
                        if i % 2:
                            last.then_inc(msg_done.sem, 1)

                def hidden(blk, k):
                    if k >= 2:
                        pe.wait_ge(h_lo.sem, h_lo.at(blk.s, k - 1))
                    cols = slice(k * P, (k + 1) * P)
                    product(pe, F[k % 2][:, :], [(split(gw_hi, gw_lo, hf, cols), split(fT_hi, fT_lo, hf)) for hf in range(2)])\
                        .then_inc(hid_done.sem, 1)

                def mlp(blk, bank):
                    pe.wait_ge(h_lo.sem, h_lo.at(blk.s))
                    for i in (2 * bank, 2 * bank + 1):
                        cols = slice(i * P, (i + 1) * P)
                        last = product(pe, F[bank][:, (i % 2) * C:(i % 2 + 1) * C],
                                       [(split(hid_hi, hid_lo, k, cols), split(t["w2_hi"], t["w2_lo"], k)) for k in range(4)])
                    last.then_inc(mlp_done.sem, 1)

                def h2_transpose(blk):
                    for half in range(2):
                        for i in range(TILES):
                            pe.wait_ge(h2_ready.sem, h2_ready.at(blk.s, i + 1))
                            last = pe.transpose(F[2 + half][:, i * P:(i + 1) * P], h2[:, i, half * P:(half + 1) * P], ident[:, :])
                        last.then_inc(h2_transposed.sem, 1)

                def gate(blk):
                    pe.wait_ge(h2_lo.sem, h2_lo.at(blk.s))
                    for i in range(TILES):
                        cols = slice(i * P, (i + 1) * P)
                        last = product(pe, F[i // 2][:, (i % 2) * C:(i % 2 + 1) * C],
                                       [(split(h2T_hi, h2T_lo, blk.par, hf, cols), split(t["sn_hi"], t["sn_lo"], hf)) for hf in range(2)])
                        if i % 2:
                            last.then_inc(lg_done.sem, 1)

                def expert(blk, k):
                    i, e = k // E, k % E
                    pe.wait_ge(combined.sem, combined.at(blk.s, k - 1))
                    cols = slice(i * P, (i + 1) * P)
                    pairs = []
                    for hf in range(2):
                        w = slice((hf * E + e) * W3, (hf * E + e + 1) * W3)
                        pairs.append((split(h2T_hi, h2T_lo, blk.par, hf, cols), (t["wqkv_hi"][:, w], t["wqkv_lo"][:, w])))
                    product(pe, X[k % 2][:, :], pairs).then_inc(expert_done.sem, 1)

                def qk_transpose(blk, i):
                    if i == 0:
                        pe.wait_ge(qk_lo_ready.sem, qk_lo_ready.at(blk.s - 1))
                    pe.wait_ge(combined.sem, combined.at(blk.s, (i + 1) * E))
                    for k in range(2):
                        last = pe.transpose(QK[k][:, i * P:(i + 1) * P], acc[:, i % 2, k * D:(k + 1) * D], ident[:, :])
                    last.then_inc(qk_transposed.sem, 1)

                def front(blk, k):
                    if k == 3:
                        f_transpose(blk)
                    if k == 6:
                        message(blk)
                    if k in (7, 8):
                        hidden(blk, k - 7)
                    if k in (10, 11):
                        hidden(blk, k - 8)
                    if k in (14, 15):
                        mlp(blk, k - 14)
                    if k == 25:
                        h2_transpose(blk)
                    if k == 28:
                        gate(blk)

                for k in range(CH):
                    front(first, k)

                def body(blk):
                    nxt = blk.plus(1)
                    for k in range(CH):
                        if nxt is not None:
                            front(nxt, k)
                        expert(blk, k)
                        if k in (10, 18, 26):
                            qk_transpose(blk, k // E - 1)
                    qk_transpose(blk, TILES - 1)

                loop_blocks(pe, B, NB, body)


class Tally:

    def __init__(self, sem, counts, ahead=0):
        self.sem, self.counts, self.ahead = sem, counts, ahead

    def at(self, blk, k=None):
        within = sum(self.counts[:blk.j]) + (self.counts[blk.j] if k is None else k)
        return (blk.b + self.ahead) * sum(self.counts) + within

    def grant(self, eng):
        eng.sem_inc(self.sem, self.ahead * sum(self.counts))


def stage3(nc, t, d):
    B, NB, C, E, D = d["B"], d["NB"], d["C"], d["E"], d["D"]
    SCALE = float(D) ** -0.5
    counts = [TILES * (NB - j) for j in range(NB)]
    GROUPS = E * C // BLOCK
    OUTS = TILES * GROUPS

    def chunks(blk):
        return NB - blk.j

    def place(blk):
        return Blk(blk.b, NB - 1 - blk.j, B, NB)

    def events(blk, nxt):
        n = counts[blk.j]
        own = [("T", 0)]
        for u in range(n):
            if u + 1 < n:
                own.append(("T", u + 1))
            own.append(("V", u))
        own += [("O", r) for r in range(OUTS)]
        m = counts[nxt.j] if nxt is not None else 0
        span = len(own) - 6
        out, k = [], 0
        for at, e in enumerate(own):
            while k < m and at >= 3 + k * (span - 3) // m:
                out.append(("S", k))
                k += 1
            out.append(e)
        assert k == m
        return out

    with ExitStack() as st:
        c = Ctx(nc, st, "c_")
        kT_hi = c.sb("kT_hi", [P, NB, BLOCK], F32R)
        kT_lo = c.sb("kT_lo", [P, NB, BLOCK], F32R)
        v_hi = c.sb("v_hi", [P, NB * TILES, D], F32R)
        v_lo = c.sb("v_lo", [P, NB * TILES, D], F32R)
        qT_hi = c.sb("qT_hi", [P, 2, BLOCK], F32R)
        qT_lo = c.sb("qT_lo", [P, 2, BLOCK], F32R)
        x1 = c.sb("x1", [P, 2, TILES, C])
        route = c.sb("route", [P, 2, TILES, E])
        weight = c.sb("weight", [P, 2, TILES, E])
        probs = c.sb("probs", [P, 2, TILES, NB * BLOCK])
        causal = c.sb("causal", [P, P])
        cmax = c.sb("cmax", [P, TILES, NB])
        tmax = c.sb("tmax", [P, TILES])
        nmax = c.sb("nmax", [P, TILES])
        csum = c.sb("csum", [P, 2, TILES, NB])
        rsum = c.sb("rsum", [P, 2, TILES])
        pT_hi = c.sb("pT_hi", [P, 2, BLOCK], F32R)
        pT_lo = c.sb("pT_lo", [P, 2, BLOCK], F32R)
        oT_hi = c.sb("oT_hi", [P, BLOCK], F32R)
        oT_lo = c.sb("oT_lo", [P, BLOCK], F32R)

        S = [c.ps(f"S{i}", [P, BLOCK]) for i in range(4)]
        T = [c.ps(f"T{i}", [P, BLOCK]) for i in range(2)]
        Y = [c.ps(f"Y{i}", [P, BLOCK]) for i in range(2)]

        setup = c.sem("setup")
        k_in = [c.flag(f"k_in{i}", 32) for i in range(NB)]
        v_in = [c.flag(f"v_in{i}", 32) for i in range(NB)]
        q_in = [c.flag(f"q_in{i}", 32) for i in range(2)]
        x1_in = [c.flag(f"x1_in{i}", 32) for i in range(2)]

        def tally(name, ahead=0):
            return Tally(c.sem(name), counts, ahead)

        s_done = tally("s_done")
        causal_done = c.flag("causal_done", TILES)
        cmax_ready = tally("cmax_ready")
        tmax_ready = c.flag("tmax_ready", TILES)
        nmax_ready = c.flag("nmax_ready", TILES)
        exp_done = tally("exp_done", 1)
        p_transposed = tally("p_transposed", 1)
        p_hi = tally("p_hi")
        p_lo = tally("p_lo", 1)
        pv_done = tally("pv_done", 1)
        rsum_ready = c.flag("rsum_ready", 1)
        rinv_ready = c.flag("rinv_ready", 1)
        weight_ready = c.flag("weight_ready", 1)
        o_hi = c.flag("o_hi", 1)
        o_lo = c.flag("o_lo", 1)
        out_done = c.flag("out_done", OUTS, ahead=1)
        summed = c.flag("summed", 2 * OUTS, ahead=1)
        stored = [c.flag(f"stored{i}", 16, ahead=1) for i in range(2)]

        first = Blk(0, 0, B, NB)

        paces = {e.engine: c.sem(f"pace_{k}") for k, e in enumerate((nc.sync, nc.gpsimd, nc.vector))}

        with nc.Block() as block:

            @block.sync
            def _(sp):
                for g in stored:
                    g.grant(sp)

                def load_k(b, ch):
                    cols = bass.ds((b * NB + ch) * BLOCK, BLOCK)
                    sp.dma_start(kT_hi[:, ch, :].bitcast(F32), t["kT_hi"][:, cols]).then_inc(k_in[ch].sem, 16)
                    sp.dma_start(kT_lo[:, ch, :].bitcast(F32), t["kT_lo"][:, cols]).then_inc(k_in[ch].sem, 16)

                def load_v(b, ch):
                    src, at = Blk(b, ch, B, NB), slice(ch * TILES, (ch + 1) * TILES)
                    sp.dma_start(v_hi[:, at, :].bitcast(F32), rows(t["v_hi"], src, D)).then_inc(v_in[ch].sem, 16)
                    sp.dma_start(v_lo[:, at, :].bitcast(F32), rows(t["v_lo"], src, D)).then_inc(v_in[ch].sem, 16)

                def load_q(blk):
                    cols = bass.ds(place(blk).s * BLOCK, BLOCK)
                    sp.dma_start(qT_hi[:, blk.par, :].bitcast(F32), t["qT_hi"][:, cols]).then_inc(q_in[blk.par].sem, 16)
                    sp.dma_start(qT_lo[:, blk.par, :].bitcast(F32), t["qT_lo"][:, cols]).then_inc(q_in[blk.par].sem, 16)

                def load_x1(blk):
                    sp.wait_ge(stored[blk.par].sem, stored[blk.par].at(blk.turn - 1))
                    settle(sp, paces)
                    sp.dma_start(x1[:, blk.par, :, :], rows(t["x1"], place(blk), C)).then_inc(x1_in[blk.par].sem, 16)
                    sp.dma_start(route[:, blk.par, :, :], rows(t["route"], place(blk), E)).then_inc(x1_in[blk.par].sem, 16)

                load_q(first)
                for ch in reversed(range(NB)):
                    load_k(0, ch)
                load_q(first.plus(1))
                for ch in range(NB):
                    load_v(0, ch)
                load_x1(first)

                def body(blk):
                    nxt, after = blk.plus(1), blk.plus(2)
                    more = not (isinstance(blk.b, int) and blk.b == B - 1)
                    ch = NB - 1 - blk.j
                    if more:
                        sp.wait_ge(s_done.sem, s_done.at(blk))
                        settle(sp, paces)
                        load_k(blk.b + 1, ch)
                    if after is not None:
                        sp.wait_ge(s_done.sem, s_done.at(blk))
                        settle(sp, paces)
                        load_q(after)
                    if nxt is not None:
                        load_x1(nxt)
                    if more:
                        sp.wait_ge(pv_done.sem, pv_done.at(blk))
                        settle(sp, paces)
                        load_v(blk.b + 1, ch)
                    sp.wait_ge(summed.sem, summed.at(blk.s))
                    settle(sp, paces)
                    sp.dma_start(rows(t["out2d"], place(blk), C), x1[:, blk.par, :, :]).then_inc(stored[blk.par].sem, 16)

                loop_blocks(sp, B, NB, body)
                for g in stored:
                    sp.wait_ge(g.sem, g.at(B * NB // 2 - 1))
                    settle(sp, paces)

            @block.gpsimd
            def _(pool):
                pool.memset(causal[:, :], 0.0).then_inc(setup, 1)
                pool.wait_ge(setup, 1)
                pool.affine_select(out=causal[:, :], in_=causal[:, :], compare_op=ALU.is_ge, fill=MASKED, base=0,
                                   pattern=[[-1, P]], channel_multiplier=1).then_inc(setup, 1)

                def body(blk):
                    p = blk.par
                    pool.wait_ge(rsum_ready.sem, rsum_ready.at(blk.s))
                    pool.tensor_tensor(rsum[:, 1, :], rsum[:, 0, :], t["minus_one"][:, 0:TILES], ALU.pow).then_inc(rinv_ready.sem, 1)
                    pool.wait_ge(rinv_ready.sem, rinv_ready.at(blk.s))
                    pool.wait_ge(x1_in[p].sem, x1_in[p].at(blk.turn))
                    pool.wait_ge(summed.sem, summed.at(blk.s - 1))
                    pool.tensor_tensor(weight[:, p, :, :], route[:, p, :, :],
                                       rsum[:, 1, :].unsqueeze(2).to_broadcast([P, TILES, E]), ALU.mult).then_inc(weight_ready.sem, 1)

                loop_blocks(pool, B, NB, body)

            @block.scalar
            def _(act):
                exp_done.grant(act)

                def exponentials(blk, k):
                    n = chunks(blk)
                    i, ch = k // n, n - 1 - k % n
                    width = (i + 1) * P if ch == n - 1 else BLOCK
                    if k % n == 0:
                        act.wait_ge(nmax_ready.sem, nmax_ready.at(blk.s, i + 1))
                    if k == 0 and not (isinstance(blk.s, int) and blk.s < 2):
                        act.wait_ge(p_transposed.sem, p_transposed.at(blk.plus(-2)))
                    act.activation(probs[:, blk.par, i, ch * BLOCK:ch * BLOCK + width], S[k % 4][:, 0:width], ACT.Exp,
                                   bias=nmax[:, i:i + 1], scale=SCALE,
                                   accum_out=csum[:, blk.par, i, ch:ch + 1]).then_inc(exp_done.sem, 1)

                def scores(blk, k):
                    if k >= chunks(blk):
                        exponentials(blk, k - chunks(blk))
                    if k == counts[blk.j] - 1:
                        for last in range(counts[blk.j] - chunks(blk), counts[blk.j]):
                            exponentials(blk, last)

                for k in range(counts[0]):
                    scores(first, k)

                def body(blk):
                    nxt = blk.plus(1)
                    for what, k in events(blk, nxt):
                        if what == "S":
                            scores(nxt, k)
                        if what == "T":
                            lo = max(0, k - (counts[blk.j] - TILES)) * P
                            act.wait_ge(p_transposed.sem, p_transposed.at(blk, k + 1))
                            act.wait_ge(pv_done.sem, pv_done.at(blk, k - 1))
                            act.activation(pT_hi[:, k % 2, lo:], T[k % 2][:, lo:], ACT.Copy).then_inc(p_hi.sem, 1)
                        if what == "V" and k == counts[blk.j] - 1:
                            act.wait_ge(pv_done.sem, pv_done.at(blk))
                            act.activation(oT_hi[:, :], Y[0][:, :], ACT.Copy).then_inc(o_hi.sem, 1)

                loop_blocks(act, B, NB, body)

            @block.vector
            def _(dve):
                p_lo.grant(dve)
                summed.grant(dve)

                def scores(blk, k):
                    n = chunks(blk)
                    i, ch = k // n, n - 1 - k % n
                    width = (i + 1) * P if ch == n - 1 else BLOCK
                    dve.wait_ge(s_done.sem, s_done.at(blk, k + 1))
                    if ch == n - 1:
                        dve.tensor_tensor(S[k % 4][:, i * P:(i + 1) * P], S[k % 4][:, i * P:(i + 1) * P], causal[:, :],
                                          ALU.add).then_inc(causal_done.sem, 1)
                        dve.wait_ge(causal_done.sem, causal_done.at(blk.s, i + 1))
                    dve.tensor_reduce(cmax[:, i, ch:ch + 1], S[k % 4][:, 0:width], AX_X, ALU.max).then_inc(cmax_ready.sem, 1)
                    if ch == 0:
                        dve.wait_ge(cmax_ready.sem, cmax_ready.at(blk, k + 1))
                        dve.tensor_reduce(tmax[:, i:i + 1], cmax[:, i, 0:n], AX_X, ALU.max).then_inc(tmax_ready.sem, 1)
                        dve.wait_ge(tmax_ready.sem, tmax_ready.at(blk.s, i + 1))
                        if not (isinstance(blk.s, int) and blk.s == 0):
                            dve.wait_ge(exp_done.sem, exp_done.at(blk, (i - 3) * n if i < 3 else 0))
                        dve.tensor_scalar(nmax[:, i:i + 1], tmax[:, i:i + 1], -SCALE, None, ALU.mult).then_inc(nmax_ready.sem, 1)

                def row_sums(blk):
                    dve.wait_ge(exp_done.sem, exp_done.at(blk))
                    dve.tensor_reduce(rsum[:, 0, :], csum[:, blk.par, :, 0:chunks(blk)], AX_X, ALU.add).then_inc(rsum_ready.sem, 1)

                def project(blk, r):
                    i, g = r // GROUPS, r % GROUPS
                    dve.wait_ge(out_done.sem, out_done.at(blk.s, r + 1))
                    if r == 0:
                        dve.wait_ge(weight_ready.sem, weight_ready.at(blk.s))
                    acc = x1[:, blk.par, i, :]
                    for e in range(2):
                        if g or e:
                            dve.wait_ge(summed.sem, summed.at(blk.s, 2 * r + e))
                        dve.scalar_tensor_tensor(out=acc, in0=Y[(r + 1) % 2][:, e * C:(e + 1) * C],
                                                 scalar=weight[:, blk.par, i, 2 * g + e:2 * g + e + 1], in1=acc,
                                                 op0=ALU.mult, op1=ALU.add).then_inc(summed.sem, 1)

                dve.wait_ge(setup, 2)
                for k in range(counts[0]):
                    scores(first, k)

                def body(blk):
                    nxt = blk.plus(1)
                    row_sums(blk)
                    for what, k in events(blk, nxt):
                        if what == "S":
                            scores(nxt, k)
                        if what == "T":
                            lo = max(0, k - (counts[blk.j] - TILES)) * P
                            dve.wait_ge(p_hi.sem, p_hi.at(blk, k + 1))
                            dve.tensor_tensor(pT_lo[:, k % 2, lo:], T[k % 2][:, lo:], pT_hi[:, k % 2, lo:].bitcast(F32),
                                              ALU.subtract).then_inc(p_lo.sem, 1)
                        if what == "V" and k == counts[blk.j] - 1:
                            dve.wait_ge(o_hi.sem, o_hi.at(blk.s))
                            dve.tensor_tensor(oT_lo[:, :], Y[0][:, :], oT_hi[:, :].bitcast(F32), ALU.subtract).then_inc(o_lo.sem, 1)
                        if what == "O":
                            project(blk, k)

                loop_blocks(dve, B, NB, body)

            @block.tensor
            def _(pe):
                p_transposed.grant(pe)
                pv_done.grant(pe)
                out_done.grant(pe)
                ident = t["ident"]

                def scores(blk, k):
                    n = chunks(blk)
                    i, ch = k // n, n - 1 - k % n
                    width = max(2 * P, (i + 1) * P) if ch == n - 1 else BLOCK
                    if k == 0:
                        pe.wait_ge(q_in[blk.par].sem, q_in[blk.par].at(blk.turn))
                    if i == 0:
                        pe.wait_ge(k_in[ch].sem, k_in[ch].at(blk.b))
                    pe.wait_ge(exp_done.sem, exp_done.at(blk, k - 3))
                    cols = slice(i * P, (i + 1) * P)
                    product(pe, S[k % 4][:, 0:width],
                            [((qT_hi[:, blk.par, cols], qT_lo[:, blk.par, cols]),
                              (kT_hi[:, ch, 0:width], kT_lo[:, ch, 0:width]))]).then_inc(s_done.sem, 1)

                def transpose(blk, u):
                    first_tile = max(0, u - (counts[blk.j] - TILES))
                    if u == 0:
                        pe.wait_ge(exp_done.sem, exp_done.at(blk))
                    pe.wait_ge(p_lo.sem, p_lo.at(blk, u - 1))
                    for i in range(first_tile, TILES):
                        last = pe.transpose(T[u % 2][:, i * P:(i + 1) * P], probs[:, blk.par, i, u * P:(u + 1) * P], ident[:, :])
                    last.then_inc(p_transposed.sem, 1)

                def values(blk, u):
                    lo = max(0, u - (counts[blk.j] - TILES)) * P
                    if u % TILES == 0:
                        pe.wait_ge(v_in[u // TILES].sem, v_in[u // TILES].at(blk.b))
                    if u == 0:
                        pe.wait_ge(summed.sem, summed.at(blk.s - 1))
                    pe.wait_ge(p_lo.sem, p_lo.at(blk, u + 1))
                    product(pe, Y[0][:, lo:], [((v_hi[:, u, :], v_lo[:, u, :]), (pT_hi[:, u % 2, lo:], pT_lo[:, u % 2, lo:]))],
                            begin=(u == 0), end=(u == counts[blk.j] - 1)).then_inc(pv_done.sem, 1)

                def project(blk, r):
                    i, g = r // GROUPS, r % GROUPS
                    if r == 0:
                        pe.wait_ge(o_lo.sem, o_lo.at(blk.s))
                    pe.wait_ge(summed.sem, summed.at(blk.s, 2 * (r - 1)))
                    w = slice(g * BLOCK, (g + 1) * BLOCK)
                    cols = slice(i * P, (i + 1) * P)
                    product(pe, Y[(r + 1) % 2][:, :], [((oT_hi[:, cols], oT_lo[:, cols]), (t["wo_hi"][:, w], t["wo_lo"][:, w]))])\
                        .then_inc(out_done.sem, 1)

                for k in range(counts[0]):
                    scores(first, k)

                def body(blk):
                    nxt = blk.plus(1)
                    for what, k in events(blk, nxt):
                        {"S": lambda: scores(nxt, k), "T": lambda: transpose(blk, k), "V": lambda: values(blk, k),
                         "O": lambda: project(blk, k)}[what]()

                loop_blocks(pe, B, NB, body)


def dims():
    return dict(B=4, NB=4, C=256, E=8, D=128, WCOLS=2 * 8 * 384 + 8 * 256)


def build(nc, A, out, upto=3):
    d = dims()
    N, C = d["B"] * d["NB"] * BLOCK, d["C"]

    def scratch(name, shape):
        return nc.dram_tensor(name, shape, F32, kind="Internal").ap()

    with ExitStack() as st:
        c = Ctx(nc, st, "")
        t = dict(x2d=A["x"].rearrange("b l c -> (b l) c"), out2d=out.rearrange("b l c -> (b l) c"), **A)
        for name, cols in (("feat", C), ("base", C), ("x1", C)):
            t[name] = scratch("s_" + name, [N, C])
        for name, cols in (("ks", C), ("g_hi", 2 * C), ("g_lo", 2 * C), ("gw_hi", 4 * C), ("gw_lo", 4 * C)):
            t[name] = scratch("s_" + name, [d["B"] * P, cols])
        for name in ("qT_hi", "qT_lo", "kT_hi", "kT_lo"):
            t[name] = scratch("s_" + name, [P, N])
        for name in ("v_hi", "v_lo"):
            t[name] = scratch("s_" + name, [N, P])
        t["route"] = scratch("s_route", [N, 8])
        t["ident"] = c.sb("ident", [P, P])
        t["minus_half"] = c.sb("minus_half", [P, 32])
        t["half"] = c.sb("half", [P, 32])
        t["minus_one"] = c.sb("minus_one", [P, 32])
        t["sig"] = c.sb("sig", [P, 8])
        t["wo_hi"] = c.sb("wo_hi", [P, d["E"] * C], F32R)
        t["wo_lo"] = c.sb("wo_lo", [P, d["E"] * C], F32R)
        with ExitStack() as until_attention:
            c = Ctx(nc, until_attention, "")
            t["sn_hi"] = c.sb("sn_hi", [P, 2, C], F32R)
            t["sn_lo"] = c.sb("sn_lo", [P, 2, C], F32R)
            t["w2_hi"] = c.sb("w2_hi", [P, 4, C], F32R)
            t["w2_lo"] = c.sb("w2_lo", [P, 4, C], F32R)
            t["wqkv_hi"] = c.sb("wqkv_hi", [P, 6 * d["E"] * d["D"]], F32R)
            t["wqkv_lo"] = c.sb("wqkv_lo", [P, 6 * d["E"] * d["D"]], F32R)
            stage1(nc, t, d)
            if upto >= 2:
                stage2(nc, t, d)
        if upto >= 3:
            stage3(nc, t, d)


_INS = {"x": "L0_attn_x", "Wq": "L0_attn_Wq", "Wm": "L0_attn_Wm", "W1": "L0_attn_W1", "W2": "L0_attn_W2",
        "g1": "L0_attn_g1", "b1": "L0_attn_b1", "g2": "L0_attn_g2", "b2": "L0_attn_b2",
        "sim": "L0_ffn_sim_matrix", "gates": "L0_ffn_gates", "Wqe": "L0_ffn_q_proj", "Wke": "L0_ffn_k_proj",
        "Wve": "L0_ffn_v_proj", "Woe": "L0_ffn_o_proj"}


def kernel(**inputs):
    import numpy as np
    import concourse.bacc as bacc
    from concourse.bass_utils import run_bass_kernel_spmd

    nc = bacc.Bacc("TRN2", target_bir_lowering=False, num_devices=1)
    arrays, handles = {}, {}
    for short, name in _INS.items():
        arrays["in_" + name] = np.ascontiguousarray(inputs[name])
        handles[short] = nc.dram_tensor("in_" + name, arrays["in_" + name].shape, F32, kind="ExternalInput").ap()
    out = nc.dram_tensor("out", arrays["in_L0_attn_x"].shape, F32, kind="ExternalOutput").ap()
    build(nc, handles, out)
    r = run_bass_kernel_spmd(nc, [arrays], core_ids=[0])
    return r.results[0]["out"]
```

```python
from contextlib import ExitStack

import concourse.bass as bass
from concourse import mybir

ALU = mybir.AluOpType
ACT = mybir.ActivationFunctionType
F32 = mybir.dt.float32
F32R = mybir.dt.float32r
AX_X = mybir.AxisListType.X

P = 128
TILES = 4
BLOCK = P * TILES
LN_EPS = 1e-5
ATTN_EPS = 1e-6
NORM_EPS = 1e-12
MASKED = -3.0e38


class Affine:

    def __init__(self, register, mul=1, off=0):
        self.register, self.mul, self.off = register, mul, off

    def __add__(self, k):
        return Affine(self.register, self.mul, self.off + k)

    def __sub__(self, k):
        return self + -k

    def __mul__(self, k):
        return Affine(self.register, self.mul * k, self.off * k)


def value(n):
    return n.register * n.mul + n.off if isinstance(n, Affine) else n


class Blk:

    def __init__(self, b, j, batches, per_batch):
        self.b, self.j, self.batches, self.per_batch = b, j, batches, per_batch

    @property
    def s(self):
        return self.b * self.per_batch + self.j

    @property
    def par(self):
        return self.j % 2

    @property
    def turn(self):
        return self.b * (self.per_batch // 2) + self.j // 2

    def plus(self, k):
        j = self.j + k
        b = self.b + j // self.per_batch if not 0 <= j < self.per_batch else self.b
        if isinstance(b, int) and b >= self.batches:
            return None
        return Blk(b, j % self.per_batch, self.batches, self.per_batch)


class Flag:

    def __init__(self, sem, per, ahead=0):
        self.sem, self.per, self.ahead = sem, per, ahead

    def at(self, n, k=None):
        return value((n + self.ahead) * self.per + (self.per if k is None else k))

    def grant(self, eng):
        eng.sem_inc(self.sem, self.ahead * self.per)


def settle(eng, paces):
    eng.sem_inc(paces[eng.engine])


def loop_blocks(eng, batches, per_batch, body):
    with eng.Fori(0, batches - 1, 1) as b:
        for j in range(per_batch):
            own = Affine(eng.snap(b + (j + 1)), 1, -(j + 1))
            body(Blk(own, j, batches, per_batch))
    for j in range(per_batch):
        body(Blk(batches - 1, j, batches, per_batch))


class Ctx:

    def __init__(self, nc, stack, prefix):
        self.nc, self.stack, self.prefix = nc, stack, prefix

    def sb(self, name, shape, dt=F32):
        return self.stack.enter_context(self.nc.sbuf_tensor(self.prefix + name, shape, dt))

    def ps(self, name, shape, dt=F32):
        return self.stack.enter_context(self.nc.psum_tensor(self.prefix + name, shape, dt))

    def sem(self, name):
        return self.stack.enter_context(self.nc.semaphore(self.prefix + name))

    def flag(self, name, per, ahead=0):
        return Flag(self.sem(name), per, ahead)


def rows(dram, blk, width):
    return dram[bass.ds(value(blk.s * BLOCK), BLOCK), :].rearrange("(t p) c -> p t c", p=P)


def product(eng, out, pairs, begin=True, end=True):
    n = 3 * len(pairs)
    i = 0
    for (ah, al), (bh, bl) in pairs:
        for a, b in ((ah, bl), (ah, bh), (al, bh)):
            last = eng.matmul(out, a, b, start=(begin and i == 0), stop=(end and i == n - 1))
            i += 1
    return last


def stage1(nc, t, d):
    B, NB, C = d["B"], d["NB"], d["C"]
    H = 8
    with ExitStack() as st:
        c = Ctx(nc, st, "a_")
        x = c.sb("x", [P, 2, TILES, C])
        h = c.sb("h", [P, 2, TILES, C])
        base = c.sb("base", [P, 2, TILES, C])
        stats = c.sb("stats", [P, 2, TILES, 6])
        mv = c.sb("mv", [P, 2, TILES, 2])
        ve = c.sb("ve", [P, 2, TILES])
        rstd = c.sb("rstd", [P, 2, TILES])
        rstd1 = c.sb("rstd1", [P, 2, TILES])
        negmu = c.sb("negmu", [P, 2, TILES])
        negmur = c.sb("negmur", [P, 2, TILES])
        hT_hi = c.sb("hT_hi", [P, 2, BLOCK], F32R)
        hT_lo = c.sb("hT_lo", [P, 2, BLOCK], F32R)
        negpart = c.sb("negpart", [P, 2, 2, C])
        expneg = c.sb("expneg", [P, 2, 2, C])
        q = c.sb("q", [P, 2, TILES, C])
        feat = c.sb("feat", [P, 2, TILES, C])
        fsum = c.sb("fsum", [P, TILES, C])
        wq_raw = c.sb("wq_raw", [P, 2, C])
        wq_hi = c.sb("wq_hi", [P, 2, C], F32R)
        wq_lo = c.sb("wq_lo", [P, 2, C], F32R)
        wm = c.sb("wm", [P, 2, C])
        w1 = c.sb("w1", [P, 2, 2 * C])
        w2_raw = c.sb("w2_raw", [P, 4, C])
        w_raw = c.sb("w_raw", [P, d["WCOLS"]])
        ones = c.sb("ones", [P, P])
        headmask = c.sb("headmask", [P, P])
        kvT = c.sb("kvT", [P, 2, P])
        gT = c.sb("gT", [P, 2, C])
        ks_st = c.sb("ks_st", [P, C])
        g_st_hi = c.sb("g_st_hi", [P, 2 * C], F32R)
        g_st_lo = c.sb("g_st_lo", [P, 2 * C], F32R)
        gw_st_hi = c.sb("gw_st_hi", [P, 2, 2 * C], F32R)
        gw_st_lo = c.sb("gw_st_lo", [P, 2, 2 * C], F32R)
        sim = c.sb("sim", [P, 2, 8])
        simsq = c.sb("simsq", [P, 2, 8])
        simn = c.sb("simn", [P, 3, 8])
        sn = c.sb("sn", [P, 2, 8])
        gates = c.sb("gates", [P, 2, 8])

        trp = [c.ps(f"trp{i}", [P, BLOCK]) for i in range(2)]
        qp = [c.ps(f"qp{i}", [P, 2, C]) for i in range(2)]
        kvp = [c.ps(f"kvp{i}", [P, 2, C]) for i in range(2)]
        misc = [c.ps(f"misc{i}", [P, 2 * C]) for i in range(2)]

        w_in = c.sem("w_in")
        small_in = c.sem("small_in")
        raw_in = c.sem("raw_in")
        x_in = [c.flag(f"x_in{i}", 16) for i in range(2)]
        consts = c.sem("consts")
        wq_split = c.sem("wq_split")
        w2_split = c.sem("w2_split")
        w_split = c.flag("w_split", 4)
        gate_pool = c.sem("gate_pool")
        gate_act = c.sem("gate_act")
        gate_pe = c.sem("gate_pe")
        gate_dve = c.sem("gate_dve")
        st_ready = c.flag("st_ready", TILES)
        mv_ready = c.flag("mv_ready", TILES)
        pool_small = c.flag("pool_small", 5)
        h_ready = c.flag("h_ready", TILES)
        base_ready = c.flag("base_ready", TILES)
        base_out = [c.flag(f"base_out{i}", 16) for i in range(2)]
        transposed = c.flag("transposed", 2)
        hi_ready = c.flag("hi_ready", 2)
        lo_ready = c.flag("lo_ready", 2)
        q_done = c.flag("q_done", 2)
        neg_ready = c.flag("neg_ready", 2)
        q_copied = c.flag("q_copied", 2)
        exp_ready = c.flag("exp_ready", 2)
        feat_ready = c.flag("feat_ready", 2)
        feat_out = [c.flag(f"feat_out{i}", 16, ahead=1) for i in range(2)]
        summed = c.flag("summed", 1, ahead=1)
        kv_read = c.flag("kv_read", 1)
        kv_masked = c.flag("kv_masked", 2)
        ks_done = c.flag("ks_done", 1, ahead=1)
        ks_copied = c.flag("ks_copied", 1)
        g_done = c.flag("g_done", 1)
        gT_done = c.flag("gT_done", 1)
        gT_copied = c.flag("gT_copied", 1)
        gw_done = c.flag("gw_done", 2)
        fold_hi = c.flag("fold_hi", 3)
        fold_lo = c.flag("fold_lo", 3, ahead=1)
        fold_out = c.flag("fold_out", 16 * 5, ahead=1)

        x2d, feat2d, base2d = t["x2d"], t["feat"], t["base"]

        paces = {e.engine: c.sem(f"pace_{k}") for k, e in enumerate((nc.sync, nc.gpsimd, nc.vector, nc.scalar))}

        with nc.Block() as block:

            @block.sync
            def _(sp):
                for g in feat_out:
                    g.grant(sp)
                fold_out.grant(sp)
                first = Blk(0, 0, B, NB)
                sp.dma_start(wq_raw[:, :, :], t["Wq"].rearrange("(h p) n -> p h n", p=P)).then_inc(w_in, 16)
                for k in (0, 1):
                    blk = first.plus(k)
                    sp.dma_start(x[:, blk.par, :, :], rows(x2d, blk, C)).then_inc(x_in[blk.par].sem, 16)
                sp.dma_start(sim[:, :, :], t["sim"].rearrange("(h p) n -> p h n", p=P)).then_inc(small_in, 16)
                sp.dma_start(gates[:, 0, :], t["gates"].partition_broadcast(P)).then_inc(small_in, 16)
                sp.dma_start(wm[:, :, :], t["Wm"].rearrange("(h p) n -> p h n", p=P)).then_inc(small_in, 16)
                sp.dma_start(w1[:, :, :], t["W1"].rearrange("(h p) n -> p h n", p=P)).then_inc(small_in, 16)
                sp.dma_start(w2_raw[:, :, :], t["W2"].rearrange("(h p) n -> p h n", p=P)).then_inc(small_in, 16)

                def load_x(blk):
                    before = blk.plus(-2)
                    sp.wait_ge(h_ready.sem, h_ready.at(before.s))
                    settle(sp, paces)
                    sp.wait_ge(base_ready.sem, base_ready.at(before.s))
                    settle(sp, paces)
                    sp.dma_start(x[:, blk.par, :, :], rows(x2d, blk, C)).then_inc(x_in[blk.par].sem, 16)

                def store_base(blk):
                    sp.wait_ge(base_ready.sem, base_ready.at(blk.s))
                    settle(sp, paces)
                    sp.dma_start(rows(base2d, blk, C), base[:, blk.par, :, :]).then_inc(base_out[blk.par].sem, 16)

                def store_feat(blk):
                    sp.wait_ge(feat_ready.sem, feat_ready.at(blk.s))
                    settle(sp, paces)
                    sp.dma_start(rows(feat2d, blk, C), feat[:, blk.par, :, :]).then_inc(feat_out[blk.par].sem, 16)

                for k in (0, 1):
                    load_x(first.plus(k + 2))
                    store_base(first.plus(k))
                E, D = d["E"], d["D"]
                for k, name in enumerate(("Wqe", "Wke", "Wve")):
                    for half in range(2):
                        dst = w_raw[:, half * E * 3 * D:(half + 1) * E * 3 * D].rearrange("p (e n) -> p e n", e=E)
                        sp.dma_start(dst[:, :, k * D:(k + 1) * D],
                                     t[name][:, half * P:(half + 1) * P, :].rearrange("e p n -> p e n")).then_inc(raw_in, 16)
                sp.dma_start(w_raw[:, 6 * E * D:].rearrange("p (e n) -> p e n", e=E),
                             t["Woe"].rearrange("e p n -> p e n")).then_inc(raw_in, 16)

                store_base(first.plus(2))
                store_feat(first)
                store_feat(first.plus(1))

                def body(blk):
                    if blk.plus(4) is not None:
                        load_x(blk.plus(4))
                    if blk.plus(3) is not None:
                        store_base(blk.plus(3))
                    if blk.plus(2) is not None:
                        store_feat(blk.plus(2))

                loop_blocks(sp, B, NB, body)
                turns = B * NB // 2
                for par in range(2):
                    sp.wait_ge(base_out[par].sem, base_out[par].at(turns - 1))
                    sp.wait_ge(feat_out[par].sem, feat_out[par].at(turns - 1))
                sp.wait_ge(fold_out.sem, fold_out.at(B - 1))
                settle(sp, paces)

            @block.gpsimd
            def _(pool):
                summed.grant(pool)
                pool.memset(t["ident"][:, :], 0.0).then_inc(consts, 1)
                pool.memset(ones[:, :], 1.0).then_inc(consts, 1)
                pool.memset(t["minus_half"][:, :], -0.5).then_inc(consts, 1)
                pool.memset(t["half"][:, :], 0.5).then_inc(consts, 1)
                pool.memset(t["minus_one"][:, :], -1.0).then_inc(consts, 1)
                pool.memset(headmask[:, :], 0.0).then_inc(consts, 1)
                pool.wait_ge(consts, 6)
                pool.affine_select(out=t["ident"][:, :], in_=t["ident"][:, :], compare_op=ALU.not_equal, fill=1.0,
                                   base=0, pattern=[[-1, P]], channel_multiplier=1).then_inc(consts, 1)
                for k in range(4):
                    pool.wait_ge(consts, 7 + k)
                    pool.memset(headmask[32 * k:32 * k + 32, 32 * k:32 * k + 32], 1.0).then_inc(consts, 1)

                def row_scales(blk):
                    p = blk.par
                    if not (isinstance(blk.s, int) and blk.s < 2):
                        pool.wait_ge(h_ready.sem, h_ready.at(blk.s - 2))
                        pool.wait_ge(base_ready.sem, base_ready.at(blk.s - 2))
                    pool.wait_ge(mv_ready.sem, mv_ready.at(blk.s))
                    settle(pool, paces)
                    pool.tensor_scalar(ve[:, p, :], mv[:, p, :, 1], LN_EPS, None, ALU.add).then_inc(pool_small.sem, 1)
                    pool.tensor_scalar(negmu[:, p, :], mv[:, p, :, 0], -1.0, None, ALU.mult).then_inc(pool_small.sem, 1)
                    pool.wait_ge(pool_small.sem, pool_small.at(blk.s, 1))
                    pool.tensor_tensor(rstd[:, p, :], ve[:, p, :], t["minus_half"][:, 0:TILES], ALU.pow).then_inc(pool_small.sem, 1)
                    pool.wait_ge(pool_small.sem, pool_small.at(blk.s, 3))
                    settle(pool, paces)
                    pool.tensor_scalar(rstd1[:, p, :], rstd[:, p, :], 1.0, None, ALU.add).then_inc(pool_small.sem, 1)
                    pool.tensor_tensor(negmur[:, p, :], negmu[:, p, :], rstd[:, p, :], ALU.mult).then_inc(pool_small.sem, 1)

                first = Blk(0, 0, B, NB)
                pool.wait_ge(consts, 11)
                row_scales(first)
                row_scales(first.plus(1))

                pool.wait_ge(gate_dve, 2)
                pool.tensor_tensor(simn[:, 1, :], simn[:, 0, :], t["half"][:, 0:8], ALU.pow).then_inc(gate_pool, 1)
                pool.wait_ge(gate_pool, 1)
                pool.tensor_scalar(simn[:, 0, :], simn[:, 1, :], NORM_EPS, None, ALU.max).then_inc(gate_pool, 1)
                pool.wait_ge(gate_pool, 2)
                pool.tensor_tensor(simn[:, 2, :], simn[:, 0, :], t["minus_one"][:, 0:8], ALU.pow).then_inc(gate_pool, 1)
                pool.wait_ge(gate_act, 1)
                pool.tensor_scalar(gates[:, 0, :], gates[:, 1, :], 1.0, None, ALU.add).then_inc(gate_pool, 1)
                pool.wait_ge(gate_pool, 4)
                pool.tensor_tensor(t["sig"][:, :], gates[:, 0, :], t["minus_one"][:, 0:8], ALU.pow).then_inc(gate_pool, 1)
                row_scales(first.plus(2))
                wqkv_raw, wo_raw = w_raw[:, 0:6 * d["E"] * d["D"]], w_raw[:, 6 * d["E"] * d["D"]:]

                def body(blk):
                    pool.wait_ge(feat_ready.sem, feat_ready.at(blk.s))
                    if blk.j == 0:
                        pool.wait_ge(ks_done.sem, ks_done.at(blk.b - 1))
                        settle(pool, paces)
                        pool.tensor_copy(fsum[:, :, :], feat[:, blk.par, :, :]).then_inc(summed.sem, 1)
                    else:
                        pool.wait_ge(summed.sem, summed.at(blk.s - 1))
                        pool.tensor_tensor(fsum[:, :, :], fsum[:, :, :], feat[:, blk.par, :, :], ALU.add).then_inc(summed.sem, 1)
                    if blk.plus(3) is not None:
                        row_scales(blk.plus(3))
                    pool.wait_ge(raw_in, 16 * 7)
                    settle(pool, paces)
                    parts = []
                    for raw, hi, lo in ((wqkv_raw, t["wqkv_hi"], t["wqkv_lo"]), (wo_raw, t["wo_hi"], t["wo_lo"])):
                        n = raw.shape[1] // (B * NB)
                        cols = bass.ds(value(blk.s * n), n)
                        pool.tensor_copy(hi[:, cols], raw[:, cols]).then_inc(w_split.sem, 1)
                        parts.append((raw[:, cols], hi[:, cols], lo[:, cols]))
                    for k, (raw, hi, lo) in enumerate(parts):
                        pool.wait_ge(w_split.sem, w_split.at(blk.s, k + 1))
                        pool.tensor_tensor(lo, raw, hi.bitcast(F32), ALU.subtract).then_inc(w_split.sem, 1)

                loop_blocks(pool, B, NB, body)

            @block.vector
            def _(dve):
                fold_lo.grant(dve)
                dve.wait_ge(w_in, 16)
                dve.tensor_copy(wq_hi[:, :, :], wq_raw[:, :, :]).then_inc(wq_split, 1)
                dve.wait_ge(wq_split, 1)
                dve.tensor_tensor(wq_lo[:, :, :], wq_raw[:, :, :], wq_hi[:, :, :].bitcast(F32), ALU.subtract).then_inc(wq_split, 1)

                def moments(blk):
                    p = blk.par
                    dve.wait_ge(x_in[p].sem, x_in[p].at(blk.turn))
                    for i in range(TILES):
                        dve.bn_stats(stats[:, p, i, :], x[:, p, i, :]).then_inc(st_ready.sem, 1)
                    dve.wait_ge(st_ready.sem, st_ready.at(blk.s))
                    settle(dve, paces)
                    for i in range(TILES):
                        dve.bn_aggr(mv[:, p, i, :], stats[:, p, i, :]).then_inc(mv_ready.sem, 1)

                def normalise(blk):
                    p = blk.par
                    dve.wait_ge(pool_small.sem, pool_small.at(blk.s))
                    if not (isinstance(blk.s, int) and blk.s < 2):
                        dve.wait_ge(transposed.sem, transposed.at(blk.s - 2))
                    for i in range(TILES):
                        dve.tensor_scalar(h[:, p, i, :], x[:, p, i, :], mv[:, p, i, 0:1], rstd[:, p, i:i + 1],
                                          ALU.subtract, ALU.mult).then_inc(h_ready.sem, 1)

                def split_low(blk):
                    for half in range(2):
                        dve.wait_ge(hi_ready.sem, hi_ready.at(blk.s, half + 1))
                        dve.tensor_tensor(hT_lo[:, half, :], trp[half][:, :], hT_hi[:, half, :].bitcast(F32),
                                          ALU.subtract).then_inc(lo_ready.sem, 1)

                def features(blk):
                    if not (isinstance(blk.s, int) and blk.s < 2):
                        dve.wait_ge(feat_out[blk.par].sem, feat_out[blk.par].at(blk.turn - 1))
                        dve.wait_ge(summed.sem, summed.at(blk.s - 2))
                        dve.wait_ge(kv_read.sem, kv_read.at(blk.s - 2))
                    for bank in range(2):
                        dve.wait_ge(exp_ready.sem, exp_ready.at(blk.s, bank + 1))
                        dve.scalar_tensor_tensor(out=feat[:, blk.par, 2 * bank:2 * bank + 2, :],
                                                 in0=q[:, blk.par, 2 * bank:2 * bank + 2, :], scalar=0.0,
                                                 in1=expneg[:, bank, :, :], op0=ALU.max, op1=ALU.add).then_inc(feat_ready.sem, 1)

                first = Blk(0, 0, B, NB)
                moments(first)
                moments(first.plus(1))
                normalise(first)
                normalise(first.plus(1))
                dve.memset(t["sn_hi"][:, :, :].bitcast(F32), 0.0).then_inc(gate_dve, 0 + 1)
                dve.memset(t["sn_lo"][:, :, :].bitcast(F32), 0.0).then_inc(w2_split, 1)
                dve.wait_ge(small_in, 16 * 5)
                dve.tensor_tensor(simsq[:, :, :], sim[:, :, :], sim[:, :, :], ALU.mult).then_inc(wq_split, 1)
                dve.wait_ge(gate_pe, 1)
                dve.tensor_copy(simn[:, 0, :], misc[0][:, 0:8]).then_inc(gate_dve, 1)
                dve.wait_ge(gate_pool, 3)
                for half in range(2):
                    dve.tensor_tensor(sn[:, half, :], sim[:, half, :], simn[:, 2, :], ALU.mult).then_inc(gate_dve, 1)
                dve.wait_ge(gate_dve, 4)
                dve.tensor_copy(t["sn_hi"][:, :, 0:8], sn[:, :, :]).then_inc(gate_dve, 1)
                dve.wait_ge(gate_dve, 5)
                dve.wait_ge(w2_split, 1)
                dve.tensor_tensor(t["sn_lo"][:, :, 0:8], sn[:, :, :], t["sn_hi"][:, :, 0:8].bitcast(F32), ALU.subtract).then_inc(gate_dve, 1)
                split_low(first)
                dve.tensor_copy(t["w2_hi"][:, :, :], w2_raw[:, :, :]).then_inc(w2_split, 1)
                dve.wait_ge(w2_split, 2)
                dve.tensor_tensor(t["w2_lo"][:, :, :], w2_raw[:, :, :], t["w2_hi"][:, :, :].bitcast(F32), ALU.subtract).then_inc(w2_split, 1)
                features(first)
                moments(first.plus(2))
                split_low(first.plus(1))
                normalise(first.plus(2))
                features(first.plus(1))

                def body(blk):
                    after, coming = blk.plus(2), blk.plus(3)
                    if coming is not None:
                        moments(coming)
                    if after is not None:
                        split_low(after)
                    if blk.j == NB - 1:
                        dve.wait_ge(kv_read.sem, kv_read.at(blk.s))
                        for half in range(2):
                            dve.tensor_tensor(kvT[:, half, :], kvp[half][:, 0, half * P:(half + 1) * P], headmask[:, :],
                                              ALU.mult).then_inc(kv_masked.sem, 1)
                    if coming is not None:
                        normalise(coming)
                    if blk.j == NB - 1:
                        dve.wait_ge(fold_out.sem, fold_out.at(blk.b - 1))
                        dve.wait_ge(fold_hi.sem, fold_hi.at(blk.b, 1))
                        dve.tensor_tensor(g_st_lo[:, :], misc[1][:, :], g_st_hi[:, :].bitcast(F32), ALU.subtract).then_inc(fold_lo.sem, 1)
                    if after is not None:
                        features(after)
                    if blk.j == NB - 1:
                        for half in range(2):
                            dve.wait_ge(fold_hi.sem, fold_hi.at(blk.b, 2 + half))
                            dve.tensor_tensor(gw_st_lo[:, half, :], misc[half][:, :], gw_st_hi[:, half, :].bitcast(F32),
                                              ALU.subtract).then_inc(fold_lo.sem, 1)

                loop_blocks(dve, B, NB, body)

            @block.scalar
            def _(act):
                def split_high(blk):
                    for half in range(2):
                        act.wait_ge(transposed.sem, transposed.at(blk.s, half + 1))
                        act.activation(hT_hi[:, half, :], trp[half][:, :], ACT.Copy).then_inc(hi_ready.sem, 1)

                def exps(blk):
                    for bank in range(2):
                        act.wait_ge(q_done.sem, q_done.at(blk.s, bank + 1))
                        if bank == 0 and not (isinstance(blk.s, int) and blk.s < 2):
                            act.wait_ge(kv_read.sem, kv_read.at(blk.s - 2))
                        if not (isinstance(blk.s, int) and blk.s == 0):
                            act.wait_ge(feat_ready.sem, feat_ready.at(blk.s - 1, bank + 1))
                        act.activation(negpart[:, bank, :, :], qp[bank][:, :, :], ACT.Relu, scale=-1.0).then_inc(neg_ready.sem, 1)
                        act.activation(q[:, blk.par, 2 * bank:2 * bank + 2, :], qp[bank][:, :, :], ACT.Copy).then_inc(q_copied.sem, 1)
                        act.wait_ge(neg_ready.sem, neg_ready.at(blk.s, bank + 1))
                        act.wait_ge(q_copied.sem, q_copied.at(blk.s, bank + 1))
                        act.activation(expneg[:, bank, :, :], negpart[:, bank, :, :], ACT.Exp, scale=-1.0).then_inc(exp_ready.sem, 1)

                def residual(blk):
                    p = blk.par
                    act.wait_ge(pool_small.sem, pool_small.at(blk.s))
                    act.wait_ge(x_in[p].sem, x_in[p].at(blk.turn))
                    if not (isinstance(blk.s, int) and blk.s < 2):
                        act.wait_ge(base_out[p].sem, base_out[p].at(blk.turn - 1))
                    for i in range(TILES):
                        act.activation(base[:, p, i, :], x[:, p, i, :], ACT.Identity, scale=rstd1[:, p, i:i + 1],
                                       bias=negmur[:, p, i:i + 1]).then_inc(base_ready.sem, 1)

                act.wait_ge(small_in, 16 * 5)
                act.activation(gates[:, 1, :], gates[:, 0, :], ACT.Exp, scale=-1.0).then_inc(gate_act, 1)
                first = Blk(0, 0, B, NB)
                residual(first)
                residual(first.plus(1))
                split_high(first)
                exps(first)
                split_high(first.plus(1))
                residual(first.plus(2))
                exps(first.plus(1))

                def body(blk):
                    after = blk.plus(2)
                    if after is not None:
                        split_high(after)
                    if blk.plus(3) is not None:
                        residual(blk.plus(3))
                    if blk.j == NB - 1:
                        act.wait_ge(fold_out.sem, fold_out.at(blk.b - 1))
                        act.wait_ge(ks_done.sem, ks_done.at(blk.b))
                        act.activation(ks_st[:, :], misc[0][:, 0:C], ACT.Copy).then_inc(ks_copied.sem, 1)
                        act.wait_ge(g_done.sem, g_done.at(blk.b))
                        act.activation(g_st_hi[:, :], misc[1][:, :], ACT.Copy).then_inc(fold_hi.sem, 1)
                        act.wait_ge(gT_done.sem, gT_done.at(blk.b))
                        act.activation(gT[:, :, :], kvp[0][:, :, :], ACT.Copy).then_inc(gT_copied.sem, 1)
                    if after is not None:
                        exps(after)
                    if blk.j == NB - 1:
                        for half in range(2):
                            act.wait_ge(gw_done.sem, gw_done.at(blk.b, half + 1))
                            act.activation(gw_st_hi[:, half, :], misc[half][:, :], ACT.Copy).then_inc(fold_hi.sem, 1)
                        act.wait_ge(ks_copied.sem, ks_copied.at(blk.b))
                        settle(act, paces)
                        act.wait_ge(fold_hi.sem, fold_hi.at(blk.b))
                        settle(act, paces)
                        act.wait_ge(fold_lo.sem, fold_lo.at(blk.b))
                        settle(act, paces)
                        r = bass.ds(value(blk.b * P), P)
                        act.dma_start(t["ks"][r, :], ks_st[:, :]).then_inc(fold_out.sem, 16)
                        act.dma_start(t["g_hi"][r, :], g_st_hi[:, :].bitcast(F32)).then_inc(fold_out.sem, 16)
                        act.dma_start(t["g_lo"][r, :], g_st_lo[:, :].bitcast(F32)).then_inc(fold_out.sem, 16)
                        act.dma_start(t["gw_hi"][r, :], gw_st_hi[:, :, :].bitcast(F32).rearrange("p h n -> p (h n)")).then_inc(fold_out.sem, 16)
                        act.dma_start(t["gw_lo"][r, :], gw_st_lo[:, :, :].bitcast(F32).rearrange("p h n -> p (h n)")).then_inc(fold_out.sem, 16)

                loop_blocks(act, B, NB, body)

            @block.tensor
            def _(pe):
                ks_done.grant(pe)
                ident = t["ident"]

                def transposes(blk):
                    if not (isinstance(blk.s, int) and blk.s == 0):
                        pe.wait_ge(lo_ready.sem, lo_ready.at(blk.s - 1))
                    for half in range(2):
                        for i in range(TILES):
                            pe.wait_ge(h_ready.sem, h_ready.at(blk.s, i + 1))
                            last = pe.transpose(trp[half][:, i * P:(i + 1) * P], h[:, blk.par, i, half * P:(half + 1) * P], ident[:, :])
                        last.then_inc(transposed.sem, 1)

                def project_q(blk):
                    if not (isinstance(blk.s, int) and blk.s == 0):
                        pe.wait_ge(exp_ready.sem, exp_ready.at(blk.s - 1))
                    for half in range(2):
                        pe.wait_ge(lo_ready.sem, lo_ready.at(blk.s, half + 1))
                    for i in range(TILES):
                        cols = slice(i * P, (i + 1) * P)
                        last = product(pe, qp[i // 2][:, i % 2, :],
                                       [((hT_hi[:, hf, cols], hT_lo[:, hf, cols]), (wq_hi[:, hf, :], wq_lo[:, hf, :]))
                                        for hf in range(2)])
                        if i % 2:
                            last.then_inc(q_done.sem, 1)

                first = Blk(0, 0, B, NB)
                pe.wait_ge(consts, 11)
                pe.wait_ge(wq_split, 3)
                for half in range(2):
                    last = pe.matmul(misc[0][:, 0:8], ones[:, :], simsq[:, half, :], start=(half == 0), stop=(half == 1))
                last.then_inc(gate_pe, 1)
                transposes(first)
                project_q(first)
                transposes(first.plus(1))
                project_q(first.plus(1))

                def values_keys(blk, tiles):
                    for i in tiles:
                        pe.wait_ge(feat_ready.sem, feat_ready.at(blk.s, i // 2 + 1))
                        for half in range(2):
                            last = pe.matmul(kvp[half][:, 0, :], q[:, blk.par, i, half * P:(half + 1) * P], feat[:, blk.par, i, :],
                                             start=(blk.j == 0 and i == 0), stop=(blk.j == NB - 1 and i == TILES - 1))
                    return last

                def fold(blk):
                    pe.wait_ge(summed.sem, summed.at(blk.s))
                    pe.wait_ge(fold_lo.sem, fold_lo.at(blk.b - 1))
                    for i in range(TILES):
                        last = pe.matmul(misc[0][:, 0:C], ones[:, :], fsum[:, i, :], start=(i == 0), stop=(i == TILES - 1))
                    last.then_inc(ks_done.sem, 1)
                    pe.wait_ge(kv_masked.sem, kv_masked.at(blk.b))
                    for half in range(2):
                        last = pe.matmul(misc[1][:, half * C:(half + 1) * C], kvT[:, half, :], wm[:, half, :], start=True, stop=True)
                    last.then_inc(g_done.sem, 1)
                    for nh in range(2):
                        for half in range(2):
                            last = pe.matmul(kvp[0][:, nh, half * P:(half + 1) * P], wm[:, half, nh * P:(nh + 1) * P],
                                             kvT[:, half, :], start=True, stop=True)
                    last.then_inc(gT_done.sem, 1)

                def fold_hidden(blk):
                    pe.wait_ge(gT_copied.sem, gT_copied.at(blk.b))
                    pe.wait_ge(ks_copied.sem, ks_copied.at(blk.b))
                    pe.wait_ge(fold_lo.sem, fold_lo.at(blk.b, 1))
                    for half in range(2):
                        for nh in range(2):
                            last = pe.matmul(misc[half][:, :], gT[:, nh, half * P:(half + 1) * P], w1[:, nh, :],
                                             start=(nh == 0), stop=(nh == 1))
                        last.then_inc(gw_done.sem, 1)

                def body(blk):
                    after = blk.plus(2)
                    values_keys(blk, (0, 1))
                    if after is not None:
                        transposes(after)
                    last = values_keys(blk, (2, 3))
                    last.then_inc(kv_read.sem, 1)
                    if blk.j == NB - 1:
                        fold(blk)
                    if after is not None:
                        project_q(after)
                    if blk.j == NB - 1:
                        fold_hidden(blk)

                loop_blocks(pe, B, NB, body)


def stage2(nc, t, d):
    B, NB, C, E, D = d["B"], d["NB"], d["C"], d["E"], d["D"]
    W3 = 3 * D
    CH = TILES * E
    with ExitStack() as st:
        c = Ctx(nc, st, "b_")
        feat = c.sb("feat", [P, 2, TILES, C])
        base = c.sb("base", [P, 2, TILES, C])
        ksum = c.sb("ksum", [P, C])
        g_hi = c.sb("g_hi", [P, 2, C], F32R)
        g_lo = c.sb("g_lo", [P, 2, C], F32R)
        gw_hi = c.sb("gw_hi", [P, 2, 2 * C], F32R)
        gw_lo = c.sb("gw_lo", [P, 2, 2 * C], F32R)
        den = c.sb("den", [P, 2, TILES * 8])
        z = c.sb("z", [P, TILES * 8])
        fz = c.sb("fz", [P, TILES, C])
        fT_hi = c.sb("fT_hi", [P, 2, BLOCK], F32R)
        fT_lo = c.sb("fT_lo", [P, 2, BLOCK], F32R)
        hid_hi = c.sb("hid_hi", [P, 4, BLOCK], F32R)
        hid_lo = c.sb("hid_lo", [P, 4, BLOCK], F32R)
        g1b = c.sb("g1b", [P, C])
        g2b = c.sb("g2b", [P, C])
        b1b = c.sb("b1b", [P, C])
        b2b = c.sb("b2b", [P, C])
        b12 = c.sb("b12", [P, C])
        stats = c.sb("stats", [P, 3, TILES, 6])
        mv = c.sb("mv", [P, 3, TILES, 2])
        ve = c.sb("ve", [P, 3, TILES])
        rstd = c.sb("rstd", [P, 3, TILES])
        negmu = c.sb("negmu", [P, TILES])
        negmur = c.sb("negmur", [P, TILES])
        nrm = c.sb("nrm", [P, 4, TILES])
        rnorm = c.sb("rnorm", [P, TILES])
        u = c.sb("u", [P, TILES, C])
        x1 = c.sb("x1", [P, 2, TILES, C])
        h2 = c.sb("h2", [P, TILES, C])
        h2T_hi = c.sb("h2T_hi", [P, 2, 2, BLOCK], F32R)
        h2T_lo = c.sb("h2T_lo", [P, 2, 2, BLOCK], F32R)
        lg = c.sb("lg", [P, TILES, E])
        logit = c.sb("logit", [P, TILES, E])
        above = c.sb("above", [P, TILES, E, E])
        atleast = c.sb("atleast", [P, TILES, E, E])
        before = c.sb("before", [P, E, E])
        notbefore = c.sb("notbefore", [P, E, E])
        rank = c.sb("rank", [P, TILES, E])
        top = c.sb("top", [P, 3, TILES])
        fallback = c.sb("fallback", [P, TILES, E])
        positive = c.sb("positive", [P, TILES, E])
        mask = c.sb("mask", [P, 2, TILES, E])
        gated = c.sb("gated", [P, TILES, E])
        expo = c.sb("expo", [P, 2, TILES, E])
        halves = c.sb("halves", [P, TILES, 6])
        total = c.sb("total", [P, 2, TILES])
        route = c.sb("route", [P, 2, TILES, E])
        acc = c.sb("acc", [P, TILES, W3])
        v_hi = c.sb("v_hi", [P, 2, TILES, D], F32R)
        v_lo = c.sb("v_lo", [P, 2, TILES, D], F32R)
        qk_hi = c.sb("qk_hi", [P, 2, 2, BLOCK], F32R)
        qk_lo = c.sb("qk_lo", [P, 2, 2, BLOCK], F32R)

        F = [c.ps(f"F{i}", [P, BLOCK]) for i in range(4)]
        X = [c.ps(f"X{i}", [P, W3]) for i in range(4)]

        setup_in = c.sem("setup_in")
        setup = c.sem("setup")
        feat_in = [c.flag(f"feat_in{i}", 16) for i in range(2)]
        base_in = [c.flag(f"base_in{i}", 16) for i in range(2)]
        ks_in = c.flag("ks_in", 16)
        fold_in = c.flag("fold_in", 16 * 4)
        prod_ready = c.flag("prod_ready", 1)
        den_ready = c.flag("den_ready", 1)
        z_steps = c.flag("z_steps", 2)
        fz_ready = c.flag("fz_ready", 1)
        res_ready = c.flag("res_ready", 1)
        f_transposed = c.flag("f_transposed", 2)
        f_hi = c.flag("f_hi", 2)
        f_lo = c.flag("f_lo", 2)
        msg_done = c.flag("msg_done", 2)
        hid_done = c.flag("hid_done", 4)
        h_hi = c.flag("h_hi", 4)
        h_lo = c.flag("h_lo", 4)
        mlp_done = c.flag("mlp_done", 2)
        st_ready = c.flag("st_ready", 3 * TILES)
        mv_ready = c.flag("mv_ready", 3 * TILES)
        rstd_steps = c.flag("rstd_steps", 6)
        h2_steps = c.flag("h2_steps", 2)
        rn_steps = c.flag("rn_steps", 5)
        u_ready = c.flag("u_ready", 2 * TILES)
        x1_steps = c.flag("x1_steps", 2 * TILES)
        x1_out = [c.flag(f"x1_out{i}", 16, ahead=1) for i in range(2)]
        h2_ready = c.flag("h2_ready", TILES)
        h2_transposed = c.flag("h2_transposed", 2)
        h2_hi = c.flag("h2_hi", 2)
        h2_lo = c.flag("h2_lo", 2)
        lg_done = c.flag("lg_done", 2)
        lg_ready = c.flag("lg_ready", 2)
        gate_steps = c.flag("gate_steps", 3)
        pair_steps = c.flag("pair_steps", 5)
        top_steps = c.flag("top_steps", 3)
        route_steps = c.flag("route_steps", 5)
        mask_ready = c.flag("mask_ready", 1)
        expo_in = c.flag("expo_in", 1)
        expo_ready = c.flag("expo_ready", 1)
        route_ready = c.flag("route_ready", 1, ahead=1)
        route_out = [c.flag(f"route_out{i}", 16, ahead=1) for i in range(2)]
        expert_done = c.flag("expert_done", CH)
        combined = c.flag("combined", CH, ahead=1)
        qk_transposed = c.flag("qk_transposed", 1, ahead=1)
        v_hi_ready = c.flag("v_hi_ready", TILES)
        v_lo_ready = c.flag("v_lo_ready", TILES, ahead=1)
        v_out = [c.flag(f"v_out{i}", 32, ahead=1) for i in range(2)]
        qk_hi_ready = c.flag("qk_hi_ready", 2)
        qk_lo_ready = c.flag("qk_lo_ready", 2, ahead=2)
        qk_out = [c.flag(f"qk_out{i}", 64, ahead=1) for i in range(2)]

        first = Blk(0, 0, B, NB)
        turns = B * NB // 2

        def tile_expert(k):
            return k // (2 * E) * 2 + k % 2, k % (2 * E) // 2

        def last_of_tile(i):
            return i // 2 * 2 * E + 2 * (E - 1) + i % 2

        paces = {e.engine: c.sem(f"pace_{k}") for k, e in enumerate((nc.sync, nc.gpsimd, nc.vector))}

        with nc.Block() as block:

            @block.sync
            def _(sp):
                for g in (*x1_out, *route_out, *v_out, *qk_out):
                    g.grant(sp)

                def load_feat(blk):
                    sp.dma_start(feat[:, blk.par, :, :], rows(t["feat"], blk, C)).then_inc(feat_in[blk.par].sem, 16)

                def load_base(blk):
                    sp.dma_start(base[:, blk.par, :, :], rows(t["base"], blk, C)).then_inc(base_in[blk.par].sem, 16)

                def load_ksum(b):
                    sp.dma_start(ksum[:, :], t["ks"][bass.ds(value(b * P), P), :]).then_inc(ks_in.sem, 16)

                def load_fold(b):
                    r = bass.ds(value(b * P), P)
                    sp.dma_start(g_hi[:, :, :].bitcast(F32).rearrange("p h n -> p (h n)"), t["g_hi"][r, :]).then_inc(fold_in.sem, 16)
                    sp.dma_start(g_lo[:, :, :].bitcast(F32).rearrange("p h n -> p (h n)"), t["g_lo"][r, :]).then_inc(fold_in.sem, 16)
                    sp.dma_start(gw_hi[:, :, :].bitcast(F32).rearrange("p h n -> p (h n)"), t["gw_hi"][r, :]).then_inc(fold_in.sem, 16)
                    sp.dma_start(gw_lo[:, :, :].bitcast(F32).rearrange("p h n -> p (h n)"), t["gw_lo"][r, :]).then_inc(fold_in.sem, 16)

                load_ksum(0)
                load_feat(first)
                load_fold(0)
                load_base(first)
                load_feat(first.plus(1))
                load_base(first.plus(1))
                for dst, name in ((g1b, "g1"), (g2b, "g2"), (b1b, "b1"), (b2b, "b2")):
                    sp.dma_start(dst[:, :], t[name].partition_broadcast(P)).then_inc(setup_in, 16)

                def body(blk):
                    nxt, after = blk.plus(1), blk.plus(2)
                    if after is not None:
                        sp.wait_ge(fz_ready.sem, fz_ready.at(blk.s))
                        settle(sp, paces)
                        load_feat(after)
                        sp.wait_ge(res_ready.sem, res_ready.at(blk.s))
                        settle(sp, paces)
                        load_base(after)
                    if blk.j == NB - 2 and after is not None:
                        sp.wait_ge(prod_ready.sem, prod_ready.at(nxt.s))
                        settle(sp, paces)
                        load_ksum(after.b)
                        sp.wait_ge(hid_done.sem, hid_done.at(nxt.s))
                        settle(sp, paces)
                        load_fold(after.b)
                    sp.wait_ge(v_lo_ready.sem, v_lo_ready.at(blk.s))
                    settle(sp, paces)
                    sp.dma_start(rows(t["v_hi"], blk, D), v_hi[:, blk.par, :, :].bitcast(F32)).then_inc(v_out[blk.par].sem, 16)
                    sp.dma_start(rows(t["v_lo"], blk, D), v_lo[:, blk.par, :, :].bitcast(F32)).then_inc(v_out[blk.par].sem, 16)
                    cols = bass.ds(value(blk.s * BLOCK), BLOCK)
                    for name, src, ready in (("T_hi", qk_hi, qk_hi_ready), ("T_lo", qk_lo, qk_lo_ready)):
                        sp.wait_ge(ready.sem, ready.at(blk.s))
                        settle(sp, paces)
                        for i, w in enumerate("qk"):
                            sp.dma_start(t[w + name][:, cols], src[:, blk.par, i, :].bitcast(F32)).then_inc(qk_out[blk.par].sem, 16)
                    if nxt is not None:
                        store_front(nxt)

                def store_front(blk):
                    sp.wait_ge(x1_steps.sem, x1_steps.at(blk.s))
                    settle(sp, paces)
                    sp.dma_start(rows(t["x1"], blk, C), x1[:, blk.par, :, :]).then_inc(x1_out[blk.par].sem, 16)
                    sp.wait_ge(route_ready.sem, route_ready.at(blk.s))
                    settle(sp, paces)
                    sp.dma_start(rows(t["route"], blk, E), route[:, blk.par, :, :]).then_inc(route_out[blk.par].sem, 16)

                store_front(first)
                loop_blocks(sp, B, NB, body)
                for par in range(2):
                    for g in (x1_out, route_out, v_out, qk_out):
                        sp.wait_ge(g[par].sem, g[par].at(turns - 1))
                        settle(sp, paces)

            @block.gpsimd
            def _(pool):
                v_lo_ready.grant(pool)
                route_ready.grant(pool)
                pool.memset(before[:, :, :], 1.0).then_inc(setup, 1)
                pool.wait_ge(setup, 1)
                pool.affine_select(out=before[:, :, :], in_=before[:, :, :], compare_op=ALU.is_gt, fill=0.0, base=0,
                                   pattern=[[1, E], [-1, E]], channel_multiplier=0).then_inc(setup, 1)
                pool.wait_ge(setup, 2)
                pool.tensor_scalar(notbefore[:, :, :], before[:, :, :], -1.0, 1.0, ALU.mult, ALU.add).then_inc(setup, 1)
                pool.wait_ge(setup_in, 64)
                pool.tensor_tensor(b12[:, :], b1b[:, :], b2b[:, :], ALU.add).then_inc(setup, 1)
                pool.wait_ge(setup, 4)

                def ksum_product(blk):
                    pool.wait_ge(feat_in[blk.par].sem, feat_in[blk.par].at(blk.turn))
                    pool.wait_ge(ks_in.sem, ks_in.at(blk.b))
                    if not (isinstance(blk.s, int) and blk.s == 0):
                        pool.wait_ge(f_transposed.sem, f_transposed.at(blk.s - 1))
                    pool.tensor_tensor(fz[:, :, :], feat[:, blk.par, :, :],
                                       ksum[:, :].unsqueeze(1).to_broadcast([P, TILES, C]), ALU.mult).then_inc(prod_ready.sem, 1)

                def normalise_feat(blk):
                    pool.wait_ge(den_ready.sem, den_ready.at(blk.s))
                    settle(pool, paces)
                    pool.tensor_scalar(den[:, 1, :], den[:, 0, :], ATTN_EPS, None, ALU.add).then_inc(z_steps.sem, 1)
                    pool.wait_ge(z_steps.sem, z_steps.at(blk.s, 1))
                    pool.tensor_tensor(z[:, :], den[:, 1, :], t["minus_one"][:, :], ALU.pow).then_inc(z_steps.sem, 1)
                    pool.wait_ge(z_steps.sem, z_steps.at(blk.s, 2))
                    pool.tensor_tensor(fz[:, :, :].rearrange("p t (h k) -> p (t h) k", h=8),
                                       feat[:, blk.par, :, :].rearrange("p t (h k) -> p (t h) k", h=8),
                                       z[:, :].unsqueeze(2).to_broadcast([P, TILES * 8, C // 8]), ALU.mult).then_inc(fz_ready.sem, 1)

                def residual(blk):
                    pool.wait_ge(base_in[blk.par].sem, base_in[blk.par].at(blk.turn))
                    pool.wait_ge(x1_out[blk.par].sem, x1_out[blk.par].at(blk.turn - 1))
                    pool.tensor_tensor(x1[:, blk.par, :, :], base[:, blk.par, :, :],
                                       b12[:, :].unsqueeze(1).to_broadcast([P, TILES, C]), ALU.add).then_inc(res_ready.sem, 1)

                def rstds(blk, n):
                    pool.wait_ge(mv_ready.sem, mv_ready.at(blk.s, (n + 1) * TILES))
                    settle(pool, paces)
                    pool.tensor_scalar(ve[:, n, :], mv[:, n, :, 1], LN_EPS, None, ALU.add).then_inc(rstd_steps.sem, 1)
                    pool.wait_ge(rstd_steps.sem, rstd_steps.at(blk.s, 2 * n + 1))
                    pool.tensor_tensor(rstd[:, n, :], ve[:, n, :], t["minus_half"][:, 0:TILES], ALU.pow).then_inc(rstd_steps.sem, 1)

                def x1_scales(blk):
                    pool.wait_ge(rstd_steps.sem, rstd_steps.at(blk.s))
                    settle(pool, paces)
                    pool.tensor_scalar(negmu[:, :], mv[:, 2, :, 0], -1.0, None, ALU.mult).then_inc(h2_steps.sem, 1)
                    pool.wait_ge(h2_steps.sem, h2_steps.at(blk.s, 1))
                    pool.tensor_tensor(negmur[:, :], negmu[:, :], rstd[:, 2, :], ALU.mult).then_inc(h2_steps.sem, 1)
                    pool.tensor_scalar(nrm[:, 0, :], mv[:, 2, :, 1], float(C), None, ALU.mult).then_inc(rn_steps.sem, 1)
                    pool.wait_ge(rn_steps.sem, rn_steps.at(blk.s, 1))
                    pool.tensor_tensor(nrm[:, 1, :], nrm[:, 0, :], t["half"][:, 0:TILES], ALU.pow).then_inc(rn_steps.sem, 1)
                    pool.wait_ge(rn_steps.sem, rn_steps.at(blk.s, 2))
                    pool.tensor_tensor(nrm[:, 2, :], nrm[:, 1, :], rstd[:, 2, :], ALU.mult).then_inc(rn_steps.sem, 1)
                    pool.wait_ge(rn_steps.sem, rn_steps.at(blk.s, 3))
                    settle(pool, paces)
                    pool.tensor_scalar(nrm[:, 3, :], nrm[:, 2, :], NORM_EPS, None, ALU.max).then_inc(rn_steps.sem, 1)
                    pool.wait_ge(rn_steps.sem, rn_steps.at(blk.s, 4))
                    pool.tensor_tensor(rnorm[:, :], nrm[:, 3, :], t["minus_one"][:, 0:TILES], ALU.pow).then_inc(rn_steps.sem, 1)

                def routing(blk):
                    p = blk.par
                    pool.wait_ge(expo_ready.sem, expo_ready.at(blk.s))
                    pool.wait_ge(mask_ready.sem, mask_ready.at(blk.s))
                    pool.tensor_tensor(expo[:, 1, :, :], expo[:, 0, :, :], mask[:, p, :, :], ALU.mult).then_inc(route_steps.sem, 1)
                    pool.wait_ge(route_steps.sem, route_steps.at(blk.s, 1))
                    pool.tensor_tensor(halves[:, :, 0:4], expo[:, 1, :, 0:4], expo[:, 1, :, 4:8], ALU.add).then_inc(route_steps.sem, 1)
                    pool.wait_ge(route_steps.sem, route_steps.at(blk.s, 2))
                    pool.tensor_tensor(halves[:, :, 4:6], halves[:, :, 0:2], halves[:, :, 2:4], ALU.add).then_inc(route_steps.sem, 1)
                    pool.wait_ge(route_steps.sem, route_steps.at(blk.s, 3))
                    pool.tensor_tensor(total[:, 0, :], halves[:, :, 4], halves[:, :, 5], ALU.add).then_inc(route_steps.sem, 1)
                    pool.wait_ge(route_steps.sem, route_steps.at(blk.s, 4))
                    pool.tensor_tensor(total[:, 1, :], total[:, 0, :], t["minus_one"][:, 0:TILES], ALU.pow).then_inc(route_steps.sem, 1)
                    pool.wait_ge(route_steps.sem, route_steps.at(blk.s, 5))
                    pool.wait_ge(route_out[p].sem, route_out[p].at(blk.turn - 1))
                    pool.tensor_tensor(route[:, p, :, :], expo[:, 1, :, :],
                                       total[:, 1, :].unsqueeze(2).to_broadcast([P, TILES, E]), ALU.mult).then_inc(route_ready.sem, 1)

                def v_low(blk, i):
                    p = blk.par
                    if i == 0:
                        pool.wait_ge(v_out[p].sem, v_out[p].at(blk.turn - 1))
                    pool.wait_ge(v_hi_ready.sem, v_hi_ready.at(blk.s, i + 1))
                    pool.tensor_tensor(v_lo[:, p, i, :], acc[:, i, 2 * D:], v_hi[:, p, i, :].bitcast(F32),
                                       ALU.subtract).then_inc(v_lo_ready.sem, 1)

                ksum_product(first)
                normalise_feat(first)
                residual(first)
                ksum_product(first.plus(1))
                normalise_feat(first.plus(1))
                for n in range(3):
                    rstds(first, n)
                x1_scales(first)
                routing(first)

                def body(blk):
                    nxt, after = blk.plus(1), blk.plus(2)
                    if nxt is not None:
                        residual(nxt)
                        rstds(nxt, 0)
                        rstds(nxt, 1)
                        rstds(nxt, 2)
                        x1_scales(nxt)
                    v_low(blk, 0)
                    v_low(blk, 1)
                    if after is not None:
                        ksum_product(after)
                        normalise_feat(after)
                    if nxt is not None:
                        routing(nxt)
                    v_low(blk, 2)
                    v_low(blk, 3)

                loop_blocks(pool, B, NB, body)

            @block.scalar
            def _(act):
                def f_high(blk):
                    for half in range(2):
                        act.wait_ge(f_transposed.sem, f_transposed.at(blk.s, half + 1))
                        act.activation(fT_hi[:, half, :], F[half][:, :], ACT.Copy).then_inc(f_hi.sem, 1)

                def hidden_high(blk, k):
                    act.wait_ge(hid_done.sem, hid_done.at(blk.s, k + 1))
                    act.activation(hid_hi[:, k, :], F[k % 2][:, :], ACT.Relu).then_inc(h_hi.sem, 1)

                def normalise_x1(blk):
                    act.wait_ge(h2_steps.sem, h2_steps.at(blk.s))
                    act.wait_ge(x1_steps.sem, x1_steps.at(blk.s))
                    for i in range(TILES):
                        act.activation(h2[:, i, :], x1[:, blk.par, i, :], ACT.Identity, scale=rstd[:, 2, i:i + 1],
                                       bias=negmur[:, i:i + 1]).then_inc(h2_ready.sem, 1)

                def h2_high(blk):
                    for half in range(2):
                        act.wait_ge(h2_transposed.sem, h2_transposed.at(blk.s, half + 1))
                        act.activation(h2T_hi[:, blk.par, half, :], F[2 + half][:, :], ACT.Copy).then_inc(h2_hi.sem, 1)

                def gate_exp(blk):
                    act.wait_ge(expo_in.sem, expo_in.at(blk.s))
                    act.activation(expo[:, 0, :, :], gated[:, :, :], ACT.Exp).then_inc(expo_ready.sem, 1)

                def v_high(blk, i):
                    act.wait_ge(combined.sem, combined.at(blk.s, last_of_tile(i) + 1))
                    if i == 0:
                        act.wait_ge(v_out[blk.par].sem, v_out[blk.par].at(blk.turn - 1))
                    act.activation(v_hi[:, blk.par, i, :], acc[:, i, 2 * D:], ACT.Copy).then_inc(v_hi_ready.sem, 1)

                def qk_high(blk):
                    act.wait_ge(qk_out[blk.par].sem, qk_out[blk.par].at(blk.turn - 1))
                    act.wait_ge(qk_transposed.sem, qk_transposed.at(blk.s))
                    for k in range(2):
                        act.activation(qk_hi[:, blk.par, k, :], F[2 + k][:, :], ACT.Copy).then_inc(qk_hi_ready.sem, 1)

                f_high(first)
                for k in range(4):
                    hidden_high(first, k)
                normalise_x1(first)
                h2_high(first)
                f_high(first.plus(1))
                gate_exp(first)

                def body(blk):
                    nxt, after = blk.plus(1), blk.plus(2)
                    if nxt is not None:
                        for k in range(4):
                            hidden_high(nxt, k)
                        normalise_x1(nxt)
                    v_high(blk, 0)
                    v_high(blk, 1)
                    if nxt is not None:
                        h2_high(nxt)
                        gate_exp(nxt)
                    v_high(blk, 2)
                    v_high(blk, 3)
                    if after is not None:
                        f_high(after)
                    qk_high(blk)

                loop_blocks(act, B, NB, body)

            @block.vector
            def _(dve):
                combined.grant(dve)
                qk_lo_ready.grant(dve)
                msg = [F[2 + i // 2][:, (i % 2) * C:(i % 2 + 1) * C] for i in range(TILES)]
                mlp = [F[i // 2][:, (i % 2) * C:(i % 2 + 1) * C] for i in range(TILES)]

                def denominators(blk):
                    dve.wait_ge(prod_ready.sem, prod_ready.at(blk.s))
                    dve.tensor_reduce(den[:, 0, :], fz[:, :, :].rearrange("p t (h k) -> p (t h) k", h=8),
                                      AX_X, ALU.add).then_inc(den_ready.sem, 1)

                def f_low(blk, half):
                    dve.wait_ge(f_hi.sem, f_hi.at(blk.s, half + 1))
                    dve.tensor_tensor(fT_lo[:, half, :], F[half][:, :], fT_hi[:, half, :].bitcast(F32),
                                      ALU.subtract).then_inc(f_lo.sem, 1)

                def moments(blk, n, i):
                    if n == 0:
                        dve.wait_ge(msg_done.sem, msg_done.at(blk.s, i // 2 + 1))
                    elif n == 1:
                        dve.wait_ge(mlp_done.sem, mlp_done.at(blk.s, i // 2 + 1))
                    else:
                        dve.wait_ge(x1_steps.sem, x1_steps.at(blk.s, TILES + i + 1))
                    src = (msg[i], mlp[i], x1[:, blk.par, i, :])[n]
                    dve.bn_stats(stats[:, n, i, :], src).then_inc(st_ready.sem, 1)

                def gather(blk, n):
                    dve.wait_ge(st_ready.sem, st_ready.at(blk.s, (n + 1) * TILES))
                    settle(dve, paces)
                    for i in range(TILES):
                        dve.bn_aggr(mv[:, n, i, :], stats[:, n, i, :]).then_inc(mv_ready.sem, 1)

                def centre(blk, n, i):
                    dve.wait_ge(mv_ready.sem, mv_ready.at(blk.s, n * TILES + i + 1))
                    dve.scalar_tensor_tensor(out=u[:, i, :], in0=(msg, mlp)[n][i], scalar=mv[:, n, i, 0:1],
                                             in1=(g1b, g2b)[n][:, :], op0=ALU.subtract, op1=ALU.mult).then_inc(u_ready.sem, 1)

                def add_norm(blk, n, i):
                    dve.wait_ge(u_ready.sem, u_ready.at(blk.s, n * TILES + i + 1))
                    dve.wait_ge(rstd_steps.sem, rstd_steps.at(blk.s, 2 * n + 2))
                    if n == 0:
                        dve.wait_ge(res_ready.sem, res_ready.at(blk.s))
                    else:
                        dve.wait_ge(x1_steps.sem, x1_steps.at(blk.s, i + 1))
                    dve.scalar_tensor_tensor(out=x1[:, blk.par, i, :], in0=u[:, i, :], scalar=rstd[:, n, i:i + 1],
                                             in1=x1[:, blk.par, i, :], op0=ALU.mult, op1=ALU.add).then_inc(x1_steps.sem, 1)

                def hidden_low(blk, k):
                    dve.wait_ge(h_hi.sem, h_hi.at(blk.s, k + 1))
                    dve.scalar_tensor_tensor(out=hid_lo[:, k, :], in0=F[k % 2][:, :], scalar=0.0,
                                             in1=hid_hi[:, k, :].bitcast(F32), op0=ALU.max, op1=ALU.subtract).then_inc(h_lo.sem, 1)

                def h2_low(blk, half):
                    dve.wait_ge(h2_hi.sem, h2_hi.at(blk.s, half + 1))
                    dve.tensor_tensor(h2T_lo[:, blk.par, half, :], F[2 + half][:, :], h2T_hi[:, blk.par, half, :].bitcast(F32),
                                      ALU.subtract).then_inc(h2_lo.sem, 1)

                def logits(blk):
                    dve.wait_ge(rn_steps.sem, rn_steps.at(blk.s))
                    for bank in range(2):
                        dve.wait_ge(lg_done.sem, lg_done.at(blk.s, bank + 1))
                        dve.tensor_tensor(lg[:, 2 * bank:2 * bank + 2, :],
                                          F[bank][:, :].rearrange("p (t n) -> p t n", t=2)[:, :, 0:E],
                                          rnorm[:, 2 * bank:2 * bank + 2].unsqueeze(2).to_broadcast([P, 2, E]),
                                          ALU.mult).then_inc(lg_ready.sem, 1)

                def router(blk, part):
                    p = blk.par

                    def per_tile(a):
                        return a.unsqueeze(2).to_broadcast([P, TILES, E])

                    def pairs(a):
                        return a.rearrange("p t e j -> p t (e j)")

                    def order(a):
                        return a[:, :, :].rearrange("p e j -> p (e j)").unsqueeze(1).to_broadcast([P, TILES, E * E])

                    def step(k, ins):
                        ins.then_inc(gate_steps.sem, 1)
                        dve.wait_ge(gate_steps.sem, gate_steps.at(blk.s, k))

                    lj = logit[:, :, :].unsqueeze(2).to_broadcast([P, TILES, E, E])
                    le = logit[:, :, :].unsqueeze(3).to_broadcast([P, TILES, E, E])
                    if part == 0:
                        dve.wait_ge(lg_ready.sem, lg_ready.at(blk.s))
                        step(1, dve.tensor_tensor(logit[:, :, :], lg[:, :, :],
                                                  t["sig"][:, :].unsqueeze(1).to_broadcast([P, TILES, E]), ALU.subtract))
                        dve.tensor_tensor(above[:, :, :, :], lj, le, ALU.is_gt).then_inc(pair_steps.sem, 1)
                        dve.tensor_tensor(atleast[:, :, :, :], lj, le, ALU.is_ge).then_inc(pair_steps.sem, 1)
                    if part == 1:
                        dve.wait_ge(pair_steps.sem, pair_steps.at(blk.s, 2))
                        dve.tensor_tensor(pairs(atleast), pairs(atleast), order(before), ALU.mult).then_inc(pair_steps.sem, 1)
                        dve.tensor_tensor(pairs(above), pairs(above), order(notbefore), ALU.mult).then_inc(pair_steps.sem, 1)
                        dve.tensor_reduce(top[:, 0, :], logit[:, :, :], AX_X, ALU.max).then_inc(top_steps.sem, 1)
                    if part == 2:
                        dve.wait_ge(pair_steps.sem, pair_steps.at(blk.s, 4))
                        dve.tensor_tensor(pairs(above), pairs(above), pairs(atleast), ALU.add).then_inc(pair_steps.sem, 1)
                        dve.wait_ge(top_steps.sem, top_steps.at(blk.s, 1))
                        dve.tensor_scalar(top[:, 1, :], top[:, 0, :], 0.0, None, ALU.is_le).then_inc(top_steps.sem, 1)
                        dve.tensor_scalar(top[:, 2, :], top[:, 0, :], 0.0, None, ALU.max).then_inc(top_steps.sem, 1)
                        dve.wait_ge(pair_steps.sem, pair_steps.at(blk.s, 5))
                        dve.tensor_reduce(rank[:, :, :], above[:, :, :, :], AX_X, ALU.add).then_inc(gate_steps.sem, 1)
                    if part == 3:
                        dve.wait_ge(route_ready.sem, route_ready.at(blk.s - 1))
                        dve.wait_ge(top_steps.sem, top_steps.at(blk.s, 3))
                        dve.scalar_tensor_tensor(out=gated[:, :, :], in0=logit[:, :, :], scalar=0.0, in1=per_tile(top[:, 2, :]),
                                                 op0=ALU.max, op1=ALU.subtract).then_inc(expo_in.sem, 1)
                        dve.wait_ge(gate_steps.sem, gate_steps.at(blk.s, 2))
                        step(3, dve.scalar_tensor_tensor(out=fallback[:, :, :], in0=rank[:, :, :], scalar=2.0,
                                                         in1=per_tile(top[:, 1, :]), op0=ALU.is_lt, op1=ALU.mult))
                        dve.scalar_tensor_tensor(out=mask[:, p, :, :], in0=logit[:, :, :], scalar=0.0, in1=fallback[:, :, :],
                                                 op0=ALU.is_gt, op1=ALU.max).then_inc(mask_ready.sem, 1)

                def combine(blk, k):
                    i, e = tile_expert(k)
                    m = mask[:, blk.par, i, e:e + 1]
                    dve.wait_ge(expert_done.sem, expert_done.at(blk.s, k + 1))
                    if k == 0:
                        dve.wait_ge(mask_ready.sem, mask_ready.at(blk.s))
                        dve.wait_ge(qk_transposed.sem, qk_transposed.at(blk.s - 1))
                    if e == 0:
                        dve.wait_ge(v_lo_ready.sem, v_lo_ready.at(blk.s - 1, i + 1))
                        dve.tensor_scalar(acc[:, i, :], X[k % 4][:, :], m, None, ALU.mult).then_inc(combined.sem, 1)
                    else:
                        dve.wait_ge(combined.sem, combined.at(blk.s, k - 1))
                        dve.scalar_tensor_tensor(out=acc[:, i, :], in0=X[k % 4][:, :], scalar=m, in1=acc[:, i, :],
                                                 op0=ALU.mult, op1=ALU.add).then_inc(combined.sem, 1)

                def qk_low(blk):
                    for k in range(2):
                        dve.wait_ge(qk_hi_ready.sem, qk_hi_ready.at(blk.s, k + 1))
                        dve.tensor_tensor(qk_lo[:, blk.par, k, :], F[2 + k][:, :], qk_hi[:, blk.par, k, :].bitcast(F32),
                                          ALU.subtract).then_inc(qk_lo_ready.sem, 1)

                def two(what, blk, n, k):
                    what(blk, n, 2 * k)
                    what(blk, n, 2 * k + 1)

                def front(blk, k):
                    if k in (3, 4):
                        two(moments, blk, 0, k - 3)
                    if k == 4:
                        gather(blk, 0)
                    if k in (4, 5):
                        hidden_low(blk, k - 4)
                    if k in (6, 7):
                        two(centre, blk, 0, k - 6)
                    if k in (7, 8):
                        hidden_low(blk, k - 5)
                    if k in (9, 10):
                        two(add_norm, blk, 0, k - 9)
                    if k in (10, 11):
                        two(moments, blk, 1, k - 10)
                    if k == 11:
                        gather(blk, 1)
                    if k in (12, 13):
                        two(centre, blk, 1, k - 12)
                    if k in (14, 15):
                        two(add_norm, blk, 1, k - 14)
                    if k in (15, 16):
                        two(moments, blk, 2, k - 15)
                    if k == 16:
                        gather(blk, 2)
                    if k in (22, 23):
                        h2_low(blk, k - 22)
                    if k == 27:
                        logits(blk)
                    if k >= 28:
                        router(blk, k - 28)

                dve.wait_ge(setup, 4)
                denominators(first)
                f_low(first, 0)
                f_low(first, 1)
                denominators(first.plus(1))
                for k in range(CH):
                    front(first, k)
                f_low(first.plus(1), 0)
                f_low(first.plus(1), 1)

                def body(blk):
                    nxt, after = blk.plus(1), blk.plus(2)
                    for k in range(CH):
                        if nxt is not None:
                            front(nxt, k)
                        if k == 20 and after is not None:
                            denominators(after)
                        combine(blk, k)
                    if after is not None:
                        f_low(after, 0)
                        f_low(after, 1)
                    dve.wait_ge(qk_out[blk.par].sem, qk_out[blk.par].at(blk.turn - 1))
                    qk_low(blk)

                loop_blocks(dve, B, NB, body)

            @block.tensor
            def _(pe):
                qk_transposed.grant(pe)
                ident = t["ident"]

                def split(hi, lo, *at):
                    return hi[(slice(None), *at)], lo[(slice(None), *at)]

                def f_transpose(blk):
                    if not (isinstance(blk.s, int) and blk.s == 0):
                        pe.wait_ge(lg_ready.sem, lg_ready.at(blk.s - 1))
                    pe.wait_ge(fz_ready.sem, fz_ready.at(blk.s))
                    for half in range(2):
                        for i in range(TILES):
                            last = pe.transpose(F[half][:, i * P:(i + 1) * P], fz[:, i, half * P:(half + 1) * P], ident[:, :])
                        last.then_inc(f_transposed.sem, 1)

                def message(blk):
                    pe.wait_ge(f_lo.sem, f_lo.at(blk.s))
                    pe.wait_ge(fold_in.sem, fold_in.at(blk.b))
                    for i in range(TILES):
                        cols = slice(i * P, (i + 1) * P)
                        last = product(pe, F[2 + i // 2][:, (i % 2) * C:(i % 2 + 1) * C],
                                       [(split(fT_hi, fT_lo, hf, cols), split(g_hi, g_lo, hf)) for hf in range(2)])
                        if i % 2:
                            last.then_inc(msg_done.sem, 1)

                def hidden(blk, k):
                    if k >= 2:
                        pe.wait_ge(h_lo.sem, h_lo.at(blk.s, k - 1))
                    cols = slice(k * P, (k + 1) * P)
                    product(pe, F[k % 2][:, :], [(split(gw_hi, gw_lo, hf, cols), split(fT_hi, fT_lo, hf)) for hf in range(2)])\
                        .then_inc(hid_done.sem, 1)

                def mlp(blk, bank):
                    pe.wait_ge(h_lo.sem, h_lo.at(blk.s))
                    for i in (2 * bank, 2 * bank + 1):
                        cols = slice(i * P, (i + 1) * P)
                        last = product(pe, F[bank][:, (i % 2) * C:(i % 2 + 1) * C],
                                       [(split(hid_hi, hid_lo, k, cols), split(t["w2_hi"], t["w2_lo"], k)) for k in range(4)])
                    last.then_inc(mlp_done.sem, 1)

                def h2_transpose(blk):
                    for half in range(2):
                        for i in range(TILES):
                            pe.wait_ge(h2_ready.sem, h2_ready.at(blk.s, i + 1))
                            last = pe.transpose(F[2 + half][:, i * P:(i + 1) * P], h2[:, i, half * P:(half + 1) * P], ident[:, :])
                        last.then_inc(h2_transposed.sem, 1)

                def gate(blk):
                    pe.wait_ge(h2_lo.sem, h2_lo.at(blk.s))
                    for i in range(TILES):
                        cols = slice(i * P, (i + 1) * P)
                        last = product(pe, F[i // 2][:, (i % 2) * C:(i % 2 + 1) * C],
                                       [(split(h2T_hi, h2T_lo, blk.par, hf, cols), split(t["sn_hi"], t["sn_lo"], hf)) for hf in range(2)])
                        if i % 2:
                            last.then_inc(lg_done.sem, 1)

                def expert(blk, k):
                    i, e = tile_expert(k)
                    pe.wait_ge(combined.sem, combined.at(blk.s, k - 3))
                    cols = slice(i * P, (i + 1) * P)
                    pairs = []
                    for hf in range(2):
                        w = slice((hf * E + e) * W3, (hf * E + e + 1) * W3)
                        pairs.append((split(h2T_hi, h2T_lo, blk.par, hf, cols), (t["wqkv_hi"][:, w], t["wqkv_lo"][:, w])))
                    product(pe, X[k % 4][:, :], pairs).then_inc(expert_done.sem, 1)

                def qk_transpose(blk):
                    for i in range(TILES):
                        pe.wait_ge(combined.sem, combined.at(blk.s, last_of_tile(i) + 1))
                        for k in range(2):
                            last = pe.transpose(F[2 + k][:, i * P:(i + 1) * P], acc[:, i, k * D:(k + 1) * D], ident[:, :])
                    last.then_inc(qk_transposed.sem, 1)

                def front(blk, k):
                    if k == 2:
                        pe.wait_ge(qk_lo_ready.sem, qk_lo_ready.at(blk.s - 2))
                        message(blk)
                    if k in (3, 4):
                        hidden(blk, k - 3)
                    if k in (6, 7):
                        hidden(blk, k - 4)
                    if k in (9, 10):
                        mlp(blk, k - 9)
                    if k == 21:
                        h2_transpose(blk)
                    if k == 25:
                        gate(blk)

                f_transpose(first)
                for k in range(CH):
                    front(first, k)
                f_transpose(first.plus(1))

                def body(blk):
                    nxt, after = blk.plus(1), blk.plus(2)
                    for k in range(CH):
                        if nxt is not None:
                            front(nxt, k)
                        expert(blk, k)
                    if after is not None:
                        f_transpose(after)
                    qk_transpose(blk)

                loop_blocks(pe, B, NB, body)


class Tally:

    def __init__(self, sem, counts, ahead=0):
        self.sem, self.counts, self.ahead = sem, counts, ahead

    def at(self, blk, k=None):
        within = sum(self.counts[:blk.j]) + (self.counts[blk.j] if k is None else k)
        return value((blk.b + self.ahead) * sum(self.counts) + within)

    def grant(self, eng):
        eng.sem_inc(self.sem, self.ahead * sum(self.counts))


def stage3(nc, t, d):
    B, NB, C, E, D = d["B"], d["NB"], d["C"], d["E"], d["D"]
    SCALE = float(D) ** -0.5
    counts = [TILES * (NB - j) for j in range(NB)]
    GROUPS = E * C // BLOCK
    OUTS = TILES * GROUPS

    def chunks(blk):
        return NB - blk.j

    def place(blk):
        return Blk(blk.b, NB - 1 - blk.j, B, NB)

    def events(blk, nxt):
        n = counts[blk.j]
        own = [("T", 0), ("T", 1)]
        for u in range(n):
            if u + 2 < n:
                own.append(("T", u + 2))
            own.append(("V", u))
        values_end = len(own)
        own += [("O", r) for r in range(OUTS)]
        m = counts[nxt.j] if nxt is not None else 0
        share = max(2, m * values_end // (values_end + OUTS)) - 2
        places = [2, 3] + [4 + (x + 1) * (values_end - 5) // (share + 1) for x in range(share)]
        at_o = min(2, m - len(places))
        places += [values_end] * at_o
        rest = m - len(places)
        places += [values_end + 2 + (OUTS - 5) * x // max(1, rest) for x in range(rest)]
        out, k = [], 0
        for at, e in enumerate(own):
            while k < m and at >= places[k]:
                out.append(("S", k))
                k += 1
            out.append(e)
        assert k == m
        return out

    def events_act(blk, nxt):
        LAG = 2
        order = events(blk, nxt)
        if nxt is None:
            return order
        where = {k: at for at, (what, k) in enumerate(order) if what == "S"}
        m, n = counts[nxt.j], chunks(nxt)
        at_x = []
        for k in range(m):
            at = where[k // n * n + n - 1] + LAG
            if k + 4 < m:
                at = min(at, where[k + 4])
            at_x.append(max([at] + at_x[-1:]))
        out, k = [], 0
        for at, e in enumerate(order):
            while k < m and at_x[k] <= at:
                out.append(("X", k))
                k += 1
            if e[0] != "S":
                out.append(e)
        assert k == m
        return out

    with ExitStack() as st:
        c = Ctx(nc, st, "c_")
        kT_hi = c.sb("kT_hi", [P, NB, BLOCK], F32R)
        kT_lo = c.sb("kT_lo", [P, NB, BLOCK], F32R)
        v_hi = c.sb("v_hi", [P, NB * TILES, D], F32R)
        v_lo = c.sb("v_lo", [P, NB * TILES, D], F32R)
        qT_hi = c.sb("qT_hi", [P, 2, BLOCK], F32R)
        qT_lo = c.sb("qT_lo", [P, 2, BLOCK], F32R)
        x1 = c.sb("x1", [P, 2, TILES, C])
        route = c.sb("route", [P, 2, TILES, E])
        weight = c.sb("weight", [P, 2, TILES, E])
        probs = c.sb("probs", [P, 2, TILES, NB * BLOCK])
        causal = c.sb("causal", [P, P])
        cmax = c.sb("cmax", [P, TILES, NB])
        tmax = c.sb("tmax", [P, TILES])
        nmax = c.sb("nmax", [P, TILES])
        csum = c.sb("csum", [P, 2, TILES, NB])
        rsum = c.sb("rsum", [P, 2, TILES])
        pT_hi = c.sb("pT_hi", [P, 3, BLOCK], F32R)
        pT_lo = c.sb("pT_lo", [P, 3, BLOCK], F32R)
        oT_hi = c.sb("oT_hi", [P, BLOCK], F32R)
        oT_lo = c.sb("oT_lo", [P, BLOCK], F32R)
        term = c.sb("term", [P, 4, C])

        S = [c.ps(f"S{i}", [P, BLOCK]) for i in range(4)]
        T = [c.ps(f"T{i}", [P, BLOCK]) for i in range(2)]
        Y = [c.ps(f"Y{i}", [P, BLOCK]) for i in range(2)]
        T_BANKS = [*T, Y[1]]

        setup = c.sem("setup")
        k_in = [c.flag(f"k_in{i}", 32) for i in range(NB)]
        v_in = [c.flag(f"v_in{i}", 32) for i in range(NB)]
        q_in = [c.flag(f"q_in{i}", 32) for i in range(2)]
        x1_in = [c.flag(f"x1_in{i}", 32) for i in range(2)]

        def tally(name, ahead=0):
            return Tally(c.sem(name), counts, ahead)

        s_done = tally("s_done")
        causal_done = c.flag("causal_done", TILES)
        cmax_ready = tally("cmax_ready")
        tmax_ready = c.flag("tmax_ready", TILES)
        nmax_ready = c.flag("nmax_ready", TILES)
        exp_done = tally("exp_done", 1)
        p_transposed = tally("p_transposed", 1)
        p_hi = tally("p_hi")
        p_lo = tally("p_lo", 1)
        pv_done = tally("pv_done", 1)
        rsum_ready = c.flag("rsum_ready", 1)
        rinv_ready = c.flag("rinv_ready", 1)
        weight_ready = c.flag("weight_ready", 1)
        o_hi = c.flag("o_hi", 1)
        o_lo = c.flag("o_lo", 1)
        out_done = c.flag("out_done", OUTS, ahead=1)
        summed = c.flag("summed", OUTS, ahead=1)
        scaled = c.flag("scaled", OUTS, ahead=1)
        added = c.flag("added", OUTS, ahead=1)
        stored = [c.flag(f"stored{i}", 16, ahead=1) for i in range(2)]

        first = Blk(0, 0, B, NB)

        OUT_BANKS = [Y[1], T[0], T[1], Y[0]]

        def tile_group(r):
            return r // (2 * GROUPS) * 2 + r % 2, r % (2 * GROUPS) // 2

        paces = {e.engine: c.sem(f"pace_{k}") for k, e in enumerate((nc.sync, nc.gpsimd, nc.vector))}

        with nc.Block() as block:

            @block.sync
            def _(sp):
                for g in stored:
                    g.grant(sp)

                def load_k(b, ch):
                    cols = bass.ds(value((b * NB + ch) * BLOCK), BLOCK)
                    sp.dma_start(kT_hi[:, ch, :].bitcast(F32), t["kT_hi"][:, cols]).then_inc(k_in[ch].sem, 16)
                    sp.dma_start(kT_lo[:, ch, :].bitcast(F32), t["kT_lo"][:, cols]).then_inc(k_in[ch].sem, 16)

                def load_v(b, ch):
                    src, at = Blk(b, ch, B, NB), slice(ch * TILES, (ch + 1) * TILES)
                    sp.dma_start(v_hi[:, at, :].bitcast(F32), rows(t["v_hi"], src, D)).then_inc(v_in[ch].sem, 16)
                    sp.dma_start(v_lo[:, at, :].bitcast(F32), rows(t["v_lo"], src, D)).then_inc(v_in[ch].sem, 16)

                def load_q(blk):
                    cols = bass.ds(value(place(blk).s * BLOCK), BLOCK)
                    sp.dma_start(qT_hi[:, blk.par, :].bitcast(F32), t["qT_hi"][:, cols]).then_inc(q_in[blk.par].sem, 16)
                    sp.dma_start(qT_lo[:, blk.par, :].bitcast(F32), t["qT_lo"][:, cols]).then_inc(q_in[blk.par].sem, 16)

                def load_x1(blk):
                    sp.wait_ge(stored[blk.par].sem, stored[blk.par].at(blk.turn - 1))
                    settle(sp, paces)
                    sp.dma_start(x1[:, blk.par, :, :], rows(t["x1"], place(blk), C)).then_inc(x1_in[blk.par].sem, 16)
                    sp.dma_start(route[:, blk.par, :, :], rows(t["route"], place(blk), E)).then_inc(x1_in[blk.par].sem, 16)

                load_q(first)
                for ch in reversed(range(NB)):
                    load_k(0, ch)
                load_q(first.plus(1))
                for ch in range(NB):
                    load_v(0, ch)
                load_x1(first)

                def body(blk):
                    nxt, after = blk.plus(1), blk.plus(2)
                    more = not (isinstance(blk.b, int) and blk.b == B - 1)
                    ch = NB - 1 - blk.j
                    if more:
                        sp.wait_ge(s_done.sem, s_done.at(blk))
                        settle(sp, paces)
                        load_k(blk.b + 1, ch)
                    if after is not None:
                        sp.wait_ge(s_done.sem, s_done.at(blk))
                        settle(sp, paces)
                        load_q(after)
                    if nxt is not None:
                        load_x1(nxt)
                    if more:
                        sp.wait_ge(pv_done.sem, pv_done.at(blk))
                        settle(sp, paces)
                        load_v(blk.b + 1, ch)
                    sp.wait_ge(summed.sem, summed.at(blk.s))
                    settle(sp, paces)
                    sp.wait_ge(added.sem, added.at(blk.s))
                    settle(sp, paces)
                    sp.dma_start(rows(t["out2d"], place(blk), C), x1[:, blk.par, :, :]).then_inc(stored[blk.par].sem, 16)

                loop_blocks(sp, B, NB, body)
                for g in stored:
                    sp.wait_ge(g.sem, g.at(B * NB // 2 - 1))
                    settle(sp, paces)

            @block.gpsimd
            def _(pool):
                pool.memset(causal[:, :], 0.0).then_inc(setup, 1)
                pool.wait_ge(setup, 1)
                pool.affine_select(out=causal[:, :], in_=causal[:, :], compare_op=ALU.is_ge, fill=MASKED, base=0,
                                   pattern=[[-1, P]], channel_multiplier=1).then_inc(setup, 1)

                added.grant(pool)

                def body(blk):
                    p = blk.par
                    pool.wait_ge(rsum_ready.sem, rsum_ready.at(blk.s))
                    pool.tensor_tensor(rsum[:, 1, :], rsum[:, 0, :], t["minus_one"][:, 0:TILES], ALU.pow).then_inc(rinv_ready.sem, 1)
                    pool.wait_ge(rinv_ready.sem, rinv_ready.at(blk.s))
                    pool.wait_ge(x1_in[p].sem, x1_in[p].at(blk.turn))
                    pool.wait_ge(summed.sem, summed.at(blk.s - 1))
                    pool.tensor_tensor(weight[:, p, :, :], route[:, p, :, :],
                                       rsum[:, 1, :].unsqueeze(2).to_broadcast([P, TILES, E]), ALU.mult).then_inc(weight_ready.sem, 1)
                    for q in range(OUTS):
                        i = tile_group(q // 2 * 2 + 1)[0]
                        pool.wait_ge(scaled.sem, scaled.at(blk.s, q + 1))
                        pool.wait_ge(added.sem, added.at(blk.s, q))
                        pool.tensor_tensor(x1[:, p, i, :], x1[:, p, i, :], term[:, q % 4, :], ALU.add).then_inc(added.sem, 1)

                loop_blocks(pool, B, NB, body)

            @block.scalar
            def _(act):
                exp_done.grant(act)
                scaled.grant(act)

                def exponentials(blk, k):
                    n = chunks(blk)
                    i, ch = k // n, n - 1 - k % n
                    width = (i + 1) * P if ch == n - 1 else BLOCK
                    if k % n == 0:
                        act.wait_ge(nmax_ready.sem, nmax_ready.at(blk.s, i + 1))
                    if k == 0 and not (isinstance(blk.s, int) and blk.s < 2):
                        act.wait_ge(p_transposed.sem, p_transposed.at(blk.plus(-2)))
                    act.activation(probs[:, blk.par, i, ch * BLOCK:ch * BLOCK + width], S[k % 4][:, 0:width], ACT.Exp,
                                   bias=nmax[:, i:i + 1], scale=SCALE,
                                   accum_out=csum[:, blk.par, i, ch:ch + 1]).then_inc(exp_done.sem, 1)

                def project(blk, r):
                    i, g = tile_group(r)
                    act.wait_ge(out_done.sem, out_done.at(blk.s, r + 1))
                    if r == 1:
                        act.wait_ge(weight_ready.sem, weight_ready.at(blk.s))
                    for e in range(2):
                        q = r - 1 + e
                        act.wait_ge(added.sem, added.at(blk.s, q - 3))
                        act.activation(term[:, q % 4, :], OUT_BANKS[r % 4][:, e * C:(e + 1) * C], ACT.Copy,
                                       scale=weight[:, blk.par, i, 2 * g + e:2 * g + e + 1]).then_inc(scaled.sem, 1)

                for k in range(counts[0]):
                    exponentials(first, k)

                def body(blk):
                    nxt = blk.plus(1)
                    for what, k in events_act(blk, nxt):
                        if what == "X":
                            exponentials(nxt, k)
                        if what == "O" and k % 2 == 1:
                            project(blk, k)
                        if what == "T":
                            lo = max(0, k - (counts[blk.j] - TILES)) * P
                            act.wait_ge(p_transposed.sem, p_transposed.at(blk, k + 1))
                            act.wait_ge(pv_done.sem, pv_done.at(blk, max(0, k - 2)))
                            act.activation(pT_hi[:, k % 3, lo:], T_BANKS[k % 3][:, lo:], ACT.Copy).then_inc(p_hi.sem, 1)
                        if what == "V" and k == counts[blk.j] - 1:
                            act.wait_ge(pv_done.sem, pv_done.at(blk))
                            act.activation(oT_hi[:, :], Y[0][:, :], ACT.Copy).then_inc(o_hi.sem, 1)

                loop_blocks(act, B, NB, body)

            @block.vector
            def _(dve):
                p_lo.grant(dve)
                summed.grant(dve)

                def scores(blk, k):
                    n = chunks(blk)
                    i, ch = k // n, n - 1 - k % n
                    width = (i + 1) * P if ch == n - 1 else BLOCK
                    dve.wait_ge(s_done.sem, s_done.at(blk, k + 1))
                    if ch == n - 1:
                        dve.tensor_tensor(S[k % 4][:, i * P:(i + 1) * P], S[k % 4][:, i * P:(i + 1) * P], causal[:, :],
                                          ALU.add).then_inc(causal_done.sem, 1)
                        dve.wait_ge(causal_done.sem, causal_done.at(blk.s, i + 1))
                    dve.tensor_reduce(cmax[:, i, ch:ch + 1], S[k % 4][:, 0:width], AX_X, ALU.max).then_inc(cmax_ready.sem, 1)
                    if ch == 0:
                        dve.wait_ge(cmax_ready.sem, cmax_ready.at(blk, k + 1))
                        dve.tensor_reduce(tmax[:, i:i + 1], cmax[:, i, 0:n], AX_X, ALU.max).then_inc(tmax_ready.sem, 1)
                        dve.wait_ge(tmax_ready.sem, tmax_ready.at(blk.s, i + 1))
                        if not (isinstance(blk.s, int) and blk.s == 0):
                            dve.wait_ge(exp_done.sem, exp_done.at(blk, (i - 3) * n if i < 3 else 0))
                        dve.tensor_scalar(nmax[:, i:i + 1], tmax[:, i:i + 1], -SCALE, None, ALU.mult).then_inc(nmax_ready.sem, 1)

                def row_sums(blk):
                    dve.wait_ge(exp_done.sem, exp_done.at(blk))
                    dve.tensor_reduce(rsum[:, 0, :], csum[:, blk.par, :, 0:chunks(blk)], AX_X, ALU.add).then_inc(rsum_ready.sem, 1)

                def project(blk, r):
                    i, g = tile_group(r)
                    dve.wait_ge(out_done.sem, out_done.at(blk.s, r + 1))
                    if r == 0:
                        dve.wait_ge(weight_ready.sem, weight_ready.at(blk.s))
                    acc = x1[:, blk.par, i, :]
                    for e in range(2):
                        dve.wait_ge(summed.sem, summed.at(blk.s, r + e))
                        dve.scalar_tensor_tensor(out=acc, in0=OUT_BANKS[r % 4][:, e * C:(e + 1) * C],
                                                 scalar=weight[:, blk.par, i, 2 * g + e:2 * g + e + 1],
                                                 in1=acc, op0=ALU.mult, op1=ALU.add).then_inc(summed.sem, 1)

                dve.wait_ge(setup, 2)
                for k in range(counts[0]):
                    scores(first, k)

                def body(blk):
                    nxt = blk.plus(1)
                    row_sums(blk)
                    for what, k in events(blk, nxt):
                        if what == "S":
                            scores(nxt, k)
                        if what == "T":
                            lo = max(0, k - (counts[blk.j] - TILES)) * P
                            dve.wait_ge(p_hi.sem, p_hi.at(blk, k + 1))
                            dve.tensor_tensor(pT_lo[:, k % 3, lo:], T_BANKS[k % 3][:, lo:], pT_hi[:, k % 3, lo:].bitcast(F32),
                                              ALU.subtract).then_inc(p_lo.sem, 1)
                        if what == "V" and k == counts[blk.j] - 1:
                            dve.wait_ge(o_hi.sem, o_hi.at(blk.s))
                            dve.tensor_tensor(oT_lo[:, :], Y[0][:, :], oT_hi[:, :].bitcast(F32), ALU.subtract).then_inc(o_lo.sem, 1)
                        if what == "O" and k % 2 == 0:
                            project(blk, k)

                loop_blocks(dve, B, NB, body)

            @block.tensor
            def _(pe):
                p_transposed.grant(pe)
                pv_done.grant(pe)
                out_done.grant(pe)
                ident = t["ident"]

                def scores(blk, k):
                    n = chunks(blk)
                    i, ch = k // n, n - 1 - k % n
                    width = max(2 * P, (i + 1) * P) if ch == n - 1 else BLOCK
                    if k == 0:
                        pe.wait_ge(q_in[blk.par].sem, q_in[blk.par].at(blk.turn))
                    if i == 0:
                        pe.wait_ge(k_in[ch].sem, k_in[ch].at(blk.b))
                    pe.wait_ge(exp_done.sem, exp_done.at(blk, k - 3))
                    cols = slice(i * P, (i + 1) * P)
                    product(pe, S[k % 4][:, 0:width],
                            [((qT_hi[:, blk.par, cols], qT_lo[:, blk.par, cols]),
                              (kT_hi[:, ch, 0:width], kT_lo[:, ch, 0:width]))]).then_inc(s_done.sem, 1)

                def transpose(blk, u):
                    first_tile = max(0, u - (counts[blk.j] - TILES))
                    if u == 0:
                        pe.wait_ge(exp_done.sem, exp_done.at(blk))
                        pe.wait_ge(scaled.sem, scaled.at(blk.s - 1, OUTS - 2))
                    if u == 1:
                        pe.wait_ge(summed.sem, summed.at(blk.s - 1))
                    pe.wait_ge(p_lo.sem, p_lo.at(blk, max(0, u - 2)))
                    for i in range(first_tile, TILES):
                        last = pe.transpose(T_BANKS[u % 3][:, i * P:(i + 1) * P], probs[:, blk.par, i, u * P:(u + 1) * P], ident[:, :])
                    last.then_inc(p_transposed.sem, 1)

                def values(blk, u):
                    lo = max(0, u - (counts[blk.j] - TILES)) * P
                    if u % TILES == 0:
                        pe.wait_ge(v_in[u // TILES].sem, v_in[u // TILES].at(blk.b))
                    if u == 0:
                        pe.wait_ge(scaled.sem, scaled.at(blk.s - 1))
                    pe.wait_ge(p_lo.sem, p_lo.at(blk, u + 1))
                    product(pe, Y[0][:, lo:], [((v_hi[:, u, :], v_lo[:, u, :]), (pT_hi[:, u % 3, lo:], pT_lo[:, u % 3, lo:]))],
                            begin=(u == 0), end=(u == counts[blk.j] - 1)).then_inc(pv_done.sem, 1)

                def project(blk, r):
                    i, g = tile_group(r)
                    if r == 0:
                        pe.wait_ge(o_lo.sem, o_lo.at(blk.s))
                    if r >= 4 and r % 2 == 0:
                        pe.wait_ge(summed.sem, summed.at(blk.s, r - 2))
                    if r >= 4 and r % 2 == 1:
                        pe.wait_ge(scaled.sem, scaled.at(blk.s, r - 3))
                    w = slice(g * BLOCK, (g + 1) * BLOCK)
                    cols = slice(i * P, (i + 1) * P)
                    product(pe, OUT_BANKS[r % 4][:, :], [((oT_hi[:, cols], oT_lo[:, cols]), (t["wo_hi"][:, w], t["wo_lo"][:, w]))])\
                        .then_inc(out_done.sem, 1)

                for k in range(counts[0]):
                    scores(first, k)

                def body(blk):
                    nxt = blk.plus(1)
                    for what, k in events(blk, nxt):
                        if what == "S":
                            scores(nxt, k)
                        if what == "T":
                            transpose(blk, k)
                        if what == "V":
                            values(blk, k)
                        if what == "O":
                            project(blk, k)

                loop_blocks(pe, B, NB, body)


def dims():
    return dict(B=4, NB=4, C=256, E=8, D=128, WCOLS=2 * 8 * 384 + 8 * 256)


def build(nc, A, out, upto=3):
    d = dims()
    N, C = d["B"] * d["NB"] * BLOCK, d["C"]

    def scratch(name, shape):
        return nc.dram_tensor(name, shape, F32, kind="Internal").ap()

    with ExitStack() as st:
        c = Ctx(nc, st, "")
        t = dict(x2d=A["x"].rearrange("b l c -> (b l) c"), out2d=out.rearrange("b l c -> (b l) c"), **A)
        for name, cols in (("feat", C), ("base", C), ("x1", C)):
            t[name] = scratch("s_" + name, [N, C])
        for name, cols in (("ks", C), ("g_hi", 2 * C), ("g_lo", 2 * C), ("gw_hi", 4 * C), ("gw_lo", 4 * C)):
            t[name] = scratch("s_" + name, [d["B"] * P, cols])
        for name in ("qT_hi", "qT_lo", "kT_hi", "kT_lo"):
            t[name] = scratch("s_" + name, [P, N])
        for name in ("v_hi", "v_lo"):
            t[name] = scratch("s_" + name, [N, P])
        t["route"] = scratch("s_route", [N, 8])
        t["ident"] = c.sb("ident", [P, P])
        t["minus_half"] = c.sb("minus_half", [P, 32])
        t["half"] = c.sb("half", [P, 32])
        t["minus_one"] = c.sb("minus_one", [P, 32])
        t["sig"] = c.sb("sig", [P, 8])
        t["wo_hi"] = c.sb("wo_hi", [P, d["E"] * C], F32R)
        t["wo_lo"] = c.sb("wo_lo", [P, d["E"] * C], F32R)
        with ExitStack() as until_attention:
            c = Ctx(nc, until_attention, "")
            t["sn_hi"] = c.sb("sn_hi", [P, 2, C], F32R)
            t["sn_lo"] = c.sb("sn_lo", [P, 2, C], F32R)
            t["w2_hi"] = c.sb("w2_hi", [P, 4, C], F32R)
            t["w2_lo"] = c.sb("w2_lo", [P, 4, C], F32R)
            t["wqkv_hi"] = c.sb("wqkv_hi", [P, 6 * d["E"] * d["D"]], F32R)
            t["wqkv_lo"] = c.sb("wqkv_lo", [P, 6 * d["E"] * d["D"]], F32R)
            stage1(nc, t, d)
            if upto >= 2:
                stage2(nc, t, d)
        if upto >= 3:
            stage3(nc, t, d)


_INS = {"x": "L0_attn_x", "Wq": "L0_attn_Wq", "Wm": "L0_attn_Wm", "W1": "L0_attn_W1", "W2": "L0_attn_W2",
        "g1": "L0_attn_g1", "b1": "L0_attn_b1", "g2": "L0_attn_g2", "b2": "L0_attn_b2",
        "sim": "L0_ffn_sim_matrix", "gates": "L0_ffn_gates", "Wqe": "L0_ffn_q_proj", "Wke": "L0_ffn_k_proj",
        "Wve": "L0_ffn_v_proj", "Woe": "L0_ffn_o_proj"}


def kernel(**inputs):
    import numpy as np
    import concourse.bacc as bacc
    from concourse.bass_utils import run_bass_kernel_spmd

    nc = bacc.Bacc("TRN2", target_bir_lowering=False, num_devices=1)
    arrays, handles = {}, {}
    for short, name in _INS.items():
        arrays["in_" + name] = np.ascontiguousarray(inputs[name])
        handles[short] = nc.dram_tensor("in_" + name, arrays["in_" + name].shape, F32, kind="ExternalInput").ap()
    out = nc.dram_tensor("out", arrays["in_L0_attn_x"].shape, F32, kind="ExternalOutput").ap()
    build(nc, handles, out)
    r = run_bass_kernel_spmd(nc, [arrays], core_ids=[0])
    return r.results[0]["out"]
```

```python
from contextlib import ExitStack

import concourse.bass as bass
from concourse import mybir

ALU = mybir.AluOpType
ACT = mybir.ActivationFunctionType
F32 = mybir.dt.float32
F32R = mybir.dt.float32r
AX_X = mybir.AxisListType.X

P = 128
TILES = 4
BLOCK = P * TILES
LN_EPS = 1e-5
ATTN_EPS = 1e-6
NORM_EPS = 1e-12
MASKED = -3.0e38


class Affine:

    def __init__(self, register, mul=1, off=0):
        self.register, self.mul, self.off = register, mul, off

    def __add__(self, k):
        return Affine(self.register, self.mul, self.off + k)

    def __sub__(self, k):
        return self + -k

    def __mul__(self, k):
        return Affine(self.register, self.mul * k, self.off * k)


def value(n):
    return n.register * n.mul + n.off if isinstance(n, Affine) else n


class Blk:

    def __init__(self, b, j, batches, per_batch):
        self.b, self.j, self.batches, self.per_batch = b, j, batches, per_batch

    @property
    def s(self):
        return self.b * self.per_batch + self.j

    @property
    def par(self):
        return self.j % 2

    @property
    def turn(self):
        return self.b * (self.per_batch // 2) + self.j // 2

    def plus(self, k):
        j = self.j + k
        b = self.b + j // self.per_batch if not 0 <= j < self.per_batch else self.b
        if isinstance(b, int) and b >= self.batches:
            return None
        return Blk(b, j % self.per_batch, self.batches, self.per_batch)


class Flag:

    def __init__(self, sem, per, ahead=0):
        self.sem, self.per, self.ahead = sem, per, ahead

    def at(self, n, k=None):
        return value((n + self.ahead) * self.per + (self.per if k is None else k))

    def grant(self, eng):
        eng.sem_inc(self.sem, self.ahead * self.per)


def settle(eng, paces):
    eng.sem_inc(paces[eng.engine])


def loop_blocks(eng, batches, per_batch, body):
    with eng.Fori(0, batches - 1, 1) as b:
        for j in range(per_batch):
            own = Affine(eng.snap(b + (j + 1)), 1, -(j + 1))
            body(Blk(own, j, batches, per_batch))
    for j in range(per_batch):
        body(Blk(batches - 1, j, batches, per_batch))


class Ctx:

    def __init__(self, nc, stack, prefix):
        self.nc, self.stack, self.prefix = nc, stack, prefix

    def sb(self, name, shape, dt=F32):
        return self.stack.enter_context(self.nc.sbuf_tensor(self.prefix + name, shape, dt))

    def ps(self, name, shape, dt=F32):
        return self.stack.enter_context(self.nc.psum_tensor(self.prefix + name, shape, dt))

    def sem(self, name):
        return self.stack.enter_context(self.nc.semaphore(self.prefix + name))

    def flag(self, name, per, ahead=0):
        return Flag(self.sem(name), per, ahead)


def rows(dram, blk, width):
    return dram[bass.ds(value(blk.s * BLOCK), BLOCK), :].rearrange("(t p) c -> p t c", p=P)


def fold_matrices(ap, C):
    return [ap[:, a * C:b * C].rearrange("p (h n) -> p h n", h=2) for a, b in ((0, 2), (2, 4), (4, 8), (8, 12))]


def product(eng, out, pairs, begin=True, end=True):
    n = 3 * len(pairs)
    i = 0
    for (ah, al), (bh, bl) in pairs:
        for a, b in ((ah, bl), (ah, bh), (al, bh)):
            last = eng.matmul(out, a, b, start=(begin and i == 0), stop=(end and i == n - 1))
            i += 1
    return last


def stage1(nc, t, d, scaled):
    B, NB, C = d["B"], d["NB"], d["C"]
    E, D = d["E"], d["D"]
    W3 = 3 * D
    with ExitStack() as st:
        c = Ctx(nc, st, "a_")
        x = c.sb("x", [P, 2, TILES, C])
        h = c.sb("h", [P, 2, TILES, C])
        base = c.sb("base", [P, 2, TILES, C])
        stats = c.sb("stats", [P, 2, TILES, 6])
        mv = c.sb("mv", [P, 2, TILES, 2])
        ve = c.sb("ve", [P, 2, TILES])
        rstd = c.sb("rstd", [P, 2, TILES])
        rstd1 = c.sb("rstd1", [P, 2, TILES])
        negmu = c.sb("negmu", [P, 2, TILES])
        negmur = c.sb("negmur", [P, 2, TILES])
        hT_hi = c.sb("hT_hi", [P, 2, BLOCK], F32R)
        hT_lo = c.sb("hT_lo", [P, 2, BLOCK], F32R)
        negpart = c.sb("negpart", [P, 2, 2, C])
        expneg = c.sb("expneg", [P, 2, 2, C])
        q = c.sb("q", [P, 2, TILES, C])
        feat = c.sb("feat", [P, 2, TILES, C])
        fsum = c.sb("fsum", [P, TILES, C])
        wq_raw = c.sb("wq_raw", [P, 2, C])
        wq_hi = c.sb("wq_hi", [P, 2, C], F32R)
        wq_lo = c.sb("wq_lo", [P, 2, C], F32R)
        wm = c.sb("wm", [P, 2, C])
        w1 = c.sb("w1", [P, 2, 2 * C])
        w2_raw = c.sb("w2_raw", [P, 4, C])
        w_raw = c.sb("w_raw", [P, 2, W3 + P])
        ones = c.sb("ones", [P, P])
        headmask = c.sb("headmask", [P, P])
        kvT = c.sb("kvT", [P, 2, P])
        gT = c.sb("gT", [P, 2, C])
        fold_st = c.sb("fold_st", [P, 13 * C], F32R)
        ks_st = fold_st[:, 0:C].bitcast(F32)
        g_st_hi, g_st_lo, gw_st_hi, gw_st_lo = fold_matrices(fold_st[:, C:], C)
        sim = c.sb("sim", [P, 2, 8])
        simsq = c.sb("simsq", [P, 2, 8])
        simn = c.sb("simn", [P, 3, 8])
        sn = c.sb("sn", [P, 2, 8])
        gates = c.sb("gates", [P, 2, 8])

        trp = [c.ps(f"trp{i}", [P, BLOCK]) for i in range(2)]
        qp = [c.ps(f"qp{i}", [P, 2, C]) for i in range(2)]
        kvp = [c.ps(f"kvp{i}", [P, 2, C]) for i in range(2)]
        misc = [c.ps(f"misc{i}", [P, 2 * C]) for i in range(2)]

        w_in = c.sem("w_in")
        small_in = c.sem("small_in")
        raw_in = [c.flag(f"raw_in{i}", 16 * 4) for i in range(2)]
        x_in = [c.flag(f"x_in{i}", 16) for i in range(2)]
        consts = c.sem("consts")
        wq_split = c.sem("wq_split")
        w2_split = c.sem("w2_split")
        sim_squared = c.sem("sim_squared")
        w_split = c.flag("w_split", 2, ahead=1)
        w_high = c.flag("w_high", 2)
        gate_pool = c.sem("gate_pool")
        gate_act = c.sem("gate_act")
        gate_pe = c.sem("gate_pe")
        gate_dve = c.sem("gate_dve")
        st_ready = c.flag("st_ready", TILES)
        mv_ready = c.flag("mv_ready", TILES)
        pool_small = c.flag("pool_small", 5)
        h_ready = c.flag("h_ready", TILES)
        base_ready = c.flag("base_ready", TILES)
        base_out = [c.flag(f"base_out{i}", 16) for i in range(2)]
        transposed = c.flag("transposed", 2)
        hi_ready = c.flag("hi_ready", 2)
        lo_ready = c.flag("lo_ready", 2)
        q_done = c.flag("q_done", 2)
        neg_ready = c.flag("neg_ready", 2)
        q_copied = c.flag("q_copied", 2)
        exp_ready = c.flag("exp_ready", 2)
        feat_ready = c.flag("feat_ready", 2)
        feat_out = [c.flag(f"feat_out{i}", 16, ahead=1) for i in range(2)]
        summed = c.flag("summed", 1, ahead=1)
        kv_read = c.flag("kv_read", 1)
        kv_masked = c.flag("kv_masked", 2)
        ks_done = c.flag("ks_done", 1, ahead=1)
        ks_copied = c.flag("ks_copied", 1)
        g_done = c.flag("g_done", 1)
        gT_done = c.flag("gT_done", 1)
        gT_copied = c.flag("gT_copied", 1)
        gw_done = c.flag("gw_done", 2)
        fold_hi = c.flag("fold_hi", 3)
        fold_lo = c.flag("fold_lo", 3, ahead=1)
        fold_out = c.flag("fold_out", 16, ahead=1)

        x2d, feat2d, base2d = t["x2d"], t["feat"], t["base"]
        first = Blk(0, 0, B, NB)

        def weight_parts(blk):
            p = blk.par
            qkv = bass.ds(value(blk.turn * W3 + p * E * W3), W3)
            o = bass.ds(value(blk.turn * 2 * P + p * P), P)
            return ((w_raw[:, p, 0:W3], t["wqkv_hi"][:, qkv], t["wqkv_lo"][:, qkv]),
                    (w_raw[:, p, W3:], t["wo_hi"][:, o], t["wo_lo"][:, o]))

        def prepares(blk, j):
            return isinstance(blk.b, int) and blk.b == B - 1 and blk.j == j

        paces = {e.engine: c.sem(f"pace_{k}") for k, e in enumerate((nc.sync, nc.gpsimd, nc.vector, nc.scalar))}

        with nc.Block() as block:

            @block.sync
            def _(sp):
                for g in feat_out:
                    g.grant(sp)
                fold_out.grant(sp)
                sp.dma_start(wq_raw[:, :, :], t["Wq"].rearrange("(h p) n -> p h n", p=P)).then_inc(w_in, 16)
                for k in (0, 1):
                    blk = first.plus(k)
                    sp.dma_start(x[:, blk.par, :, :], rows(x2d, blk, C)).then_inc(x_in[blk.par].sem, 16)
                sp.dma_start(sim[:, :, :], t["sim"].rearrange("(h p) n -> p h n", p=P)).then_inc(small_in, 16)
                sp.dma_start(gates[:, 0, :], t["gates"].partition_broadcast(P)).then_inc(small_in, 16)
                sp.dma_start(wm[:, :, :], t["Wm"].rearrange("(h p) n -> p h n", p=P)).then_inc(small_in, 16)
                sp.dma_start(w1[:, :, :], t["W1"].rearrange("(h p) n -> p h n", p=P)).then_inc(small_in, 16)
                sp.dma_start(w2_raw[:, :, :], t["W2"].rearrange("(h p) n -> p h n", p=P)).then_inc(small_in, 16)

                def load_weights(blk):
                    if not (isinstance(blk.s, int) and blk.s == 0):
                        sp.wait_ge(w_split.sem, w_split.at(blk.s - 2))
                        settle(sp, paces)
                    for k, name in enumerate(("Wqe", "Wke", "Wve")):
                        part = t[name].rearrange("e c n -> (e c) n")[bass.ds(value(blk.s * P), P), :]
                        sp.dma_start(w_raw[:, blk.par, k * D:(k + 1) * D], part).then_inc(raw_in[blk.par].sem, 16)
                    part = t["Woe"].rearrange("e p n -> (e p) n")[bass.ds(value(blk.turn * P), P), blk.par * P:(blk.par + 1) * P]
                    sp.dma_start(w_raw[:, blk.par, W3:], part).then_inc(raw_in[blk.par].sem, 16)

                def load_x(blk):
                    before = blk.plus(-2)
                    sp.wait_ge(h_ready.sem, h_ready.at(before.s))
                    settle(sp, paces)
                    sp.wait_ge(base_ready.sem, base_ready.at(before.s))
                    settle(sp, paces)
                    sp.dma_start(x[:, blk.par, :, :], rows(x2d, blk, C)).then_inc(x_in[blk.par].sem, 16)

                def store_base(blk):
                    sp.wait_ge(base_ready.sem, base_ready.at(blk.s))
                    settle(sp, paces)
                    sp.dma_start(rows(base2d, blk, C), base[:, blk.par, :, :]).then_inc(base_out[blk.par].sem, 16)

                def store_feat(blk):
                    sp.wait_ge(feat_ready.sem, feat_ready.at(blk.s))
                    settle(sp, paces)
                    sp.dma_start(rows(feat2d, blk, C), feat[:, blk.par, :, :]).then_inc(feat_out[blk.par].sem, 16)

                for k in (0, 1):
                    load_x(first.plus(k + 2))
                    store_base(first.plus(k))
                load_weights(first)
                store_feat(first)
                store_feat(first.plus(1))

                def body(blk):
                    if blk.plus(4) is not None:
                        load_x(blk.plus(4))
                    if prepares(blk, 0):
                        for k in range(2):
                            sp.wait_ge(feat_out[k].sem, feat_out[k].at(first.turn))
                            settle(sp, paces)
                        sp.wait_ge(fold_out.sem, fold_out.at(first.b))
                        settle(sp, paces)
                        scaled.load_ksum(sp, first.b)
                        scaled.load_feat(sp, first)
                        scaled.load_feat(sp, first.plus(1))
                        scaled.load_fold(sp, first.b)
                    if blk.plus(2) is not None:
                        store_base(blk.plus(2))
                    if blk.plus(1) is not None:
                        load_weights(blk.plus(1))
                    if blk.plus(2) is not None:
                        store_feat(blk.plus(2))

                loop_blocks(sp, B, NB, body)
                turns = B * NB // 2
                for par in range(2):
                    sp.wait_ge(base_out[par].sem, base_out[par].at(turns - 1))
                    sp.wait_ge(feat_out[par].sem, feat_out[par].at(turns - 1))
                sp.wait_ge(fold_out.sem, fold_out.at(B - 1))
                settle(sp, paces)

            @block.gpsimd
            def _(pool):
                summed.grant(pool)
                w_split.grant(pool)
                pool.memset(t["ident"][:, :], 0.0).then_inc(consts, 1)
                pool.memset(ones[:, :], 1.0).then_inc(consts, 1)
                pool.memset(t["minus_half"][:, :], -0.5).then_inc(consts, 1)
                pool.memset(t["half"][:, :], 0.5).then_inc(consts, 1)
                pool.memset(t["minus_one"][:, :], -1.0).then_inc(consts, 1)
                pool.memset(headmask[:, :], 0.0).then_inc(consts, 1)
                pool.wait_ge(consts, 6)
                pool.affine_select(out=t["ident"][:, :], in_=t["ident"][:, :], compare_op=ALU.not_equal, fill=1.0,
                                   base=0, pattern=[[-1, P]], channel_multiplier=1).then_inc(consts, 1)
                for k in range(4):
                    pool.wait_ge(consts, 7 + k)
                    pool.memset(headmask[32 * k:32 * k + 32, 32 * k:32 * k + 32], 1.0).then_inc(consts, 1)

                def row_scales(blk):
                    p = blk.par
                    if not (isinstance(blk.s, int) and blk.s < 2):
                        pool.wait_ge(h_ready.sem, h_ready.at(blk.s - 2))
                        pool.wait_ge(base_ready.sem, base_ready.at(blk.s - 2))
                    pool.wait_ge(mv_ready.sem, mv_ready.at(blk.s))
                    settle(pool, paces)
                    pool.tensor_scalar(ve[:, p, :], mv[:, p, :, 1], LN_EPS, None, ALU.add).then_inc(pool_small.sem, 1)
                    pool.tensor_scalar(negmu[:, p, :], mv[:, p, :, 0], -1.0, None, ALU.mult).then_inc(pool_small.sem, 1)
                    pool.wait_ge(pool_small.sem, pool_small.at(blk.s, 1))
                    pool.tensor_tensor(rstd[:, p, :], ve[:, p, :], t["minus_half"][:, 0:TILES], ALU.pow).then_inc(pool_small.sem, 1)
                    pool.wait_ge(pool_small.sem, pool_small.at(blk.s, 3))
                    settle(pool, paces)
                    pool.tensor_scalar(rstd1[:, p, :], rstd[:, p, :], 1.0, None, ALU.add).then_inc(pool_small.sem, 1)
                    pool.tensor_tensor(negmur[:, p, :], negmu[:, p, :], rstd[:, p, :], ALU.mult).then_inc(pool_small.sem, 1)

                pool.wait_ge(consts, 11)
                row_scales(first)
                row_scales(first.plus(1))

                pool.wait_ge(gate_dve, 1)
                pool.tensor_tensor(simn[:, 1, :], simn[:, 0, :], t["half"][:, 0:8], ALU.pow).then_inc(gate_pool, 1)
                pool.wait_ge(gate_pool, 1)
                pool.tensor_scalar(simn[:, 0, :], simn[:, 1, :], NORM_EPS, None, ALU.max).then_inc(gate_pool, 1)
                pool.wait_ge(gate_pool, 2)
                pool.tensor_tensor(simn[:, 2, :], simn[:, 0, :], t["minus_one"][:, 0:8], ALU.pow).then_inc(gate_pool, 1)
                pool.wait_ge(gate_act, 1)
                pool.tensor_scalar(gates[:, 0, :], gates[:, 1, :], 1.0, None, ALU.add).then_inc(gate_pool, 1)
                pool.wait_ge(gate_pool, 4)
                pool.tensor_tensor(t["sig"][:, :], gates[:, 0, :], t["minus_one"][:, 0:8], ALU.pow).then_inc(gate_pool, 1)
                row_scales(first.plus(2))

                def body(blk):
                    pool.wait_ge(feat_ready.sem, feat_ready.at(blk.s))
                    if blk.j == 0:
                        pool.wait_ge(ks_done.sem, ks_done.at(blk.b - 1))
                        settle(pool, paces)
                        pool.tensor_copy(fsum[:, :, :], feat[:, blk.par, :, :]).then_inc(summed.sem, 1)
                    else:
                        pool.wait_ge(summed.sem, summed.at(blk.s - 1))
                        pool.tensor_tensor(fsum[:, :, :], fsum[:, :, :], feat[:, blk.par, :, :], ALU.add).then_inc(summed.sem, 1)
                    if blk.plus(3) is not None:
                        row_scales(blk.plus(3))
                    for k, (raw, hi, lo) in enumerate(weight_parts(blk)):
                        pool.wait_ge(w_high.sem, w_high.at(blk.s, k + 1))
                        pool.tensor_tensor(lo, raw, hi.bitcast(F32), ALU.subtract).then_inc(w_split.sem, 1)
                    if prepares(blk, 1):
                        scaled.ksum_product(pool, first)
                    if prepares(blk, 3):
                        scaled.normalise(pool, first)

                loop_blocks(pool, B, NB, body)

            @block.vector
            def _(dve):
                fold_lo.grant(dve)
                dve.wait_ge(w_in, 16)
                dve.tensor_copy(wq_hi[:, :, :], wq_raw[:, :, :]).then_inc(wq_split, 1)
                dve.wait_ge(wq_split, 1)
                dve.tensor_tensor(wq_lo[:, :, :], wq_raw[:, :, :], wq_hi[:, :, :].bitcast(F32), ALU.subtract).then_inc(wq_split, 1)

                def moments(blk):
                    p = blk.par
                    dve.wait_ge(x_in[p].sem, x_in[p].at(blk.turn))
                    for i in range(TILES):
                        dve.bn_stats(stats[:, p, i, :], x[:, p, i, :]).then_inc(st_ready.sem, 1)
                    dve.wait_ge(st_ready.sem, st_ready.at(blk.s))
                    settle(dve, paces)
                    for i in range(TILES):
                        dve.bn_aggr(mv[:, p, i, :], stats[:, p, i, :]).then_inc(mv_ready.sem, 1)

                def normalise(blk):
                    p = blk.par
                    dve.wait_ge(pool_small.sem, pool_small.at(blk.s))
                    if not (isinstance(blk.s, int) and blk.s < 2):
                        dve.wait_ge(transposed.sem, transposed.at(blk.s - 2))
                    for i in range(TILES):
                        dve.tensor_scalar(h[:, p, i, :], x[:, p, i, :], mv[:, p, i, 0:1], rstd[:, p, i:i + 1],
                                          ALU.subtract, ALU.mult).then_inc(h_ready.sem, 1)

                def split_low(blk):
                    for half in range(2):
                        dve.wait_ge(hi_ready.sem, hi_ready.at(blk.s, half + 1))
                        dve.tensor_tensor(hT_lo[:, half, :], trp[half][:, :], hT_hi[:, half, :].bitcast(F32),
                                          ALU.subtract).then_inc(lo_ready.sem, 1)

                def features(blk):
                    if not (isinstance(blk.s, int) and blk.s < 2):
                        dve.wait_ge(feat_out[blk.par].sem, feat_out[blk.par].at(blk.turn - 1))
                        dve.wait_ge(summed.sem, summed.at(blk.s - 2))
                        dve.wait_ge(kv_read.sem, kv_read.at(blk.s - 2))
                    for bank in range(2):
                        dve.wait_ge(exp_ready.sem, exp_ready.at(blk.s, bank + 1))
                        dve.scalar_tensor_tensor(out=feat[:, blk.par, 2 * bank:2 * bank + 2, :],
                                                 in0=q[:, blk.par, 2 * bank:2 * bank + 2, :], scalar=0.0,
                                                 in1=expneg[:, bank, :, :], op0=ALU.max, op1=ALU.add).then_inc(feat_ready.sem, 1)

                moments(first)
                moments(first.plus(1))
                normalise(first)
                normalise(first.plus(1))
                dve.wait_ge(small_in, 16 * 5)
                dve.tensor_tensor(simsq[:, :, :], sim[:, :, :], sim[:, :, :], ALU.mult).then_inc(sim_squared, 1)
                dve.wait_ge(gate_pe, 1)
                dve.tensor_copy(simn[:, 0, :], misc[0][:, 0:8]).then_inc(gate_dve, 1)
                split_low(first)
                dve.wait_ge(gate_pool, 3)
                for half in range(2):
                    dve.tensor_tensor(sn[:, half, :], sim[:, half, :], simn[:, 2, :], ALU.mult).then_inc(gate_dve, 1)
                dve.wait_ge(gate_dve, 3)
                dve.tensor_copy(t["sn_hi"][:, :, :], sn[:, :, :]).then_inc(gate_dve, 1)
                dve.wait_ge(gate_dve, 4)
                dve.tensor_tensor(t["sn_lo"][:, :, :], sn[:, :, :], t["sn_hi"][:, :, :].bitcast(F32), ALU.subtract).then_inc(gate_dve, 1)
                dve.tensor_copy(t["w2_hi"][:, :, :], w2_raw[:, :, :]).then_inc(w2_split, 1)
                dve.wait_ge(w2_split, 1)
                dve.tensor_tensor(t["w2_lo"][:, :, :], w2_raw[:, :, :], t["w2_hi"][:, :, :].bitcast(F32), ALU.subtract).then_inc(w2_split, 1)
                features(first)
                moments(first.plus(2))
                split_low(first.plus(1))
                normalise(first.plus(2))
                features(first.plus(1))

                def body(blk):
                    after, coming = blk.plus(2), blk.plus(3)
                    if after is not None:
                        split_low(after)
                    if coming is not None:
                        moments(coming)
                    if blk.j == NB - 1:
                        dve.wait_ge(kv_read.sem, kv_read.at(blk.s))
                        for half in range(2):
                            dve.tensor_tensor(kvT[:, half, :], kvp[half][:, 0, half * P:(half + 1) * P], headmask[:, :],
                                              ALU.mult).then_inc(kv_masked.sem, 1)
                    if coming is not None:
                        normalise(coming)
                    if blk.j == NB - 1:
                        dve.wait_ge(fold_out.sem, fold_out.at(blk.b - 1))
                        dve.wait_ge(fold_hi.sem, fold_hi.at(blk.b, 1))
                        dve.tensor_tensor(g_st_lo, misc[1][:, :].rearrange("p (h n) -> p h n", h=2), g_st_hi.bitcast(F32), ALU.subtract).then_inc(fold_lo.sem, 1)
                    if after is not None:
                        features(after)
                    if blk.j == NB - 1:
                        for half in range(2):
                            dve.wait_ge(fold_hi.sem, fold_hi.at(blk.b, 2 + half))
                            dve.tensor_tensor(gw_st_lo[:, half, :], misc[half][:, :], gw_st_hi[:, half, :].bitcast(F32),
                                              ALU.subtract).then_inc(fold_lo.sem, 1)
                    if prepares(blk, 2):
                        scaled.denominators(dve, first, paces)

                loop_blocks(dve, B, NB, body)

            @block.scalar
            def _(act):
                def split_high(blk):
                    for half in range(2):
                        act.wait_ge(transposed.sem, transposed.at(blk.s, half + 1))
                        act.activation(hT_hi[:, half, :], trp[half][:, :], ACT.Copy).then_inc(hi_ready.sem, 1)

                def exps(blk):
                    for bank in range(2):
                        act.wait_ge(q_done.sem, q_done.at(blk.s, bank + 1))
                        if bank == 0 and not (isinstance(blk.s, int) and blk.s < 2):
                            act.wait_ge(kv_read.sem, kv_read.at(blk.s - 2))
                        if not (isinstance(blk.s, int) and blk.s == 0):
                            act.wait_ge(feat_ready.sem, feat_ready.at(blk.s - 1, bank + 1))
                        act.activation(negpart[:, bank, :, :], qp[bank][:, :, :], ACT.Relu, scale=-1.0).then_inc(neg_ready.sem, 1)
                        act.activation(q[:, blk.par, 2 * bank:2 * bank + 2, :], qp[bank][:, :, :], ACT.Copy).then_inc(q_copied.sem, 1)
                        act.wait_ge(neg_ready.sem, neg_ready.at(blk.s, bank + 1))
                        act.wait_ge(q_copied.sem, q_copied.at(blk.s, bank + 1))
                        act.activation(expneg[:, bank, :, :], negpart[:, bank, :, :], ACT.Exp, scale=-1.0).then_inc(exp_ready.sem, 1)

                def residual(blk):
                    p = blk.par
                    act.wait_ge(pool_small.sem, pool_small.at(blk.s))
                    act.wait_ge(x_in[p].sem, x_in[p].at(blk.turn))
                    if not (isinstance(blk.s, int) and blk.s < 2):
                        act.wait_ge(base_out[p].sem, base_out[p].at(blk.turn - 1))
                    for i in range(TILES):
                        act.activation(base[:, p, i, :], x[:, p, i, :], ACT.Identity, scale=rstd1[:, p, i:i + 1],
                                       bias=negmur[:, p, i:i + 1]).then_inc(base_ready.sem, 1)

                act.wait_ge(small_in, 16 * 5)
                act.activation(gates[:, 1, :], gates[:, 0, :], ACT.Exp, scale=-1.0).then_inc(gate_act, 1)
                residual(first)
                residual(first.plus(1))
                split_high(first)
                exps(first)
                split_high(first.plus(1))
                exps(first.plus(1))

                def body(blk):
                    after = blk.plus(2)
                    if after is not None:
                        split_high(after)
                        residual(after)
                    act.wait_ge(raw_in[blk.par].sem, raw_in[blk.par].at(blk.turn))
                    for raw, hi, lo in weight_parts(blk):
                        act.activation(hi, raw, ACT.Copy).then_inc(w_high.sem, 1)
                    if blk.j == NB - 1:
                        act.wait_ge(fold_out.sem, fold_out.at(blk.b - 1))
                        act.wait_ge(ks_done.sem, ks_done.at(blk.b))
                        act.activation(ks_st, misc[0][:, 0:C], ACT.Copy).then_inc(ks_copied.sem, 1)
                        act.wait_ge(g_done.sem, g_done.at(blk.b))
                        act.activation(g_st_hi, misc[1][:, :].rearrange("p (h n) -> p h n", h=2), ACT.Copy).then_inc(fold_hi.sem, 1)
                        act.wait_ge(gT_done.sem, gT_done.at(blk.b))
                        act.activation(gT[:, :, :], kvp[0][:, :, :], ACT.Copy).then_inc(gT_copied.sem, 1)
                    if after is not None:
                        exps(after)
                    if blk.j == NB - 1:
                        for half in range(2):
                            act.wait_ge(gw_done.sem, gw_done.at(blk.b, half + 1))
                            act.activation(gw_st_hi[:, half, :], misc[half][:, :], ACT.Copy).then_inc(fold_hi.sem, 1)
                        act.wait_ge(ks_copied.sem, ks_copied.at(blk.b))
                        settle(act, paces)
                        act.wait_ge(fold_hi.sem, fold_hi.at(blk.b))
                        settle(act, paces)
                        act.wait_ge(fold_lo.sem, fold_lo.at(blk.b))
                        settle(act, paces)
                        r = bass.ds(value(blk.b * P), P)
                        act.dma_start(t["fold"][r, :], fold_st[:, :].bitcast(F32)).then_inc(fold_out.sem, 16)

                loop_blocks(act, B, NB, body)

            @block.tensor
            def _(pe):
                ks_done.grant(pe)
                ident = t["ident"]

                def transposes(blk):
                    if not (isinstance(blk.s, int) and blk.s == 0):
                        pe.wait_ge(lo_ready.sem, lo_ready.at(blk.s - 1))
                    for half in range(2):
                        for i in range(TILES):
                            pe.wait_ge(h_ready.sem, h_ready.at(blk.s, i + 1))
                            last = pe.transpose(trp[half][:, i * P:(i + 1) * P], h[:, blk.par, i, half * P:(half + 1) * P], ident[:, :])
                        last.then_inc(transposed.sem, 1)

                def project_q(blk):
                    if not (isinstance(blk.s, int) and blk.s == 0):
                        pe.wait_ge(exp_ready.sem, exp_ready.at(blk.s - 1))
                    for half in range(2):
                        pe.wait_ge(lo_ready.sem, lo_ready.at(blk.s, half + 1))
                    for i in range(TILES):
                        cols = slice(i * P, (i + 1) * P)
                        last = product(pe, qp[i // 2][:, i % 2, :],
                                       [((hT_hi[:, hf, cols], hT_lo[:, hf, cols]), (wq_hi[:, hf, :], wq_lo[:, hf, :]))
                                        for hf in range(2)])
                        if i % 2:
                            last.then_inc(q_done.sem, 1)

                pe.wait_ge(consts, 11)
                pe.wait_ge(wq_split, 2)
                pe.wait_ge(sim_squared, 1)
                for half in range(2):
                    last = pe.matmul(misc[0][:, 0:8], ones[:, :], simsq[:, half, :], start=(half == 0), stop=(half == 1))
                last.then_inc(gate_pe, 1)
                transposes(first)
                project_q(first)
                transposes(first.plus(1))
                project_q(first.plus(1))

                def values_keys(blk):
                    for i in range(TILES):
                        pe.wait_ge(feat_ready.sem, feat_ready.at(blk.s, i // 2 + 1))
                        for half in range(2):
                            last = pe.matmul(kvp[half][:, 0, :], q[:, blk.par, i, half * P:(half + 1) * P], feat[:, blk.par, i, :],
                                             start=(blk.j == 0 and i == 0), stop=(blk.j == NB - 1 and i == TILES - 1))
                    return last

                def fold(blk):
                    pe.wait_ge(summed.sem, summed.at(blk.s))
                    pe.wait_ge(fold_lo.sem, fold_lo.at(blk.b - 1))
                    for i in range(TILES):
                        last = pe.matmul(misc[0][:, 0:C], ones[:, :], fsum[:, i, :], start=(i == 0), stop=(i == TILES - 1))
                    last.then_inc(ks_done.sem, 1)
                    pe.wait_ge(kv_masked.sem, kv_masked.at(blk.b))
                    for half in range(2):
                        last = pe.matmul(misc[1][:, half * C:(half + 1) * C], kvT[:, half, :], wm[:, half, :], start=True, stop=True)
                    last.then_inc(g_done.sem, 1)
                    for nh in range(2):
                        for half in range(2):
                            last = pe.matmul(kvp[0][:, nh, half * P:(half + 1) * P], wm[:, half, nh * P:(nh + 1) * P],
                                             kvT[:, half, :], start=True, stop=True)
                    last.then_inc(gT_done.sem, 1)

                def fold_hidden(blk):
                    pe.wait_ge(gT_copied.sem, gT_copied.at(blk.b))
                    pe.wait_ge(ks_copied.sem, ks_copied.at(blk.b))
                    pe.wait_ge(fold_lo.sem, fold_lo.at(blk.b, 1))
                    for half in range(2):
                        for nh in range(2):
                            last = pe.matmul(misc[half][:, :], gT[:, nh, half * P:(half + 1) * P], w1[:, nh, :],
                                             start=(nh == 0), stop=(nh == 1))
                        last.then_inc(gw_done.sem, 1)

                def body(blk):
                    after = blk.plus(2)
                    if after is not None:
                        transposes(after)
                    values_keys(blk).then_inc(kv_read.sem, 1)
                    if blk.j == NB - 1:
                        fold(blk)
                    if after is not None:
                        project_q(after)
                    if blk.j == NB - 1:
                        fold_hidden(blk)

                loop_blocks(pe, B, NB, body)


class ScaledFeatures:
    def __init__(self, c, t, d):
        C = d["C"]
        self.t, self.C, self.batches, self.per_batch = t, C, d["B"], d["NB"]
        self.feat = c.sb("feat", [P, 2, TILES, C])
        self.ksum = c.sb("ksum", [P, C])
        self.fz = c.sb("fz", [P, TILES, C])
        self.den = c.sb("den", [P, 2, TILES * 8])
        self.z = c.sb("z", [P, TILES * 8])
        self.fold = c.sb("fold", [P, 12 * C], F32R)
        self.g_hi, self.g_lo, self.gw_hi, self.gw_lo = fold_matrices(self.fold[:, :], C)
        self.feat_in = [c.flag(f"feat_in{i}", 16) for i in range(2)]
        self.ks_in = c.flag("ks_in", 16)
        self.fold_in = c.flag("fold_in", 16)
        self.prod_ready = c.flag("prod_ready", 1)
        self.den_ready = c.flag("den_ready", 1)
        self.z_steps = c.flag("z_steps", 2)
        self.ready = c.flag("fz_ready", 1)

    def load_feat(self, sp, blk):
        sp.dma_start(self.feat[:, blk.par, :, :], rows(self.t["feat"], blk, self.C)).then_inc(self.feat_in[blk.par].sem, 16)

    def load_ksum(self, sp, b):
        sp.dma_start(self.ksum[:, :], self.t["fold"][bass.ds(value(b * P), P), 0:self.C]).then_inc(self.ks_in.sem, 16)

    def load_fold(self, sp, b):
        r = bass.ds(value(b * P), P)
        sp.dma_start(self.fold[:, :].bitcast(F32), self.t["fold"][r, self.C:]).then_inc(self.fold_in.sem, 16)

    def ksum_product(self, pool, blk):
        pool.wait_ge(self.feat_in[blk.par].sem, self.feat_in[blk.par].at(blk.turn))
        pool.wait_ge(self.ks_in.sem, self.ks_in.at(blk.b))
        pool.tensor_tensor(self.fz[:, :, :], self.feat[:, blk.par, :, :],
                           self.ksum[:, :].unsqueeze(1).to_broadcast([P, TILES, self.C]), ALU.mult).then_inc(self.prod_ready.sem, 1)

    def denominators(self, dve, blk, paces):
        dve.wait_ge(self.prod_ready.sem, self.prod_ready.at(blk.s))
        dve.tensor_reduce(self.den[:, 0, :], self.fz[:, :, :].rearrange("p t (h k) -> p (t h) k", h=8),
                          AX_X, ALU.add).then_inc(self.den_ready.sem, 1)
        dve.wait_ge(self.den_ready.sem, self.den_ready.at(blk.s))
        dve.tensor_scalar(self.den[:, 1, :], self.den[:, 0, :], ATTN_EPS, None, ALU.add).then_inc(self.z_steps.sem, 1)
        dve.wait_ge(self.z_steps.sem, self.z_steps.at(blk.s, 1))
        settle(dve, paces)
        dve.reciprocal(self.z[:, :], self.den[:, 1, :]).then_inc(self.z_steps.sem, 1)

    def normalise(self, pool, blk):
        pool.wait_ge(self.z_steps.sem, self.z_steps.at(blk.s))
        pool.tensor_tensor(self.fz[:, :, :].rearrange("p t (h k) -> p (t h) k", h=8),
                           self.feat[:, blk.par, :, :].rearrange("p t (h k) -> p (t h) k", h=8),
                           self.z[:, :].unsqueeze(2).to_broadcast([P, TILES * 8, self.C // 8]), ALU.mult).then_inc(self.ready.sem, 1)


PE_AT = dict(message=(3, 4), hidden=(2, 3, 4, 5), mlp=(8, 9, 10, 11), h2_transpose=(23,), gate=(26,), gate_transpose=(27,))
DVE_AT = dict(msg_moments=(4, 5), hidden_low=(3, 4, 5, 6), denominators=(8,),
              mlp_moments=(9, 9, 11, 11), mlp_centre=(12, 12, 13, 13), mlp_add=(14, 14, 15, 15),
              x1_moments=(15, 15, 16, 16), h2_low=(23, 24), logits=(27,), router=(28, 29, 30, 31))


def at(slots, what, k):
    return [n for n, slot in enumerate(slots[what]) if slot == k]


def stage2(nc, t, d, scaled):
    B, NB, C, E, D = d["B"], d["NB"], d["C"], d["E"], d["D"]
    W3 = 3 * D
    CH = TILES * E
    with ExitStack() as st:
        c = Ctx(nc, st, "b_")
        base = c.sb("base", [P, 2, TILES, C])
        fT_hi = c.sb("fT_hi", [P, 2, BLOCK], F32R)
        fT_lo = c.sb("fT_lo", [P, 2, BLOCK], F32R)
        hid_hi = c.sb("hid_hi", [P, 4, BLOCK], F32R)
        hid_lo = c.sb("hid_lo", [P, 4, BLOCK], F32R)
        g1b = c.sb("g1b", [P, C])
        g2b = c.sb("g2b", [P, C])
        b1b = c.sb("b1b", [P, C])
        b2b = c.sb("b2b", [P, C])
        b12 = c.sb("b12", [P, C])
        stats = c.sb("stats", [P, 3, TILES, 6])
        mv = c.sb("mv", [P, 3, TILES, 2])
        ve = c.sb("ve", [P, 3, TILES])
        rstd = c.sb("rstd", [P, 3, TILES])
        negmu = c.sb("negmu", [P, 2, TILES])
        negmur = c.sb("negmur", [P, 2, TILES])
        nrm = c.sb("nrm", [P, 4, TILES])
        rnorm = c.sb("rnorm", [P, TILES])
        u = c.sb("u", [P, TILES, C])
        x1 = c.sb("x1", [P, 2, TILES, C])
        h2 = c.sb("h2", [P, TILES, C])
        h2T_hi = c.sb("h2T_hi", [P, 2, 2, BLOCK], F32R)
        h2T_lo = c.sb("h2T_lo", [P, 2, 2, BLOCK], F32R)
        lgT = c.sb("lgT", [E, BLOCK])
        lg = c.sb("lg", [P, TILES, E])
        logit = c.sb("logit", [P, TILES, E])
        above = c.sb("above", [P, TILES, E, E])
        atleast = c.sb("atleast", [P, TILES, E, E])
        before = c.sb("before", [P, E, E])
        notbefore = c.sb("notbefore", [P, E, E])
        rank = c.sb("rank", [P, TILES, E])
        top = c.sb("top", [P, 3, TILES])
        fallback = c.sb("fallback", [P, TILES, E])
        mask = c.sb("mask", [P, 2, TILES, E])
        gated = c.sb("gated", [P, TILES, E])
        expo = c.sb("expo", [P, 2, TILES, E])
        halves = c.sb("halves", [P, TILES, 6])
        total = c.sb("total", [P, 2, TILES])
        route = c.sb("route", [P, 2, TILES, E])
        acc = c.sb("acc", [P, TILES, W3])
        v_hi = c.sb("v_hi", [P, 2, TILES, D], F32R)
        v_lo = c.sb("v_lo", [P, 2, TILES, D], F32R)
        qk_hi = c.sb("qk_hi", [P, 2, 2, BLOCK], F32R)
        qk_lo = c.sb("qk_lo", [P, 2, 2, BLOCK], F32R)

        F = [c.ps(f"F{i}", [P, BLOCK]) for i in range(4)]
        X = [c.ps(f"X{i}", [P, W3]) for i in range(4)]

        setup_in = c.sem("setup_in")
        setup = c.sem("setup")
        base_in = [c.flag(f"base_in{i}", 16) for i in range(2)]
        res_ready = c.flag("res_ready", 1)
        f_transposed = c.flag("f_transposed", 2)
        f_hi = c.flag("f_hi", 2)
        f_lo = c.flag("f_lo", 2)
        msg_done = c.flag("msg_done", 2)
        hid_done = c.flag("hid_done", 4)
        h_hi = c.flag("h_hi", 4)
        h_lo = c.flag("h_lo", 4)
        mlp_done = c.flag("mlp_done", 2)
        st_ready = c.flag("st_ready", 3 * TILES)
        mv_ready = c.flag("mv_ready", 3 * TILES)
        rstd_steps = c.flag("rstd_steps", 6)
        h2_steps = c.flag("h2_steps", 2)
        rn_steps = c.flag("rn_steps", 5)
        msg_steps = c.flag("msg_steps", 2)
        msg_normal = c.flag("msg_normal", TILES)
        msg_scaled = c.flag("msg_scaled", 1)
        msg_added = c.flag("msg_added", 1)
        u_ready = c.flag("u_ready", TILES)
        x1_steps = c.flag("x1_steps", TILES)
        x1_out = [c.flag(f"x1_out{i}", 16, ahead=1) for i in range(2)]
        h2_ready = c.flag("h2_ready", TILES)
        h2_transposed = c.flag("h2_transposed", 2)
        h2_hi = c.flag("h2_hi", 2)
        h2_lo = c.flag("h2_lo", 2)
        lgT_done = c.flag("lgT_done", 1)
        lgT_copied = c.flag("lgT_copied", 1)
        lg_done = c.flag("lg_done", 1)
        lg_ready = c.flag("lg_ready", 1)
        gate_steps = c.flag("gate_steps", 3)
        pair_steps = c.flag("pair_steps", 5)
        top_steps = c.flag("top_steps", 3)
        route_steps = c.flag("route_steps", 5)
        mask_ready = c.flag("mask_ready", 1)
        expo_in = c.flag("expo_in", 1)
        expo_ready = c.flag("expo_ready", 1)
        route_ready = c.flag("route_ready", 1, ahead=1)
        route_out = [c.flag(f"route_out{i}", 16, ahead=1) for i in range(2)]
        expert_done = c.flag("expert_done", CH)
        combined = c.flag("combined", CH, ahead=1)
        qk_transposed = c.flag("qk_transposed", 1, ahead=1)
        v_hi_ready = c.flag("v_hi_ready", TILES)
        v_lo_ready = c.flag("v_lo_ready", TILES, ahead=1)
        v_out = [c.flag(f"v_out{i}", 32, ahead=1) for i in range(2)]
        qk_hi_ready = c.flag("qk_hi_ready", 2)
        qk_lo_ready = c.flag("qk_lo_ready", 2, ahead=2)
        qk_out = [c.flag(f"qk_out{i}", 64, ahead=1) for i in range(2)]

        first = Blk(0, 0, B, NB)
        turns = B * NB // 2

        def tile_expert(k):
            return k // (2 * E) * 2 + k % 2, k % (2 * E) // 2

        def last_of_tile(i):
            return i // 2 * 2 * E + 2 * (E - 1) + i % 2

        paces = {e.engine: c.sem(f"pace_{k}") for k, e in enumerate((nc.sync, nc.gpsimd, nc.vector, nc.tensor))}

        with nc.Block() as block:

            @block.sync
            def _(sp):
                for g in (*x1_out, *route_out, *v_out, *qk_out):
                    g.grant(sp)

                def load_base(blk):
                    sp.dma_start(base[:, blk.par, :, :], rows(t["base"], blk, C)).then_inc(base_in[blk.par].sem, 16)

                load_base(first)
                load_base(first.plus(1))
                for dst, name in ((g1b, "g1"), (g2b, "g2"), (b1b, "b1"), (b2b, "b2")):
                    sp.dma_start(dst[:, :], t[name].partition_broadcast(P)).then_inc(setup_in, 16)

                def body(blk):
                    nxt, after = blk.plus(1), blk.plus(2)
                    if after is not None:
                        sp.wait_ge(scaled.ready.sem, scaled.ready.at(blk.s))
                        settle(sp, paces)
                        scaled.load_feat(sp, after)
                        sp.wait_ge(res_ready.sem, res_ready.at(blk.s))
                        settle(sp, paces)
                        load_base(after)
                    if blk.j == NB - 2 and after is not None:
                        sp.wait_ge(scaled.prod_ready.sem, scaled.prod_ready.at(nxt.s))
                        settle(sp, paces)
                        scaled.load_ksum(sp, after.b)
                        sp.wait_ge(hid_done.sem, hid_done.at(nxt.s))
                        settle(sp, paces)
                        scaled.load_fold(sp, after.b)
                    sp.wait_ge(v_lo_ready.sem, v_lo_ready.at(blk.s))
                    settle(sp, paces)
                    sp.dma_start(rows(t["v_hi"], blk, D), v_hi[:, blk.par, :, :].bitcast(F32)).then_inc(v_out[blk.par].sem, 16)
                    sp.dma_start(rows(t["v_lo"], blk, D), v_lo[:, blk.par, :, :].bitcast(F32)).then_inc(v_out[blk.par].sem, 16)
                    cols = bass.ds(value(blk.s * BLOCK), BLOCK)
                    for name, src, ready in (("T_hi", qk_hi, qk_hi_ready), ("T_lo", qk_lo, qk_lo_ready)):
                        sp.wait_ge(ready.sem, ready.at(blk.s))
                        settle(sp, paces)
                        for i, w in enumerate("qk"):
                            sp.dma_start(t[w + name][:, cols], src[:, blk.par, i, :].bitcast(F32)).then_inc(qk_out[blk.par].sem, 16)
                    if nxt is not None:
                        store_front(nxt)

                def store_front(blk):
                    sp.wait_ge(x1_steps.sem, x1_steps.at(blk.s))
                    settle(sp, paces)
                    sp.dma_start(rows(t["x1"], blk, C), x1[:, blk.par, :, :]).then_inc(x1_out[blk.par].sem, 16)
                    sp.wait_ge(route_ready.sem, route_ready.at(blk.s))
                    settle(sp, paces)
                    sp.dma_start(rows(t["route"], blk, E), route[:, blk.par, :, :]).then_inc(route_out[blk.par].sem, 16)

                store_front(first)
                loop_blocks(sp, B, NB, body)
                for par in range(2):
                    for g in (x1_out, route_out, v_out, qk_out):
                        sp.wait_ge(g[par].sem, g[par].at(turns - 1))
                        settle(sp, paces)

            @block.gpsimd
            def _(pool):
                v_lo_ready.grant(pool)
                route_ready.grant(pool)
                pool.memset(before[:, :, :], 1.0).then_inc(setup, 1)
                pool.wait_ge(setup, 1)
                pool.affine_select(out=before[:, :, :], in_=before[:, :, :], compare_op=ALU.is_gt, fill=0.0, base=0,
                                   pattern=[[1, E], [-1, E]], channel_multiplier=0).then_inc(setup, 1)
                pool.wait_ge(setup, 2)
                pool.tensor_scalar(notbefore[:, :, :], before[:, :, :], -1.0, 1.0, ALU.mult, ALU.add).then_inc(setup, 1)
                pool.wait_ge(setup_in, 64)
                pool.tensor_tensor(b12[:, :], b1b[:, :], b2b[:, :], ALU.add).then_inc(setup, 1)
                pool.wait_ge(setup, 4)

                def ksum_product(blk):
                    pool.wait_ge(f_transposed.sem, f_transposed.at(blk.s - 1))
                    scaled.ksum_product(pool, blk)

                def residual(blk):
                    pool.wait_ge(base_in[blk.par].sem, base_in[blk.par].at(blk.turn))
                    pool.wait_ge(x1_out[blk.par].sem, x1_out[blk.par].at(blk.turn - 1))
                    pool.tensor_tensor(x1[:, blk.par, :, :], base[:, blk.par, :, :],
                                       b12[:, :].unsqueeze(1).to_broadcast([P, TILES, C]), ALU.add).then_inc(res_ready.sem, 1)

                def rstds(blk, n):
                    pool.wait_ge(mv_ready.sem, mv_ready.at(blk.s, (n + 1) * TILES))
                    settle(pool, paces)
                    pool.tensor_scalar(ve[:, n, :], mv[:, n, :, 1], LN_EPS, None, ALU.add).then_inc(rstd_steps.sem, 1)
                    pool.wait_ge(rstd_steps.sem, rstd_steps.at(blk.s, 2 * n + 1))
                    pool.tensor_tensor(rstd[:, n, :], ve[:, n, :], t["minus_half"][:, 0:TILES], ALU.pow).then_inc(rstd_steps.sem, 1)

                def message_offset(blk):
                    pool.wait_ge(rstd_steps.sem, rstd_steps.at(blk.s, 2))
                    settle(pool, paces)
                    pool.tensor_scalar(negmu[:, 0, :], mv[:, 0, :, 0], -1.0, None, ALU.mult).then_inc(msg_steps.sem, 1)
                    pool.wait_ge(msg_steps.sem, msg_steps.at(blk.s, 1))
                    pool.tensor_tensor(negmur[:, 0, :], negmu[:, 0, :], rstd[:, 0, :], ALU.mult).then_inc(msg_steps.sem, 1)

                def add_message(blk):
                    pool.wait_ge(msg_normal.sem, msg_normal.at(blk.s))
                    pool.tensor_tensor(u[:, :, :], u[:, :, :], g1b[:, :].unsqueeze(1).to_broadcast([P, TILES, C]),
                                       ALU.mult).then_inc(msg_scaled.sem, 1)
                    pool.wait_ge(msg_scaled.sem, msg_scaled.at(blk.s))
                    pool.wait_ge(res_ready.sem, res_ready.at(blk.s))
                    pool.tensor_tensor(x1[:, blk.par, :, :], x1[:, blk.par, :, :], u[:, :, :], ALU.add).then_inc(msg_added.sem, 1)

                def x1_scales(blk):
                    pool.wait_ge(rstd_steps.sem, rstd_steps.at(blk.s))
                    settle(pool, paces)
                    pool.tensor_scalar(negmu[:, 1, :], mv[:, 2, :, 0], -1.0, None, ALU.mult).then_inc(h2_steps.sem, 1)
                    pool.wait_ge(h2_steps.sem, h2_steps.at(blk.s, 1))
                    pool.tensor_tensor(negmur[:, 1, :], negmu[:, 1, :], rstd[:, 2, :], ALU.mult).then_inc(h2_steps.sem, 1)
                    pool.tensor_scalar(nrm[:, 0, :], mv[:, 2, :, 1], float(C), None, ALU.mult).then_inc(rn_steps.sem, 1)
                    pool.wait_ge(rn_steps.sem, rn_steps.at(blk.s, 1))
                    pool.tensor_tensor(nrm[:, 1, :], nrm[:, 0, :], t["half"][:, 0:TILES], ALU.pow).then_inc(rn_steps.sem, 1)
                    pool.wait_ge(rn_steps.sem, rn_steps.at(blk.s, 2))
                    pool.tensor_tensor(nrm[:, 2, :], nrm[:, 1, :], rstd[:, 2, :], ALU.mult).then_inc(rn_steps.sem, 1)
                    pool.wait_ge(rn_steps.sem, rn_steps.at(blk.s, 3))
                    settle(pool, paces)
                    pool.tensor_scalar(nrm[:, 3, :], nrm[:, 2, :], NORM_EPS, None, ALU.max).then_inc(rn_steps.sem, 1)
                    pool.wait_ge(rn_steps.sem, rn_steps.at(blk.s, 4))
                    pool.tensor_tensor(rnorm[:, :], nrm[:, 3, :], t["minus_one"][:, 0:TILES], ALU.pow).then_inc(rn_steps.sem, 1)

                def routing(blk):
                    p = blk.par
                    pool.wait_ge(expo_ready.sem, expo_ready.at(blk.s))
                    pool.wait_ge(mask_ready.sem, mask_ready.at(blk.s))
                    pool.tensor_tensor(expo[:, 1, :, :], expo[:, 0, :, :], mask[:, p, :, :], ALU.mult).then_inc(route_steps.sem, 1)
                    pool.wait_ge(route_steps.sem, route_steps.at(blk.s, 1))
                    pool.tensor_tensor(halves[:, :, 0:4], expo[:, 1, :, 0:4], expo[:, 1, :, 4:8], ALU.add).then_inc(route_steps.sem, 1)
                    pool.wait_ge(route_steps.sem, route_steps.at(blk.s, 2))
                    pool.tensor_tensor(halves[:, :, 4:6], halves[:, :, 0:2], halves[:, :, 2:4], ALU.add).then_inc(route_steps.sem, 1)
                    pool.wait_ge(route_steps.sem, route_steps.at(blk.s, 3))
                    pool.tensor_tensor(total[:, 0, :], halves[:, :, 4], halves[:, :, 5], ALU.add).then_inc(route_steps.sem, 1)
                    pool.wait_ge(route_steps.sem, route_steps.at(blk.s, 4))
                    pool.tensor_tensor(total[:, 1, :], total[:, 0, :], t["minus_one"][:, 0:TILES], ALU.pow).then_inc(route_steps.sem, 1)
                    pool.wait_ge(route_steps.sem, route_steps.at(blk.s, 5))
                    pool.wait_ge(route_out[p].sem, route_out[p].at(blk.turn - 1))
                    pool.tensor_tensor(route[:, p, :, :], expo[:, 1, :, :],
                                       total[:, 1, :].unsqueeze(2).to_broadcast([P, TILES, E]), ALU.mult).then_inc(route_ready.sem, 1)

                def v_low(blk, i):
                    p = blk.par
                    if i == 0:
                        pool.wait_ge(v_out[p].sem, v_out[p].at(blk.turn - 1))
                    pool.wait_ge(v_hi_ready.sem, v_hi_ready.at(blk.s, i + 1))
                    pool.tensor_tensor(v_lo[:, p, i, :], acc[:, i, 2 * D:], v_hi[:, p, i, :].bitcast(F32),
                                       ALU.subtract).then_inc(v_lo_ready.sem, 1)

                residual(first)
                ksum_product(first.plus(1))
                rstds(first, 0)
                message_offset(first)
                add_message(first)
                scaled.normalise(pool, first.plus(1))
                rstds(first, 1)
                rstds(first, 2)
                x1_scales(first)
                routing(first)

                def body(blk):
                    nxt, after = blk.plus(1), blk.plus(2)
                    if nxt is not None:
                        residual(nxt)
                    if after is not None:
                        ksum_product(after)
                    if nxt is not None:
                        rstds(nxt, 0)
                        message_offset(nxt)
                        add_message(nxt)
                    if after is not None:
                        scaled.normalise(pool, after)
                    if nxt is not None:
                        rstds(nxt, 1)
                        rstds(nxt, 2)
                        x1_scales(nxt)
                    v_low(blk, 0)
                    v_low(blk, 1)
                    if nxt is not None:
                        routing(nxt)
                    v_low(blk, 2)
                    v_low(blk, 3)

                loop_blocks(pool, B, NB, body)

            @block.scalar
            def _(act):
                def f_high(blk):
                    for half in range(2):
                        act.wait_ge(f_transposed.sem, f_transposed.at(blk.s, half + 1))
                        act.activation(fT_hi[:, half, :], F[half][:, :], ACT.Copy).then_inc(f_hi.sem, 1)

                def hidden_high(blk, k):
                    act.wait_ge(hid_done.sem, hid_done.at(blk.s, k + 1))
                    act.activation(hid_hi[:, k, :], F[k % 2][:, :], ACT.Relu).then_inc(h_hi.sem, 1)

                def normalise_message(blk):
                    act.wait_ge(msg_steps.sem, msg_steps.at(blk.s))
                    if not (isinstance(blk.s, int) and blk.s == 0):
                        act.wait_ge(x1_steps.sem, x1_steps.at(blk.s - 1))
                    for i in range(TILES):
                        act.activation(u[:, i, :], F[2 + i // 2][:, (i % 2) * C:(i % 2 + 1) * C], ACT.Identity,
                                       scale=rstd[:, 0, i:i + 1], bias=negmur[:, 0, i:i + 1]).then_inc(msg_normal.sem, 1)

                def normalise_x1(blk):
                    act.wait_ge(h2_steps.sem, h2_steps.at(blk.s))
                    act.wait_ge(x1_steps.sem, x1_steps.at(blk.s))
                    for i in range(TILES):
                        act.activation(h2[:, i, :], x1[:, blk.par, i, :], ACT.Identity, scale=rstd[:, 2, i:i + 1],
                                       bias=negmur[:, 1, i:i + 1]).then_inc(h2_ready.sem, 1)

                def h2_high(blk):
                    for half in range(2):
                        act.wait_ge(h2_transposed.sem, h2_transposed.at(blk.s, half + 1))
                        act.activation(h2T_hi[:, blk.par, half, :], F[2 + half][:, :], ACT.Copy).then_inc(h2_hi.sem, 1)

                def gate_copy(blk):
                    act.wait_ge(lgT_done.sem, lgT_done.at(blk.s))
                    act.activation(lgT[:, :], F[0][0:E, :], ACT.Copy).then_inc(lgT_copied.sem, 1)

                def gate_exp(blk):
                    act.wait_ge(expo_in.sem, expo_in.at(blk.s))
                    act.activation(expo[:, 0, :, :], gated[:, :, :], ACT.Exp).then_inc(expo_ready.sem, 1)

                def v_high(blk, i):
                    act.wait_ge(combined.sem, combined.at(blk.s, last_of_tile(i) + 1))
                    if i == 0:
                        act.wait_ge(v_out[blk.par].sem, v_out[blk.par].at(blk.turn - 1))
                    act.activation(v_hi[:, blk.par, i, :], acc[:, i, 2 * D:], ACT.Copy).then_inc(v_hi_ready.sem, 1)

                def qk_high(blk):
                    act.wait_ge(qk_out[blk.par].sem, qk_out[blk.par].at(blk.turn - 1))
                    act.wait_ge(qk_transposed.sem, qk_transposed.at(blk.s))
                    for k in range(2):
                        act.activation(qk_hi[:, blk.par, k, :], F[2 + k][:, :], ACT.Copy).then_inc(qk_hi_ready.sem, 1)

                f_high(first)
                for k in range(4):
                    hidden_high(first, k)
                normalise_message(first)
                normalise_x1(first)
                h2_high(first)
                gate_copy(first)
                f_high(first.plus(1))
                gate_exp(first)

                def body(blk):
                    nxt, after = blk.plus(1), blk.plus(2)
                    if nxt is not None:
                        for k in range(4):
                            hidden_high(nxt, k)
                        normalise_message(nxt)
                        normalise_x1(nxt)
                    v_high(blk, 0)
                    v_high(blk, 1)
                    if nxt is not None:
                        h2_high(nxt)
                        gate_copy(nxt)
                        gate_exp(nxt)
                    v_high(blk, 2)
                    v_high(blk, 3)
                    if after is not None:
                        f_high(after)
                    qk_high(blk)

                loop_blocks(act, B, NB, body)

            @block.vector
            def _(dve):
                combined.grant(dve)
                qk_lo_ready.grant(dve)
                msg = [F[2 + i // 2][:, (i % 2) * C:(i % 2 + 1) * C] for i in range(TILES)]
                mlp = [F[i // 2][:, (i % 2) * C:(i % 2 + 1) * C] for i in range(TILES)]

                def f_low(blk, half):
                    dve.wait_ge(f_hi.sem, f_hi.at(blk.s, half + 1))
                    dve.tensor_tensor(fT_lo[:, half, :], F[half][:, :], fT_hi[:, half, :].bitcast(F32),
                                      ALU.subtract).then_inc(f_lo.sem, 1)

                def moments(blk, n, i):
                    if n == 0:
                        dve.wait_ge(msg_done.sem, msg_done.at(blk.s, i // 2 + 1))
                    elif n == 1:
                        dve.wait_ge(mlp_done.sem, mlp_done.at(blk.s, i // 2 + 1))
                    else:
                        dve.wait_ge(x1_steps.sem, x1_steps.at(blk.s, i + 1))
                    src = (msg[i], mlp[i], x1[:, blk.par, i, :])[n]
                    dve.bn_stats(stats[:, n, i, :], src).then_inc(st_ready.sem, 1)

                def gather(blk, n):
                    dve.wait_ge(st_ready.sem, st_ready.at(blk.s, (n + 1) * TILES))
                    settle(dve, paces)
                    for i in range(TILES):
                        dve.bn_aggr(mv[:, n, i, :], stats[:, n, i, :]).then_inc(mv_ready.sem, 1)

                def centre(blk, i):
                    dve.wait_ge(mv_ready.sem, mv_ready.at(blk.s, TILES + i + 1))
                    if i == 0:
                        dve.wait_ge(msg_added.sem, msg_added.at(blk.s))
                    dve.scalar_tensor_tensor(out=u[:, i, :], in0=mlp[i], scalar=mv[:, 1, i, 0:1],
                                             in1=g2b[:, :], op0=ALU.subtract, op1=ALU.mult).then_inc(u_ready.sem, 1)

                def add_norm(blk, i):
                    dve.wait_ge(u_ready.sem, u_ready.at(blk.s, i + 1))
                    dve.wait_ge(rstd_steps.sem, rstd_steps.at(blk.s, 4))
                    dve.scalar_tensor_tensor(out=x1[:, blk.par, i, :], in0=u[:, i, :], scalar=rstd[:, 1, i:i + 1],
                                             in1=x1[:, blk.par, i, :], op0=ALU.mult, op1=ALU.add).then_inc(x1_steps.sem, 1)

                def hidden_low(blk, k):
                    dve.wait_ge(h_hi.sem, h_hi.at(blk.s, k + 1))
                    dve.scalar_tensor_tensor(out=hid_lo[:, k, :], in0=F[k % 2][:, :], scalar=0.0,
                                             in1=hid_hi[:, k, :].bitcast(F32), op0=ALU.max, op1=ALU.subtract).then_inc(h_lo.sem, 1)

                def h2_low(blk, half):
                    dve.wait_ge(h2_hi.sem, h2_hi.at(blk.s, half + 1))
                    dve.tensor_tensor(h2T_lo[:, blk.par, half, :], F[2 + half][:, :], h2T_hi[:, blk.par, half, :].bitcast(F32),
                                      ALU.subtract).then_inc(h2_lo.sem, 1)

                def logits(blk):
                    dve.wait_ge(rn_steps.sem, rn_steps.at(blk.s))
                    dve.wait_ge(lg_done.sem, lg_done.at(blk.s))
                    dve.tensor_tensor(lg[:, :, :], F[1][:, 0:TILES * E].rearrange("p (t n) -> p t n", t=TILES),
                                      rnorm[:, :].unsqueeze(2).to_broadcast([P, TILES, E]), ALU.mult).then_inc(lg_ready.sem, 1)

                def router(blk, part):
                    p = blk.par

                    def per_tile(a):
                        return a.unsqueeze(2).to_broadcast([P, TILES, E])

                    def pairs(a):
                        return a.rearrange("p t e j -> p t (e j)")

                    def order(a):
                        return a[:, :, :].rearrange("p e j -> p (e j)").unsqueeze(1).to_broadcast([P, TILES, E * E])

                    def step(k, ins):
                        ins.then_inc(gate_steps.sem, 1)
                        dve.wait_ge(gate_steps.sem, gate_steps.at(blk.s, k))

                    lj = logit[:, :, :].unsqueeze(2).to_broadcast([P, TILES, E, E])
                    le = logit[:, :, :].unsqueeze(3).to_broadcast([P, TILES, E, E])
                    if part == 0:
                        dve.wait_ge(lg_ready.sem, lg_ready.at(blk.s))
                        step(1, dve.tensor_tensor(logit[:, :, :], lg[:, :, :],
                                                  t["sig"][:, :].unsqueeze(1).to_broadcast([P, TILES, E]), ALU.subtract))
                        dve.tensor_tensor(above[:, :, :, :], lj, le, ALU.is_gt).then_inc(pair_steps.sem, 1)
                        dve.tensor_tensor(atleast[:, :, :, :], lj, le, ALU.is_ge).then_inc(pair_steps.sem, 1)
                    if part == 1:
                        dve.wait_ge(pair_steps.sem, pair_steps.at(blk.s, 2))
                        dve.tensor_tensor(pairs(atleast), pairs(atleast), order(before), ALU.mult).then_inc(pair_steps.sem, 1)
                        dve.tensor_tensor(pairs(above), pairs(above), order(notbefore), ALU.mult).then_inc(pair_steps.sem, 1)
                        dve.tensor_reduce(top[:, 0, :], logit[:, :, :], AX_X, ALU.max).then_inc(top_steps.sem, 1)
                    if part == 2:
                        dve.wait_ge(pair_steps.sem, pair_steps.at(blk.s, 4))
                        dve.tensor_tensor(pairs(above), pairs(above), pairs(atleast), ALU.add).then_inc(pair_steps.sem, 1)
                        dve.wait_ge(top_steps.sem, top_steps.at(blk.s, 1))
                        dve.tensor_scalar(top[:, 1, :], top[:, 0, :], 0.0, None, ALU.is_le).then_inc(top_steps.sem, 1)
                        dve.tensor_scalar(top[:, 2, :], top[:, 0, :], 0.0, None, ALU.max).then_inc(top_steps.sem, 1)
                        dve.wait_ge(pair_steps.sem, pair_steps.at(blk.s, 5))
                        dve.tensor_reduce(rank[:, :, :], above[:, :, :, :], AX_X, ALU.add).then_inc(gate_steps.sem, 1)
                    if part == 3:
                        dve.wait_ge(route_ready.sem, route_ready.at(blk.s - 1))
                        dve.wait_ge(top_steps.sem, top_steps.at(blk.s, 3))
                        dve.scalar_tensor_tensor(out=gated[:, :, :], in0=logit[:, :, :], scalar=0.0, in1=per_tile(top[:, 2, :]),
                                                 op0=ALU.max, op1=ALU.subtract).then_inc(expo_in.sem, 1)
                        dve.wait_ge(gate_steps.sem, gate_steps.at(blk.s, 2))
                        step(3, dve.scalar_tensor_tensor(out=fallback[:, :, :], in0=rank[:, :, :], scalar=2.0,
                                                         in1=per_tile(top[:, 1, :]), op0=ALU.is_lt, op1=ALU.mult))
                        dve.scalar_tensor_tensor(out=mask[:, p, :, :], in0=logit[:, :, :], scalar=0.0, in1=fallback[:, :, :],
                                                 op0=ALU.is_gt, op1=ALU.max).then_inc(mask_ready.sem, 1)

                def combine(blk, k):
                    i, e = tile_expert(k)
                    m = mask[:, blk.par, i, e:e + 1]
                    dve.wait_ge(expert_done.sem, expert_done.at(blk.s, k + 1))
                    if k == 0:
                        dve.wait_ge(mask_ready.sem, mask_ready.at(blk.s))
                        dve.wait_ge(qk_transposed.sem, qk_transposed.at(blk.s - 1))
                    if e == 0:
                        dve.wait_ge(v_lo_ready.sem, v_lo_ready.at(blk.s - 1, i + 1))
                        dve.tensor_scalar(acc[:, i, :], X[k % 4][:, :], m, None, ALU.mult).then_inc(combined.sem, 1)
                    else:
                        dve.wait_ge(combined.sem, combined.at(blk.s, k - 1))
                        dve.scalar_tensor_tensor(out=acc[:, i, :], in0=X[k % 4][:, :], scalar=m, in1=acc[:, i, :],
                                                 op0=ALU.mult, op1=ALU.add).then_inc(combined.sem, 1)

                def qk_low(blk):
                    for k in range(2):
                        dve.wait_ge(qk_hi_ready.sem, qk_hi_ready.at(blk.s, k + 1))
                        dve.tensor_tensor(qk_lo[:, blk.par, k, :], F[2 + k][:, :], qk_hi[:, blk.par, k, :].bitcast(F32),
                                          ALU.subtract).then_inc(qk_lo_ready.sem, 1)

                def front(blk, k):
                    for bank in at(DVE_AT, "msg_moments", k):
                        moments(blk, 0, 2 * bank)
                        moments(blk, 0, 2 * bank + 1)
                        if bank == 1:
                            gather(blk, 0)
                    for n in at(DVE_AT, "hidden_low", k):
                        hidden_low(blk, n)
                    for i in at(DVE_AT, "mlp_moments", k):
                        moments(blk, 1, i)
                        if i == TILES - 1:
                            gather(blk, 1)
                    for i in at(DVE_AT, "mlp_centre", k):
                        centre(blk, i)
                    for i in at(DVE_AT, "mlp_add", k):
                        add_norm(blk, i)
                    for i in at(DVE_AT, "x1_moments", k):
                        moments(blk, 2, i)
                        if i == TILES - 1:
                            gather(blk, 2)
                    for half in at(DVE_AT, "h2_low", k):
                        h2_low(blk, half)
                    if at(DVE_AT, "logits", k):
                        logits(blk)
                    for part in at(DVE_AT, "router", k):
                        router(blk, part)

                f_low(first, 0)
                f_low(first, 1)
                dve.wait_ge(setup, 4)
                for k in range(CH):
                    if at(DVE_AT, "denominators", k):
                        scaled.denominators(dve, first.plus(1), paces)
                    front(first, k)
                f_low(first.plus(1), 0)
                f_low(first.plus(1), 1)

                def body(blk):
                    nxt, after = blk.plus(1), blk.plus(2)
                    for k in range(CH):
                        if nxt is not None:
                            front(nxt, k)
                        if at(DVE_AT, "denominators", k) and after is not None:
                            scaled.denominators(dve, after, paces)
                        combine(blk, k)
                    if after is not None:
                        f_low(after, 0)
                        f_low(after, 1)
                    dve.wait_ge(qk_out[blk.par].sem, qk_out[blk.par].at(blk.turn - 1))
                    qk_low(blk)

                loop_blocks(dve, B, NB, body)

            @block.tensor
            def _(pe):
                qk_transposed.grant(pe)
                ident = t["ident"]

                def split(hi, lo, *at):
                    return hi[(slice(None), *at)], lo[(slice(None), *at)]

                def f_transpose(blk):
                    if not (isinstance(blk.s, int) and blk.s == 0):
                        pe.wait_ge(lg_ready.sem, lg_ready.at(blk.s - 1))
                    pe.wait_ge(scaled.ready.sem, scaled.ready.at(blk.s))
                    for half in range(2):
                        for i in range(TILES):
                            last = pe.transpose(F[half][:, i * P:(i + 1) * P], scaled.fz[:, i, half * P:(half + 1) * P], ident[:, :])
                        last.then_inc(f_transposed.sem, 1)

                def message(blk, bank):
                    for i in (2 * bank, 2 * bank + 1):
                        cols = slice(i * P, (i + 1) * P)
                        last = product(pe, F[2 + i // 2][:, (i % 2) * C:(i % 2 + 1) * C],
                                       [(split(fT_hi, fT_lo, hf, cols), split(scaled.g_hi, scaled.g_lo, hf)) for hf in range(2)])
                    last.then_inc(msg_done.sem, 1)

                def hidden(blk, k):
                    if k == 0:
                        pe.wait_ge(f_lo.sem, f_lo.at(blk.s))
                        pe.wait_ge(scaled.fold_in.sem, scaled.fold_in.at(blk.b))
                    if k >= 2:
                        pe.wait_ge(h_lo.sem, h_lo.at(blk.s, k - 1))
                    cols = slice(k * P, (k + 1) * P)
                    product(pe, F[k % 2][:, :], [(split(scaled.gw_hi, scaled.gw_lo, hf, cols), split(fT_hi, fT_lo, hf)) for hf in range(2)])\
                        .then_inc(hid_done.sem, 1)

                def mlp(blk, i):
                    pe.wait_ge(h_lo.sem, h_lo.at(blk.s))
                    cols = slice(i * P, (i + 1) * P)
                    last = product(pe, F[i // 2][:, (i % 2) * C:(i % 2 + 1) * C],
                                   [(split(hid_hi, hid_lo, k, cols), split(t["w2_hi"], t["w2_lo"], k)) for k in range(4)])
                    if i % 2:
                        last.then_inc(mlp_done.sem, 1)

                def h2_transpose(blk):
                    for half in range(2):
                        for i in range(TILES):
                            pe.wait_ge(h2_ready.sem, h2_ready.at(blk.s, i + 1))
                            last = pe.transpose(F[2 + half][:, i * P:(i + 1) * P], h2[:, i, half * P:(half + 1) * P], ident[:, :])
                        last.then_inc(h2_transposed.sem, 1)

                def gate(blk):
                    pe.wait_ge(h2_lo.sem, h2_lo.at(blk.s))
                    product(pe, F[0][0:E, :], [(split(t["sn_hi"], t["sn_lo"], hf), split(h2T_hi, h2T_lo, blk.par, hf)) for hf in range(2)])\
                        .then_inc(lgT_done.sem, 1)

                def gate_transpose(blk):
                    pe.wait_ge(lgT_copied.sem, lgT_copied.at(blk.s))
                    settle(pe, paces)
                    for i in range(TILES):
                        last = pe.transpose(F[1][:, i * E:(i + 1) * E], lgT[:, i * P:(i + 1) * P], ident[0:E, 0:E])
                    last.then_inc(lg_done.sem, 1)

                def expert(blk, k):
                    i, e = tile_expert(k)
                    pe.wait_ge(combined.sem, combined.at(blk.s, k - 3))
                    cols = slice(i * P, (i + 1) * P)
                    pairs = []
                    for hf in range(2):
                        w = slice((hf * E + e) * W3, (hf * E + e + 1) * W3)
                        pairs.append((split(h2T_hi, h2T_lo, blk.par, hf, cols), (t["wqkv_hi"][:, w], t["wqkv_lo"][:, w])))
                    product(pe, X[k % 4][:, :], pairs).then_inc(expert_done.sem, 1)

                def qk_transpose(blk):
                    for i in range(TILES):
                        pe.wait_ge(combined.sem, combined.at(blk.s, last_of_tile(i) + 1))
                        for k in range(2):
                            last = pe.transpose(F[2 + k][:, i * P:(i + 1) * P], acc[:, i, k * D:(k + 1) * D], ident[:, :])
                    last.then_inc(qk_transposed.sem, 1)

                def front(blk, k):
                    for bank in at(PE_AT, "message", k):
                        if bank == 0:
                            pe.wait_ge(qk_lo_ready.sem, qk_lo_ready.at(blk.s - 2))
                        message(blk, bank)
                    for n in at(PE_AT, "hidden", k):
                        hidden(blk, n)
                    for i in at(PE_AT, "mlp", k):
                        mlp(blk, i)
                    if at(PE_AT, "h2_transpose", k):
                        h2_transpose(blk)
                    if at(PE_AT, "gate", k):
                        gate(blk)
                    if at(PE_AT, "gate_transpose", k):
                        gate_transpose(blk)

                f_transpose(first)
                for k in range(CH):
                    front(first, k)
                f_transpose(first.plus(1))

                def body(blk):
                    nxt, after = blk.plus(1), blk.plus(2)
                    for k in range(CH):
                        if nxt is not None:
                            front(nxt, k)
                        expert(blk, k)
                    if after is not None:
                        f_transpose(after)
                    qk_transpose(blk)

                loop_blocks(pe, B, NB, body)


class Tally:

    def __init__(self, sem, counts, ahead=0):
        self.sem, self.counts, self.ahead = sem, counts, ahead

    def at(self, blk, k=None):
        within = sum(self.counts[:blk.j]) + (self.counts[blk.j] if k is None else k)
        return value((blk.b + self.ahead) * sum(self.counts) + within)

    def grant(self, eng):
        eng.sem_inc(self.sem, self.ahead * sum(self.counts))


def stage3(nc, t, d):
    B, NB, C, E, D = d["B"], d["NB"], d["C"], d["E"], d["D"]
    SCALE = float(D) ** -0.5
    counts = [TILES * (NB - j) for j in range(NB)]
    GROUPS = E * C // BLOCK
    OUTS = TILES * GROUPS

    LAG, STEP, AHEAD = 3, 2, 3

    def chunks(blk):
        return NB - blk.j

    def place(blk):
        return Blk(blk.b, NB - 1 - blk.j, B, NB)

    def events(blk, nxt):
        n = counts[blk.j]
        own = [("T", 0), ("T", 1)]
        for u in range(n):
            if u + 2 < n:
                own.append(("T", u + 2))
            own.append(("V", u))
        values_end = len(own)
        own += [("O", r) for r in range(OUTS)]
        m = counts[nxt.j] if nxt is not None else 0
        share = max(2, m * values_end // (values_end + OUTS)) - 2
        places = [2, 3] + [4 + (x + 1) * (values_end - 5) // (share + 1) for x in range(share)]
        at_o = min(2, m - len(places))
        places += [values_end] * at_o
        rest = m - len(places)
        places += [values_end + 2 + (OUTS - 5) * x // max(1, rest) for x in range(rest)]
        out, k = [], 0
        for at, e in enumerate(own):
            while k < m and at >= places[k]:
                out.append(("S", k))
                k += 1
            out.append(e)
        assert k == m
        return out

    def events_act(blk, nxt):
        order = events(blk, nxt)
        if nxt is None:
            return order
        where = {k: at for at, (what, k) in enumerate(order) if what == "S"}
        m, n = counts[nxt.j], chunks(nxt)
        at_x = []
        for k in range(m):
            at = where[k // n * n + n - 1] + LAG + STEP * (k % n)
            if k + 4 < m:
                at = min(at, max(where[k + 4] - AHEAD, where[k // n * n + n - 1] + 1))
            at_x.append(max([min(at, len(order) - 1)] + at_x[-1:]))
        out, k = [], 0
        for at, e in enumerate(order):
            while k < m and at_x[k] <= at:
                out.append(("X", k))
                k += 1
            if e[0] != "S":
                out.append(e)
        assert k == m
        return out

    with ExitStack() as st:
        c = Ctx(nc, st, "c_")
        kT_hi = c.sb("kT_hi", [P, NB, BLOCK], F32R)
        kT_lo = c.sb("kT_lo", [P, NB, BLOCK], F32R)
        v_hi = c.sb("v_hi", [P, NB * TILES, D], F32R)
        v_lo = c.sb("v_lo", [P, NB * TILES, D], F32R)
        qT_hi = c.sb("qT_hi", [P, 2, BLOCK], F32R)
        qT_lo = c.sb("qT_lo", [P, 2, BLOCK], F32R)
        x1 = c.sb("x1", [P, 2, TILES, C])
        route = c.sb("route", [P, 2, TILES, E])
        weight = c.sb("weight", [P, 2, TILES, E])
        probs = c.sb("probs", [P, 2, TILES, NB * BLOCK])
        causal = c.sb("causal", [P, P])
        cmax = c.sb("cmax", [P, TILES, NB])
        tmax = c.sb("tmax", [P, TILES])
        nmax = c.sb("nmax", [P, TILES])
        csum = c.sb("csum", [P, 2, TILES, NB])
        rsum = c.sb("rsum", [P, 2, TILES])
        pT_hi = c.sb("pT_hi", [P, 3, BLOCK], F32R)
        pT_lo = c.sb("pT_lo", [P, 3, BLOCK], F32R)
        oT_hi = c.sb("oT_hi", [P, BLOCK], F32R)
        oT_lo = c.sb("oT_lo", [P, BLOCK], F32R)
        term = c.sb("term", [P, 8, C])

        S = [c.ps(f"S{i}", [P, BLOCK]) for i in range(4)]
        T = [c.ps(f"T{i}", [P, BLOCK]) for i in range(2)]
        Y = [c.ps(f"Y{i}", [P, BLOCK]) for i in range(2)]
        T_BANKS = [Y[1], *T]

        setup = c.sem("setup")
        k_in = [c.flag(f"k_in{i}", 32) for i in range(NB)]
        v_in = [c.flag(f"v_in{i}", 32) for i in range(NB)]
        q_in = [c.flag(f"q_in{i}", 32) for i in range(2)]
        x1_in = [c.flag(f"x1_in{i}", 32) for i in range(2)]

        def tally(name, ahead=0):
            return Tally(c.sem(name), counts, ahead)

        s_done = tally("s_done")
        causal_done = c.flag("causal_done", TILES)
        cmax_ready = tally("cmax_ready")
        tmax_ready = c.flag("tmax_ready", TILES)
        nmax_ready = c.flag("nmax_ready", TILES)
        exp_done = tally("exp_done", 1)
        p_transposed = tally("p_transposed", 1)
        p_hi = tally("p_hi")
        p_lo = tally("p_lo", 1)
        pv_done = tally("pv_done", 1)
        rsum_ready = c.flag("rsum_ready", 1)
        rinv_ready = c.flag("rinv_ready", 1)
        weight_ready = c.flag("weight_ready", 1)
        o_hi = c.flag("o_hi", 1)
        o_lo = c.flag("o_lo", 1)
        out_done = c.flag("out_done", OUTS, ahead=1)
        summed = c.flag("summed", OUTS, ahead=1)
        scaled = c.flag("scaled", OUTS, ahead=1)
        added = c.flag("added", OUTS, ahead=1)
        stored = [c.flag(f"stored{i}", 16, ahead=1) for i in range(2)]

        first = Blk(0, 0, B, NB)

        OUT_BANKS = [Y[1], T[0], T[1], Y[0]]

        def tile_group(r):
            return r // (2 * GROUPS) * 2 + r % 2, r % (2 * GROUPS) // 2

        paces = {e.engine: c.sem(f"pace_{k}") for k, e in enumerate((nc.sync, nc.gpsimd, nc.vector))}

        with nc.Block() as block:

            @block.sync
            def _(sp):
                for g in stored:
                    g.grant(sp)

                def load_k(b, ch):
                    cols = bass.ds(value((b * NB + ch) * BLOCK), BLOCK)
                    sp.dma_start(kT_hi[:, ch, :].bitcast(F32), t["kT_hi"][:, cols]).then_inc(k_in[ch].sem, 16)
                    sp.dma_start(kT_lo[:, ch, :].bitcast(F32), t["kT_lo"][:, cols]).then_inc(k_in[ch].sem, 16)

                def load_v(b, ch):
                    src, at = Blk(b, ch, B, NB), slice(ch * TILES, (ch + 1) * TILES)
                    sp.dma_start(v_hi[:, at, :].bitcast(F32), rows(t["v_hi"], src, D)).then_inc(v_in[ch].sem, 16)
                    sp.dma_start(v_lo[:, at, :].bitcast(F32), rows(t["v_lo"], src, D)).then_inc(v_in[ch].sem, 16)

                def load_q(blk):
                    cols = bass.ds(value(place(blk).s * BLOCK), BLOCK)
                    sp.dma_start(qT_hi[:, blk.par, :].bitcast(F32), t["qT_hi"][:, cols]).then_inc(q_in[blk.par].sem, 16)
                    sp.dma_start(qT_lo[:, blk.par, :].bitcast(F32), t["qT_lo"][:, cols]).then_inc(q_in[blk.par].sem, 16)

                def load_x1(blk):
                    sp.wait_ge(stored[blk.par].sem, stored[blk.par].at(blk.turn - 1))
                    settle(sp, paces)
                    sp.dma_start(x1[:, blk.par, :, :], rows(t["x1"], place(blk), C)).then_inc(x1_in[blk.par].sem, 16)
                    sp.dma_start(route[:, blk.par, :, :], rows(t["route"], place(blk), E)).then_inc(x1_in[blk.par].sem, 16)

                load_q(first)
                for ch in reversed(range(NB)):
                    load_k(0, ch)
                load_q(first.plus(1))
                for ch in range(NB):
                    load_v(0, ch)
                load_x1(first)

                def body(blk):
                    nxt, after = blk.plus(1), blk.plus(2)
                    more = not (isinstance(blk.b, int) and blk.b == B - 1)
                    ch = NB - 1 - blk.j
                    if more and blk.j == 0:
                        sp.wait_ge(s_done.sem, s_done.at(blk))
                        settle(sp, paces)
                        load_k(blk.b + 1, ch)
                    if after is not None:
                        sp.wait_ge(s_done.sem, s_done.at(blk))
                        settle(sp, paces)
                        load_q(after)
                    if nxt is not None:
                        load_x1(nxt)
                    if more:
                        sp.wait_ge(pv_done.sem, pv_done.at(blk))
                        settle(sp, paces)
                        load_v(blk.b + 1, ch)
                    if more and blk.j < NB - 1:
                        sp.wait_ge(s_done.sem, s_done.at(nxt))
                        settle(sp, paces)
                        load_k(blk.b + 1, ch - 1)
                    sp.wait_ge(summed.sem, summed.at(blk.s))
                    settle(sp, paces)
                    sp.wait_ge(added.sem, added.at(blk.s))
                    settle(sp, paces)
                    sp.dma_start(rows(t["out2d"], place(blk), C), x1[:, blk.par, :, :]).then_inc(stored[blk.par].sem, 16)

                loop_blocks(sp, B, NB, body)
                for g in stored:
                    sp.wait_ge(g.sem, g.at(B * NB // 2 - 1))
                    settle(sp, paces)

            @block.gpsimd
            def _(pool):
                pool.memset(causal[:, :], 0.0).then_inc(setup, 1)
                pool.wait_ge(setup, 1)
                pool.affine_select(out=causal[:, :], in_=causal[:, :], compare_op=ALU.is_ge, fill=MASKED, base=0,
                                   pattern=[[-1, P]], channel_multiplier=1).then_inc(setup, 1)

                added.grant(pool)

                def body(blk):
                    p = blk.par
                    pool.wait_ge(rsum_ready.sem, rsum_ready.at(blk.s))
                    pool.tensor_tensor(rsum[:, 1, :], rsum[:, 0, :], t["minus_one"][:, 0:TILES], ALU.pow).then_inc(rinv_ready.sem, 1)
                    pool.wait_ge(rinv_ready.sem, rinv_ready.at(blk.s))
                    pool.wait_ge(x1_in[p].sem, x1_in[p].at(blk.turn))
                    pool.wait_ge(summed.sem, summed.at(blk.s - 1))
                    pool.tensor_tensor(weight[:, p, :, :], route[:, p, :, :],
                                       rsum[:, 1, :].unsqueeze(2).to_broadcast([P, TILES, E]), ALU.mult).then_inc(weight_ready.sem, 1)
                    for q in range(OUTS):
                        i = tile_group(q // 2 * 2 + 1)[0]
                        pool.wait_ge(scaled.sem, scaled.at(blk.s, q + 1))
                        pool.wait_ge(added.sem, added.at(blk.s, q))
                        pool.tensor_tensor(x1[:, p, i, :], x1[:, p, i, :], term[:, q % 8, :], ALU.add).then_inc(added.sem, 1)

                loop_blocks(pool, B, NB, body)

            @block.scalar
            def _(act):
                exp_done.grant(act)
                scaled.grant(act)

                def exponentials(blk, k):
                    n = chunks(blk)
                    i, ch = k // n, n - 1 - k % n
                    width = (i + 1) * P if ch == n - 1 else BLOCK
                    if k % n == 0:
                        act.wait_ge(nmax_ready.sem, nmax_ready.at(blk.s, i + 1))
                    if k == 0 and not (isinstance(blk.s, int) and blk.s < 2):
                        act.wait_ge(p_transposed.sem, p_transposed.at(blk.plus(-2)))
                    act.activation(probs[:, blk.par, i, ch * BLOCK:ch * BLOCK + width], S[k % 4][:, 0:width], ACT.Exp,
                                   bias=nmax[:, i:i + 1], scale=SCALE,
                                   accum_out=csum[:, blk.par, i, ch:ch + 1]).then_inc(exp_done.sem, 1)

                def project(blk, r):
                    i, g = tile_group(r)
                    act.wait_ge(out_done.sem, out_done.at(blk.s, r + 1))
                    if r == 1:
                        act.wait_ge(weight_ready.sem, weight_ready.at(blk.s))
                    for e in range(2):
                        q = r - 1 + e
                        act.wait_ge(added.sem, added.at(blk.s, q - 7))
                        act.activation(term[:, q % 8, :], OUT_BANKS[r % 4][:, e * C:(e + 1) * C], ACT.Copy,
                                       scale=weight[:, blk.par, i, 2 * g + e:2 * g + e + 1]).then_inc(scaled.sem, 1)

                for k in range(counts[0]):
                    exponentials(first, k)

                def body(blk):
                    nxt = blk.plus(1)
                    for what, k in events_act(blk, nxt):
                        if what == "X":
                            exponentials(nxt, k)
                        if what == "O" and k % 2 == 1:
                            project(blk, k)
                        if what == "T":
                            lo = max(0, k - (counts[blk.j] - TILES)) * P
                            act.wait_ge(p_transposed.sem, p_transposed.at(blk, k + 1))
                            act.wait_ge(pv_done.sem, pv_done.at(blk, max(0, k - 2)))
                            act.activation(pT_hi[:, k % 3, lo:], T_BANKS[k % 3][:, lo:], ACT.Copy).then_inc(p_hi.sem, 1)
                        if what == "V" and k == counts[blk.j] - 1:
                            act.wait_ge(pv_done.sem, pv_done.at(blk))
                            act.activation(oT_hi[:, :], Y[0][:, :], ACT.Copy).then_inc(o_hi.sem, 1)

                loop_blocks(act, B, NB, body)

            @block.vector
            def _(dve):
                p_lo.grant(dve)
                summed.grant(dve)

                def scores(blk, k):
                    n = chunks(blk)
                    i, ch = k // n, n - 1 - k % n
                    width = (i + 1) * P if ch == n - 1 else BLOCK
                    dve.wait_ge(s_done.sem, s_done.at(blk, k + 1))
                    if ch == n - 1:
                        dve.tensor_tensor(S[k % 4][:, i * P:(i + 1) * P], S[k % 4][:, i * P:(i + 1) * P], causal[:, :],
                                          ALU.add).then_inc(causal_done.sem, 1)
                        dve.wait_ge(causal_done.sem, causal_done.at(blk.s, i + 1))
                    dve.tensor_reduce(cmax[:, i, ch:ch + 1], S[k % 4][:, 0:width], AX_X, ALU.max).then_inc(cmax_ready.sem, 1)
                    if ch == 0:
                        dve.wait_ge(cmax_ready.sem, cmax_ready.at(blk, k + 1))
                        dve.tensor_reduce(tmax[:, i:i + 1], cmax[:, i, 0:n], AX_X, ALU.max).then_inc(tmax_ready.sem, 1)
                        dve.wait_ge(tmax_ready.sem, tmax_ready.at(blk.s, i + 1))
                        if not (isinstance(blk.s, int) and blk.s == 0):
                            dve.wait_ge(exp_done.sem, exp_done.at(blk, (i - 3) * n if i < 3 else 0))
                        dve.tensor_scalar(nmax[:, i:i + 1], tmax[:, i:i + 1], -SCALE, None, ALU.mult).then_inc(nmax_ready.sem, 1)

                def row_sums(blk):
                    dve.wait_ge(exp_done.sem, exp_done.at(blk))
                    dve.tensor_reduce(rsum[:, 0, :], csum[:, blk.par, :, 0:chunks(blk)], AX_X, ALU.add).then_inc(rsum_ready.sem, 1)

                def project(blk, r):
                    i, g = tile_group(r)
                    dve.wait_ge(out_done.sem, out_done.at(blk.s, r + 1))
                    if r == 0:
                        dve.wait_ge(weight_ready.sem, weight_ready.at(blk.s))
                    acc = x1[:, blk.par, i, :]
                    for e in range(2):
                        dve.wait_ge(summed.sem, summed.at(blk.s, r + e))
                        dve.scalar_tensor_tensor(out=acc, in0=OUT_BANKS[r % 4][:, e * C:(e + 1) * C],
                                                 scalar=weight[:, blk.par, i, 2 * g + e:2 * g + e + 1],
                                                 in1=acc, op0=ALU.mult, op1=ALU.add).then_inc(summed.sem, 1)

                dve.wait_ge(setup, 2)
                for k in range(counts[0]):
                    scores(first, k)

                def body(blk):
                    nxt = blk.plus(1)
                    row_sums(blk)
                    for what, k in events(blk, nxt):
                        if what == "S":
                            scores(nxt, k)
                        if what == "T":
                            lo = max(0, k - (counts[blk.j] - TILES)) * P
                            dve.wait_ge(p_hi.sem, p_hi.at(blk, k + 1))
                            dve.tensor_tensor(pT_lo[:, k % 3, lo:], T_BANKS[k % 3][:, lo:], pT_hi[:, k % 3, lo:].bitcast(F32),
                                              ALU.subtract).then_inc(p_lo.sem, 1)
                        if what == "V" and k == counts[blk.j] - 1:
                            dve.wait_ge(o_hi.sem, o_hi.at(blk.s))
                            dve.tensor_tensor(oT_lo[:, :], Y[0][:, :], oT_hi[:, :].bitcast(F32), ALU.subtract).then_inc(o_lo.sem, 1)
                        if what == "O" and k % 2 == 0:
                            project(blk, k)

                loop_blocks(dve, B, NB, body)

            @block.tensor
            def _(pe):
                p_transposed.grant(pe)
                pv_done.grant(pe)
                out_done.grant(pe)
                ident = t["ident"]

                def scores(blk, k):
                    n = chunks(blk)
                    i, ch = k // n, n - 1 - k % n
                    width = max(2 * P, (i + 1) * P) if ch == n - 1 else BLOCK
                    if k == 0:
                        pe.wait_ge(q_in[blk.par].sem, q_in[blk.par].at(blk.turn))
                    if i == 0:
                        pe.wait_ge(k_in[ch].sem, k_in[ch].at(blk.b))
                    pe.wait_ge(exp_done.sem, exp_done.at(blk, k - 3))
                    cols = slice(i * P, (i + 1) * P)
                    product(pe, S[k % 4][:, 0:width],
                            [((qT_hi[:, blk.par, cols], qT_lo[:, blk.par, cols]),
                              (kT_hi[:, ch, 0:width], kT_lo[:, ch, 0:width]))]).then_inc(s_done.sem, 1)

                def transpose(blk, u):
                    first_tile = max(0, u - (counts[blk.j] - TILES))
                    if u == 0:
                        pe.wait_ge(exp_done.sem, exp_done.at(blk))
                        pe.wait_ge(summed.sem, summed.at(blk.s - 1, OUTS - 2))
                    if u == 1:
                        pe.wait_ge(scaled.sem, scaled.at(blk.s - 1, OUTS - 2))
                    if u == 2:
                        pe.wait_ge(summed.sem, summed.at(blk.s - 1))
                    pe.wait_ge(p_lo.sem, p_lo.at(blk, max(0, u - 2)))
                    for i in range(first_tile, TILES):
                        last = pe.transpose(T_BANKS[u % 3][:, i * P:(i + 1) * P], probs[:, blk.par, i, u * P:(u + 1) * P], ident[:, :])
                    last.then_inc(p_transposed.sem, 1)

                def values(blk, u):
                    lo = max(0, u - (counts[blk.j] - TILES)) * P
                    if u % TILES == 0:
                        pe.wait_ge(v_in[u // TILES].sem, v_in[u // TILES].at(blk.b))
                    if u == 0:
                        pe.wait_ge(scaled.sem, scaled.at(blk.s - 1))
                    pe.wait_ge(p_lo.sem, p_lo.at(blk, u + 1))
                    product(pe, Y[0][:, lo:], [((v_hi[:, u, :], v_lo[:, u, :]), (pT_hi[:, u % 3, lo:], pT_lo[:, u % 3, lo:]))],
                            begin=(u == 0), end=(u == counts[blk.j] - 1)).then_inc(pv_done.sem, 1)

                def project(blk, r):
                    i, g = tile_group(r)
                    if r == 0:
                        pe.wait_ge(o_lo.sem, o_lo.at(blk.s))
                    if r >= 4 and r % 2 == 0:
                        pe.wait_ge(summed.sem, summed.at(blk.s, r - 2))
                    if r >= 4 and r % 2 == 1:
                        pe.wait_ge(scaled.sem, scaled.at(blk.s, r - 3))
                    w = slice(g * BLOCK, (g + 1) * BLOCK)
                    cols = slice(i * P, (i + 1) * P)
                    product(pe, OUT_BANKS[r % 4][:, :], [((oT_hi[:, cols], oT_lo[:, cols]), (t["wo_hi"][:, w], t["wo_lo"][:, w]))])\
                        .then_inc(out_done.sem, 1)

                for k in range(counts[0]):
                    scores(first, k)

                def body(blk):
                    nxt = blk.plus(1)
                    for what, k in events(blk, nxt):
                        if what == "S":
                            scores(nxt, k)
                        if what == "T":
                            transpose(blk, k)
                        if what == "V":
                            values(blk, k)
                        if what == "O":
                            project(blk, k)

                loop_blocks(pe, B, NB, body)


def dims():
    return dict(B=4, NB=4, C=256, E=8, D=128)


def build(nc, A, out):
    d = dims()
    N, C = d["B"] * d["NB"] * BLOCK, d["C"]

    def scratch(name, shape):
        return nc.dram_tensor(name, shape, F32, kind="Internal").ap()

    with ExitStack() as st:
        c = Ctx(nc, st, "")
        t = dict(x2d=A["x"].rearrange("b l c -> (b l) c"), out2d=out.rearrange("b l c -> (b l) c"), **A)
        for name, cols in (("feat", C), ("base", C), ("x1", C)):
            t[name] = scratch("s_" + name, [N, C])
        t["fold"] = scratch("s_fold", [d["B"] * P, 13 * C])
        for name in ("qT_hi", "qT_lo", "kT_hi", "kT_lo"):
            t[name] = scratch("s_" + name, [P, N])
        for name in ("v_hi", "v_lo"):
            t[name] = scratch("s_" + name, [N, P])
        t["route"] = scratch("s_route", [N, 8])
        t["ident"] = c.sb("ident", [P, P])
        t["minus_half"] = c.sb("minus_half", [P, 32])
        t["half"] = c.sb("half", [P, 32])
        t["minus_one"] = c.sb("minus_one", [P, 32])
        t["sig"] = c.sb("sig", [P, 8])
        t["wo_hi"] = c.sb("wo_hi", [P, d["E"] * C], F32R)
        t["wo_lo"] = c.sb("wo_lo", [P, d["E"] * C], F32R)
        with ExitStack() as until_attention:
            c = Ctx(nc, until_attention, "")
            t["sn_hi"] = c.sb("sn_hi", [P, 2, d["E"]], F32R)
            t["sn_lo"] = c.sb("sn_lo", [P, 2, d["E"]], F32R)
            t["w2_hi"] = c.sb("w2_hi", [P, 4, C], F32R)
            t["w2_lo"] = c.sb("w2_lo", [P, 4, C], F32R)
            t["wqkv_hi"] = c.sb("wqkv_hi", [P, 6 * d["E"] * d["D"]], F32R)
            t["wqkv_lo"] = c.sb("wqkv_lo", [P, 6 * d["E"] * d["D"]], F32R)
            with ExitStack() as until_experts:
                scaled = ScaledFeatures(Ctx(nc, until_experts, "m_"), t, d)
                stage1(nc, t, d, scaled)
                stage2(nc, t, d, scaled)
        stage3(nc, t, d)


_INS = {"x": "L0_attn_x", "Wq": "L0_attn_Wq", "Wm": "L0_attn_Wm", "W1": "L0_attn_W1", "W2": "L0_attn_W2",
        "g1": "L0_attn_g1", "b1": "L0_attn_b1", "g2": "L0_attn_g2", "b2": "L0_attn_b2",
        "sim": "L0_ffn_sim_matrix", "gates": "L0_ffn_gates", "Wqe": "L0_ffn_q_proj", "Wke": "L0_ffn_k_proj",
        "Wve": "L0_ffn_v_proj", "Woe": "L0_ffn_o_proj"}


def kernel(**inputs):
    import numpy as np
    import concourse.bacc as bacc
    from concourse.bass_utils import run_bass_kernel_spmd

    nc = bacc.Bacc("TRN2", target_bir_lowering=False, num_devices=1)
    arrays, handles = {}, {}
    for short, name in _INS.items():
        arrays["in_" + name] = np.ascontiguousarray(inputs[name])
        handles[short] = nc.dram_tensor("in_" + name, arrays["in_" + name].shape, F32, kind="ExternalInput").ap()
    out = nc.dram_tensor("out", arrays["in_L0_attn_x"].shape, F32, kind="ExternalOutput").ap()
    build(nc, handles, out)
    r = run_bass_kernel_spmd(nc, [arrays], core_ids=[0])
    return r.results[0]["out"]
```
